# Optimizing a Trainium2 kernel written in Bass

```python
import numpy as np
import jax
import jax.numpy as jnp

def _softmax(x, axis=-1):
    return jax.nn.softmax(x, axis=axis)

def _gelu(x):
    return jax.nn.gelu(x, approximate=True)

def _silu(x):
    return jax.nn.silu(x)

def _sigmoid(x):
    return jax.nn.sigmoid(x)

def _layernorm(x, axis=-1, eps=1e-05):
    m = jnp.mean(x, axis=axis, keepdims=True)
    v = jnp.var(x, axis=axis, keepdims=True)
    return (x - m) / jnp.sqrt(v + eps)

def _scatter_add(tgt, idx, src, axis=0):
    return tgt.at[idx].add(src)

def _segment_sum(src, seg, n):
    return jax.ops.segment_sum(src, seg, n)
kernel_name = 'mk_gnn_ffn_d2_gnn_r32_dbef95'

def setup_inputs(seed: int=0):
    np.random.seed(seed)
    _w = jnp.asarray

    def _rec_inputs():
        import jax
        import jax.numpy as jnp
        _gk = jax.random.key(seed)
        x = -0.0003713 + 1 * jax.random.normal(jax.random.fold_in(_gk, 1), (3125, 256), jnp.float32)
        src = jax.random.randint(jax.random.fold_in(_gk, 2), (50000,), 0, 3125, jnp.int32)
        dst = jax.random.randint(jax.random.fold_in(_gk, 3), (50000,), 0, 3125, jnp.int32)
        _o = jnp.argsort(dst, stable=True)
        src = src[_o]
        dst = dst[_o]
        edge_attr_16 = -0.000153872 + 1.00011 * jax.random.normal(jax.random.fold_in(_gk, 11), (50000, 16), jnp.float32)
        edge_attr_3 = -0.000563758 + 1.00031 * jax.random.normal(jax.random.fold_in(_gk, 12), (50000, 3), jnp.float32)
        edge_attr_4 = 0.0007022 + 0.999661 * jax.random.normal(jax.random.fold_in(_gk, 13), (50000, 4), jnp.float32)
        return (x, src, dst, edge_attr_16, edge_attr_3, edge_attr_4)
    x, src, dst, edge_attr_16, edge_attr_3, edge_attr_4 = _rec_inputs()

    def _L0_gnn_setup():
        import jax, jax.numpy as jnp
        import numpy as np
        N, E, C, R, HID = (50000, 15625, 64, 16, 64)
        key = jax.random.key(seed)
        ks = jax.random.split(key, 24)
        g = lambda k, shape, s=1.0: jax.random.normal(k, shape, dtype=jnp.float32) * s
        cs = C ** (-0.5)
        inp = {'h': g(ks[0], (N, 4 * C)), 'edge_index': jax.random.randint(ks[1], (2, E), 0, N), 'edge_sh': g(ks[2], (E, 4)), 'edge_rbf': g(ks[3], (E, R)), 'W_up0': g(ks[4], (C, C), cs), 'W_up1': g(ks[5], (C, C), cs), 'M1': g(ks[6], (R, HID), R ** (-0.5)), 'M2': g(ks[7], (HID, HID), HID ** (-0.5)), 'M3': g(ks[8], (HID, HID), HID ** (-0.5)), 'M4': g(ks[9], (HID, 4 * C), HID ** (-0.5)), 'W_lin0': g(ks[10], (C, C), cs), 'W_lin1': g(ks[11], (C, C), cs), 'Wsc0': g(ks[12], (C, C), cs), 'Wsc1': g(ks[13], (C, C), cs), 'Wc0': g(ks[14], (C, 5)), 'Wc1': g(ks[15], (C, 4)), 'WB0': g(ks[16], (C, C), cs), 'WB1': g(ks[17], (C, C), cs), 'gamma0': jnp.ones((C,), jnp.float32), 'beta0': jnp.zeros((C,), jnp.float32), 'gamma1': jnp.ones((C,), jnp.float32)}
        return inp
    _L0_gnn_all = _L0_gnn_setup()
    _L0_gnn_in = {k: v for k, v in _L0_gnn_all.items() if k in ('W_up0', 'W_up1', 'M1', 'M2', 'M3', 'M4', 'W_lin0', 'W_lin1', 'Wsc0', 'Wsc1', 'Wc0', 'Wc1', 'WB0', 'WB1', 'gamma0', 'beta0', 'gamma1')}
    del _L0_gnn_all

    def _L0_ffn_setup():
        import jax, jax.numpy as jnp
        import numpy as np
        BN_EPS = 0.001

        def _bn(h, g, b, m, v):
            return g * (h - m) * jax.lax.rsqrt(v + BN_EPS) + b
        key = jax.random.key(seed)
        ks = jax.random.split(key, 8)
        B, F, Df = (256, 64, 256)
        E, H, D = (8, 256, 256)
        s1 = 1.0 / np.sqrt(Df)
        s2 = 1.0 / np.sqrt(H)
        return {'x': jax.random.normal(ks[0], (B, F, Df), jnp.float32), 'Wr': jax.random.normal(ks[1], (Df, E), jnp.float32) * s1, 'br': jnp.zeros((E,), jnp.float32), 'W1': jax.random.normal(ks[2], (E, Df, H), jnp.float32) * s1, 'b1': jnp.zeros((E, H), jnp.float32), 'g1': jnp.ones((E, H), jnp.float32), 'be1': jnp.zeros((E, H), jnp.float32), 'm1': jnp.zeros((E, H), jnp.float32), 'v1': jnp.ones((E, H), jnp.float32), 'W2': jax.random.normal(ks[3], (E, H, H), jnp.float32) * s2, 'b2': jnp.zeros((E, H), jnp.float32), 'g2': jnp.ones((E, H), jnp.float32), 'be2': jnp.zeros((E, H), jnp.float32), 'm2': jnp.zeros((E, H), jnp.float32), 'v2': jnp.ones((E, H), jnp.float32), 'Wo': jax.random.normal(ks[4], (E, H, D), jnp.float32) * s2, 'bo': jnp.zeros((E, D), jnp.float32)}
    _L0_ffn_all = _L0_ffn_setup()
    _L0_ffn_in = {k: v for k, v in _L0_ffn_all.items() if k in ('Wr', 'br', 'W1', 'b1', 'g1', 'be1', 'm1', 'v1', 'W2', 'b2', 'g2', 'be2', 'm2', 'v2', 'Wo', 'bo')}
    del _L0_ffn_all

    def _L1_gnn_setup():
        import jax, jax.numpy as jnp
        import numpy as np
        MUL = 64
        N_NODES = 10000
        N_EDGES = 10000
        DIM = MUL + 3 * MUL
        SQ3 = float(np.sqrt(3.0))
        INV_MUL = float(1.0 / np.sqrt(MUL))
        INV_TP = float(1.0 / np.sqrt(2 * MUL))

        def _split(f):
            return (f[:, :MUL], f[:, MUL:].reshape(f.shape[0], MUL, 3))

        def _lin(x0, x1, w0, w1):
            return (x0 @ w0 * INV_MUL, jnp.einsum('eum,uv->evm', x1, w1) * INV_MUL)

        def _fctp(x0, x1, sh1, w00, w11, w01, w10):
            dot = jnp.einsum('eum,em->eu', x1, sh1) / SQ3
            out0 = (x0 @ w00 + dot @ w11) * INV_TP
            out1 = (jnp.einsum('eu,uv->ev', x0, w01)[:, :, None] * sh1[:, None, :] + jnp.einsum('eum,uv->evm', x1, w10)) * INV_TP
            return (out0, out1)

        def _forward(atom_feature, edge_vector, weights, edge_index):
            ls0, ls1, ld0, ld1, t1_00, t1_11, t1_01, t1_10, t2_00, t2_11, t2_01, t2_10, lh0, lh1, lsc = weights
            src, dst = (edge_index[0], edge_index[1])
            r = edge_vector / (jnp.linalg.norm(edge_vector, axis=-1, keepdims=True) + 1e-12)
            sh1 = SQ3 * r
            x0, x1 = _split(atom_feature)
            s0, s1 = _lin(x0[src], x1[src], ls0, ls1)
            d0, d1 = _lin(x0[dst], x1[dst], ld0, ld1)
            h0, h1 = _fctp(s0, s1, sh1, t1_00, t1_11, t1_01, t1_10)
            h0, h1 = _lin(h0, h1, lh0, lh1)
            sc = jax.nn.leaky_relu(h0) @ lsc * INV_MUL
            full = jnp.concatenate([sc, jnp.zeros((sc.shape[0], 3 * MUL), sc.dtype)], axis=-1)
            act = jax.nn.softmax(full, axis=-1)
            o0, o1 = _fctp(h0, h1, sh1, t2_00, t2_11, t2_01, t2_10)
            tp2_flat = jnp.concatenate([o0, o1.reshape(o1.shape[0], 3 * MUL)], axis=-1)
            msgs = act * tp2_flat
            agg = jax.ops.segment_sum(msgs, dst, num_segments=atom_feature.shape[0])
            return atom_feature + agg
        _WNAMES = ['lin_src_w0', 'lin_src_w1', 'lin_dst_w0', 'lin_dst_w1', 'tp1_w00', 'tp1_w11', 'tp1_w01', 'tp1_w10', 'tp2_w00', 'tp2_w11', 'tp2_w01', 'tp2_w10', 'lin_hidden_w0', 'lin_hidden_w1', 'lin_scalar_w']
        key = jax.random.key(seed)
        ks = jax.random.split(key, 18)
        inp = {n: jax.random.normal(ks[i], (MUL, MUL), jnp.float32) for i, n in enumerate(_WNAMES)}
        inp['atom_feature'] = jax.random.normal(ks[15], (N_NODES, DIM), jnp.float32)
        inp['edge_vector'] = jax.random.normal(ks[16], (N_EDGES, 3), jnp.float32)
        inp['edge_index'] = jax.random.randint(ks[17], (2, N_EDGES), 0, N_NODES, dtype=jnp.int32)
        return inp
    _L1_gnn_all = _L1_gnn_setup()
    _L1_gnn_in = {k: v for k, v in _L1_gnn_all.items() if k in ('lin_src_w0', 'lin_src_w1', 'lin_dst_w0', 'lin_dst_w1', 'tp1_w00', 'tp1_w11', 'tp1_w01', 'tp1_w10', 'tp2_w00', 'tp2_w11', 'tp2_w01', 'tp2_w10', 'lin_hidden_w0', 'lin_hidden_w1', 'lin_scalar_w')}
    del _L1_gnn_all

    def _L1_ffn_setup():
        import jax, jax.numpy as jnp
        import numpy as np
        D_MODEL = 256
        EXPERT_DIM = 512
        NUM_EXPERTS = 8
        TOP_K = 2
        SEQ_LEN = 64
        BATCH = 2
        key = jax.random.key(seed)
        ks = jax.random.split(key, 8)
        s = 0.02
        x = jax.random.normal(ks[0], (SEQ_LEN, BATCH, D_MODEL), dtype=jnp.float32)
        Wg = jax.random.normal(ks[1], (D_MODEL, NUM_EXPERTS), dtype=jnp.float32) * s
        bg = jax.random.normal(ks[2], (NUM_EXPERTS,), dtype=jnp.float32) * s
        bias = jnp.zeros((NUM_EXPERTS,), dtype=jnp.float32)
        W1 = jax.random.normal(ks[3], (NUM_EXPERTS, D_MODEL, EXPERT_DIM), dtype=jnp.float32) * s
        b1 = jax.random.normal(ks[4], (NUM_EXPERTS, EXPERT_DIM), dtype=jnp.float32) * s
        W2 = jax.random.normal(ks[5], (NUM_EXPERTS, EXPERT_DIM, D_MODEL), dtype=jnp.float32) * s
        b2 = jax.random.normal(ks[6], (NUM_EXPERTS, D_MODEL), dtype=jnp.float32) * s
        return {'x': x, 'Wg': Wg, 'bg': bg, 'bias': bias, 'W1': W1, 'b1': b1, 'W2': W2, 'b2': b2}
    _L1_ffn_all = _L1_ffn_setup()
    _L1_ffn_in = {k: v for k, v in _L1_ffn_all.items() if k in ('Wg', 'bg', 'bias', 'W1', 'b1', 'W2', 'b2')}
    del _L1_ffn_all
    return {'x': x, 'src': src, 'dst': dst, 'edge_attr_16': edge_attr_16, 'edge_attr_3': edge_attr_3, 'edge_attr_4': edge_attr_4, 'L0_gnn_W_up0': _L0_gnn_in['W_up0'], 'L0_gnn_W_up1': _L0_gnn_in['W_up1'], 'L0_gnn_M1': _L0_gnn_in['M1'], 'L0_gnn_M2': _L0_gnn_in['M2'], 'L0_gnn_M3': _L0_gnn_in['M3'], 'L0_gnn_M4': _L0_gnn_in['M4'], 'L0_gnn_W_lin0': _L0_gnn_in['W_lin0'], 'L0_gnn_W_lin1': _L0_gnn_in['W_lin1'], 'L0_gnn_Wsc0': _L0_gnn_in['Wsc0'], 'L0_gnn_Wsc1': _L0_gnn_in['Wsc1'], 'L0_gnn_Wc0': _L0_gnn_in['Wc0'], 'L0_gnn_Wc1': _L0_gnn_in['Wc1'], 'L0_gnn_WB0': _L0_gnn_in['WB0'], 'L0_gnn_WB1': _L0_gnn_in['WB1'], 'L0_gnn_gamma0': _L0_gnn_in['gamma0'], 'L0_gnn_beta0': _L0_gnn_in['beta0'], 'L0_gnn_gamma1': _L0_gnn_in['gamma1'], 'L0_ffn_Wr': _L0_ffn_in['Wr'], 'L0_ffn_br': _L0_ffn_in['br'], 'L0_ffn_W1': _L0_ffn_in['W1'], 'L0_ffn_b1': _L0_ffn_in['b1'], 'L0_ffn_g1': _L0_ffn_in['g1'], 'L0_ffn_be1': _L0_ffn_in['be1'], 'L0_ffn_m1': _L0_ffn_in['m1'], 'L0_ffn_v1': _L0_ffn_in['v1'], 'L0_ffn_W2': _L0_ffn_in['W2'], 'L0_ffn_b2': _L0_ffn_in['b2'], 'L0_ffn_g2': _L0_ffn_in['g2'], 'L0_ffn_be2': _L0_ffn_in['be2'], 'L0_ffn_m2': _L0_ffn_in['m2'], 'L0_ffn_v2': _L0_ffn_in['v2'], 'L0_ffn_Wo': _L0_ffn_in['Wo'], 'L0_ffn_bo': _L0_ffn_in['bo'], 'L1_gnn_lin_src_w0': _L1_gnn_in['lin_src_w0'], 'L1_gnn_lin_src_w1': _L1_gnn_in['lin_src_w1'], 'L1_gnn_lin_dst_w0': _L1_gnn_in['lin_dst_w0'], 'L1_gnn_lin_dst_w1': _L1_gnn_in['lin_dst_w1'], 'L1_gnn_tp1_w00': _L1_gnn_in['tp1_w00'], 'L1_gnn_tp1_w11': _L1_gnn_in['tp1_w11'], 'L1_gnn_tp1_w01': _L1_gnn_in['tp1_w01'], 'L1_gnn_tp1_w10': _L1_gnn_in['tp1_w10'], 'L1_gnn_tp2_w00': _L1_gnn_in['tp2_w00'], 'L1_gnn_tp2_w11': _L1_gnn_in['tp2_w11'], 'L1_gnn_tp2_w01': _L1_gnn_in['tp2_w01'], 'L1_gnn_tp2_w10': _L1_gnn_in['tp2_w10'], 'L1_gnn_lin_hidden_w0': _L1_gnn_in['lin_hidden_w0'], 'L1_gnn_lin_hidden_w1': _L1_gnn_in['lin_hidden_w1'], 'L1_gnn_lin_scalar_w': _L1_gnn_in['lin_scalar_w'], 'L1_ffn_Wg': _L1_ffn_in['Wg'], 'L1_ffn_bg': _L1_ffn_in['bg'], 'L1_ffn_bias': _L1_ffn_in['bias'], 'L1_ffn_W1': _L1_ffn_in['W1'], 'L1_ffn_b1': _L1_ffn_in['b1'], 'L1_ffn_W2': _L1_ffn_in['W2'], 'L1_ffn_b2': _L1_ffn_in['b2']}

def reference(x, src, dst, edge_attr_16, edge_attr_3, edge_attr_4, L0_gnn_W_up0, L0_gnn_W_up1, L0_gnn_M1, L0_gnn_M2, L0_gnn_M3, L0_gnn_M4, L0_gnn_W_lin0, L0_gnn_W_lin1, L0_gnn_Wsc0, L0_gnn_Wsc1, L0_gnn_Wc0, L0_gnn_Wc1, L0_gnn_WB0, L0_gnn_WB1, L0_gnn_gamma0, L0_gnn_beta0, L0_gnn_gamma1, L0_ffn_Wr, L0_ffn_br, L0_ffn_W1, L0_ffn_b1, L0_ffn_g1, L0_ffn_be1, L0_ffn_m1, L0_ffn_v1, L0_ffn_W2, L0_ffn_b2, L0_ffn_g2, L0_ffn_be2, L0_ffn_m2, L0_ffn_v2, L0_ffn_Wo, L0_ffn_bo, L1_gnn_lin_src_w0, L1_gnn_lin_src_w1, L1_gnn_lin_dst_w0, L1_gnn_lin_dst_w1, L1_gnn_tp1_w00, L1_gnn_tp1_w11, L1_gnn_tp1_w01, L1_gnn_tp1_w10, L1_gnn_tp2_w00, L1_gnn_tp2_w11, L1_gnn_tp2_w01, L1_gnn_tp2_w10, L1_gnn_lin_hidden_w0, L1_gnn_lin_hidden_w1, L1_gnn_lin_scalar_w, L1_ffn_Wg, L1_ffn_bg, L1_ffn_bias, L1_ffn_W1, L1_ffn_b1, L1_ffn_W2, L1_ffn_b2):
    import jax
    import jax.numpy as jnp

    def _L0_gnn_ref(h, edge_index, edge_sh, edge_rbf, W_up0, W_up1, M1, M2, M3, M4, W_lin0, W_lin1, Wsc0, Wsc1, Wc0, Wc1, WB0, WB1, gamma0, beta0, gamma1):
        import jax, jax.numpy as jnp
        import numpy as np
        N, E, C, R, HID = (50000, 15625, 64, 16, 64)
        n = h.shape[0]
        h0 = h[:, :C]
        h1 = h[:, C:].reshape(n, C, 3)
        up0 = h0 @ W_up0
        up1 = jnp.einsum('ncx,cd->ndx', h1, W_up1)
        r = jax.nn.silu(edge_rbf @ M1)
        r = jax.nn.silu(r @ M2)
        r = jax.nn.silu(r @ M3)
        tpw = (r @ M4).reshape(-1, 4, C)
        snd, rcv = (edge_index[0], edge_index[1])
        x0 = up0[snd]
        x1 = up1[snd]
        sh0 = edge_sh[:, 0]
        sh1 = edge_sh[:, 1:]
        inv3 = 1.0 / jnp.sqrt(jnp.float32(3.0))
        m0e = tpw[:, 0] * x0 * sh0[:, None] + tpw[:, 3] * jnp.einsum('ecx,ex->ec', x1, sh1) * inv3
        m1e = tpw[:, 1][:, :, None] * x0[:, :, None] * sh1[:, None, :] + tpw[:, 2][:, :, None] * x1 * sh0[:, None, None]
        msg0 = jax.ops.segment_sum(m0e, rcv, num_segments=n)
        msg1 = jax.ops.segment_sum(m1e, rcv, num_segments=n)
        A0 = msg0 @ W_lin0
        A1 = jnp.einsum('ncx,cd->ndx', msg1, W_lin1)
        sc0 = h0 @ Wsc0
        sc1 = jnp.einsum('ncx,cd->ndx', h1, Wsc1)
        vv = jnp.sum(A1 * A1, -1)
        B0 = Wc0[:, 0] * A0 + Wc0[:, 1] * A0 * A0 + Wc0[:, 2] * vv + Wc0[:, 3] * A0 ** 3 + Wc0[:, 4] * A0 * vv
        B1 = (Wc1[:, 0] + Wc1[:, 1] * A0 + Wc1[:, 2] * A0 * A0 + Wc1[:, 3] * vv)[..., None] * A1
        o0 = B0 @ WB0 + sc0
        o1 = jnp.einsum('ncx,cd->ndx', B1, WB1) + sc1
        eps = jnp.float32(1e-05)
        mu = jnp.mean(o0, 0)
        xc = o0 - mu
        var = jnp.mean(xc * xc, 0)
        n0 = xc * jax.lax.rsqrt(var + eps) * gamma0 + beta0
        nrm1 = jnp.mean(jnp.sum(o1 * o1, -1) / 3.0, 0)
        n1 = o1 * (jax.lax.rsqrt(nrm1 + eps) * gamma1)[None, :, None]
        return jnp.concatenate([n0, n1.reshape(n, 3 * C)], -1)

    def _L0_ffn_ref(x, Wr, br, W1, b1, g1, be1, m1, v1, W2, b2, g2, be2, m2, v2, Wo, bo):
        import jax, jax.numpy as jnp
        import numpy as np
        BN_EPS = 0.001

        def _bn(h, g, b, m, v):
            return g * (h - m) * jax.lax.rsqrt(v + BN_EPS) + b
        feat = jnp.mean(x, axis=0)
        w = jax.nn.softmax(feat @ Wr + br, axis=-1)
        h = jnp.einsum('bfd,edh->bfeh', x, W1) + b1
        h = jax.nn.relu(_bn(h, g1, be1, m1, v1))
        h = jnp.einsum('bfeh,ehk->bfek', h, W2) + b2
        h = jax.nn.relu(_bn(h, g2, be2, m2, v2))
        y = jnp.einsum('bfeh,ehd->bfed', h, Wo) + bo
        return jnp.einsum('bfed,fe->bfd', y, w)

    def _L1_gnn_ref(atom_feature, edge_vector, lin_src_w0, lin_src_w1, lin_dst_w0, lin_dst_w1, tp1_w00, tp1_w11, tp1_w01, tp1_w10, tp2_w00, tp2_w11, tp2_w01, tp2_w10, lin_hidden_w0, lin_hidden_w1, lin_scalar_w, edge_index):
        import jax, jax.numpy as jnp
        import numpy as np
        MUL = 64
        N_NODES = 10000
        N_EDGES = 10000
        DIM = MUL + 3 * MUL
        SQ3 = float(np.sqrt(3.0))
        INV_MUL = float(1.0 / np.sqrt(MUL))
        INV_TP = float(1.0 / np.sqrt(2 * MUL))

        def _split(f):
            return (f[:, :MUL], f[:, MUL:].reshape(f.shape[0], MUL, 3))

        def _lin(x0, x1, w0, w1):
            return (x0 @ w0 * INV_MUL, jnp.einsum('eum,uv->evm', x1, w1) * INV_MUL)

        def _fctp(x0, x1, sh1, w00, w11, w01, w10):
            dot = jnp.einsum('eum,em->eu', x1, sh1) / SQ3
            out0 = (x0 @ w00 + dot @ w11) * INV_TP
            out1 = (jnp.einsum('eu,uv->ev', x0, w01)[:, :, None] * sh1[:, None, :] + jnp.einsum('eum,uv->evm', x1, w10)) * INV_TP
            return (out0, out1)

        def _forward(atom_feature, edge_vector, weights, edge_index):
            ls0, ls1, ld0, ld1, t1_00, t1_11, t1_01, t1_10, t2_00, t2_11, t2_01, t2_10, lh0, lh1, lsc = weights
            src, dst = (edge_index[0], edge_index[1])
            r = edge_vector / (jnp.linalg.norm(edge_vector, axis=-1, keepdims=True) + 1e-12)
            sh1 = SQ3 * r
            x0, x1 = _split(atom_feature)
            s0, s1 = _lin(x0[src], x1[src], ls0, ls1)
            d0, d1 = _lin(x0[dst], x1[dst], ld0, ld1)
            h0, h1 = _fctp(s0, s1, sh1, t1_00, t1_11, t1_01, t1_10)
            h0, h1 = _lin(h0, h1, lh0, lh1)
            sc = jax.nn.leaky_relu(h0) @ lsc * INV_MUL
            full = jnp.concatenate([sc, jnp.zeros((sc.shape[0], 3 * MUL), sc.dtype)], axis=-1)
            act = jax.nn.softmax(full, axis=-1)
            o0, o1 = _fctp(h0, h1, sh1, t2_00, t2_11, t2_01, t2_10)
            tp2_flat = jnp.concatenate([o0, o1.reshape(o1.shape[0], 3 * MUL)], axis=-1)
            msgs = act * tp2_flat
            agg = jax.ops.segment_sum(msgs, dst, num_segments=atom_feature.shape[0])
            return atom_feature + agg
        _WNAMES = ['lin_src_w0', 'lin_src_w1', 'lin_dst_w0', 'lin_dst_w1', 'tp1_w00', 'tp1_w11', 'tp1_w01', 'tp1_w10', 'tp2_w00', 'tp2_w11', 'tp2_w01', 'tp2_w10', 'lin_hidden_w0', 'lin_hidden_w1', 'lin_scalar_w']
        weights = (lin_src_w0, lin_src_w1, lin_dst_w0, lin_dst_w1, tp1_w00, tp1_w11, tp1_w01, tp1_w10, tp2_w00, tp2_w11, tp2_w01, tp2_w10, lin_hidden_w0, lin_hidden_w1, lin_scalar_w)
        return _forward(atom_feature, edge_vector, weights, edge_index)

    def _L1_ffn_ref(x, Wg, bg, bias, W1, b1, W2, b2):
        import jax, jax.numpy as jnp
        import numpy as np
        D_MODEL = 256
        EXPERT_DIM = 512
        NUM_EXPERTS = 8
        TOP_K = 2
        SEQ_LEN = 64
        BATCH = 2
        x_flat = x.reshape(-1, D_MODEL)
        gate_logits = x_flat @ Wg + bg + bias
        topk_vals, topk_idx = jax.lax.top_k(gate_logits, TOP_K)
        topk_w = jax.nn.softmax(topk_vals, axis=-1)
        combine = (jax.nn.one_hot(topk_idx, NUM_EXPERTS, dtype=x.dtype) * topk_w[..., None]).sum(axis=1)
        h = jax.nn.relu(jnp.einsum('td,edh->teh', x_flat, W1) + b1)
        y = jnp.einsum('teh,ehd->ted', h, W2) + b2
        out = jnp.einsum('ted,te->td', y, combine)
        return out.reshape(x.shape)
    edge_index = jnp.stack([src, dst])
    x = x + _L0_gnn_ref(_layernorm(x, axis=-1), edge_index, edge_attr_4, edge_attr_16, L0_gnn_W_up0, L0_gnn_W_up1, L0_gnn_M1, L0_gnn_M2, L0_gnn_M3, L0_gnn_M4, L0_gnn_W_lin0, L0_gnn_W_lin1, L0_gnn_Wsc0, L0_gnn_Wsc1, L0_gnn_Wc0, L0_gnn_Wc1, L0_gnn_WB0, L0_gnn_WB1, L0_gnn_gamma0, L0_gnn_beta0, L0_gnn_gamma1)
    x = x + _L0_ffn_ref(_layernorm(x, axis=-1)[None], L0_ffn_Wr, L0_ffn_br, L0_ffn_W1, L0_ffn_b1, L0_ffn_g1, L0_ffn_be1, L0_ffn_m1, L0_ffn_v1, L0_ffn_W2, L0_ffn_b2, L0_ffn_g2, L0_ffn_be2, L0_ffn_m2, L0_ffn_v2, L0_ffn_Wo, L0_ffn_bo)[0]
    x = x + _L1_gnn_ref(_layernorm(x, axis=-1), edge_attr_3, L1_gnn_lin_src_w0, L1_gnn_lin_src_w1, L1_gnn_lin_dst_w0, L1_gnn_lin_dst_w1, L1_gnn_tp1_w00, L1_gnn_tp1_w11, L1_gnn_tp1_w01, L1_gnn_tp1_w10, L1_gnn_tp2_w00, L1_gnn_tp2_w11, L1_gnn_tp2_w01, L1_gnn_tp2_w10, L1_gnn_lin_hidden_w0, L1_gnn_lin_hidden_w1, L1_gnn_lin_scalar_w, edge_index)
    x = x + _L1_ffn_ref(_layernorm(x, axis=-1)[None], L1_ffn_Wg, L1_ffn_bg, L1_ffn_bias, L1_ffn_W1, L1_ffn_b1, L1_ffn_W2, L1_ffn_b2)[0]
    return x

_drawn_inputs = setup_inputs


def setup_inputs(seed=0):
    import zlib

    import numpy as np

    out = dict(_drawn_inputs(seed))
    spreads = {'L0_gnn_gamma0': (1.0, 0.2),
     'L0_gnn_beta0': (0.0, 0.1),
     'L0_gnn_gamma1': (1.0, 0.2),
     'L0_ffn_br': (0.0, 0.317),
     'L0_ffn_b1': (0.0, 0.423),
     'L0_ffn_g1': (1.0, 0.2),
     'L0_ffn_be1': (0.0, 0.431),
     'L0_ffn_m1': (0.0, 0.421),
     'L0_ffn_v1': (1.0, 0.6),
     'L0_ffn_b2': (0.0, 0.304),
     'L0_ffn_g2': (1.0, 0.2),
     'L0_ffn_be2': (0.0, 0.316),
     'L0_ffn_m2': (0.0, 0.31),
     'L0_ffn_v2': (1.0, 0.6),
     'L0_ffn_bo': (0.0, 0.1),
     'L1_ffn_bias': (0.0, 2.0)}
    factors = {'edge_attr_3': 8.0,
     'L1_gnn_lin_src_w0': 7.444,
     'L1_gnn_lin_src_w1': 8.0,
     'L1_gnn_tp1_w00': 8.0,
     'L1_gnn_tp1_w11': 8.0,
     'L1_gnn_tp1_w01': 8.0,
     'L1_gnn_tp1_w10': 8.0,
     'L1_gnn_tp2_w00': 8.0,
     'L1_gnn_tp2_w11': 8.0,
     'L1_gnn_tp2_w01': 8.0,
     'L1_gnn_tp2_w10': 8.0,
     'L1_gnn_lin_hidden_w0': 8.0,
     'L1_gnn_lin_hidden_w1': 7.918,
     'L1_gnn_lin_scalar_w': 8.0,
     'L1_ffn_bg': 200.0,
     'L1_ffn_b1': 200.0,
     'L1_ffn_b2': 200.0,
     'L1_ffn_Wg': 64.0,
     'L1_ffn_W1': 64.0,
     'L1_ffn_W2': 64.0}
    for name, (base, spread) in spreads.items():
        noise = np.random.default_rng([zlib.crc32(name.encode()), seed]).standard_normal(out[name].shape)
        drawn = base * np.exp(spread * noise) if base else spread * noise
        out[name] = jnp.asarray(drawn.astype(out[name].dtype))
    for name, factor in factors.items():
        out[name] = (out[name] * factor).astype(out[name].dtype)
    return out
```

```python
from contextlib import ExitStack

import numpy as np

import concourse.bass as bass
from concourse import mybir

F32 = mybir.dt.float32
I32 = mybir.dt.int32
U32 = mybir.dt.uint32
ALU = mybir.AluOpType
ACT = mybir.ActivationFunctionType
AX = mybir.AxisListType.X

N, D, C, E = 3125, 256, 64, 50000
P = 125
NT = N // P
CT = 5
CHUNKS = NT // CT
CN = CT * P
ET = E // P
GT = 4
G = ET // GT
GE = GT * P
R, HID = 16, 64
ACC_ROWS = 26 * 128
T2 = 448
NEXP = 8
H1 = 256
H2 = 512
SPLIT = (0, 375, 625)
LN_EPS, BN_EPS = 1e-5, 1e-3
SQ3 = float(np.sqrt(3.0))
INV_TP = float(1.0 / np.sqrt(2 * C))
INV_MUL = float(1.0 / np.sqrt(C))


class State:
    def __init__(self):
        self.mw, self.mw_loads, self.mw_in, self.s_mw = {}, {}, {}, {}


class Buffers:
    pass


def bc(ap, n, axis):
    v = ap.unsqueeze(axis)
    shape = list(v.shape)
    shape[axis] = n
    return v.broadcast_to(shape)


def linker(eng, sem):
    def link(ins):
        ins.then_inc(sem, 1)
        eng.wait_ge(sem, 1)
        eng.sem_inc(sem, -1)
    return link


def tell(eng, ins, own, *sems):
    ins.then_inc(own, 1)
    eng.wait_ge(own, 1)
    eng.sem_inc(own, -1)
    for s in sems:
        eng.sem_inc(s, 1)


class Signals:
    SHARED = {"dve_step", "act_step", "variance", "deviation", "h_ready", "turned", "hT_ready", "h_free",
              "gates_in_psum", "logits_ready", "exps_ready", "gates_ready", "gates_turned", "gates_T_ready",
              "bias_in_psum", "hidden_in_psum", "hidden_ready", "out_in_psum", "out_added"}

    def __init__(self, nc, ctx):
        self.nc, self.ctx, self.shared = nc, ctx, {}

    def get(self, phase, name):
        if name not in self.SHARED:
            return self.ctx.enter_context(self.nc.semaphore(f"{phase}_{name}"))
        if name not in self.shared:
            self.shared[name] = self.ctx.enter_context(self.nc.semaphore(name))
        return self.shared[name]



def setup(nc, ctx, I, S):
    def sb(name, shape, dt=F32):
        return ctx.enter_context(nc.sbuf_tensor(name, shape, dt))

    def sem(name):
        return S.signals.get("su", name)

    S.x = sb("x_nodes", [P, NT, D])
    S.ident = sb("ident", [128, 128])
    S.ones = sb("ones", [P, 128])
    S.src = sb("src_idx", [P, ET], I32)
    S.dst = sb("dst_idx", [P, ET], I32)
    S.dstf = sb("dst_float", [P, ET])
    S.put = sb("scatter_idx", [P, ET], I32)
    S.sh0 = sb("edge_sh", [P, ET, 4])
    S.shn = sb("edge_unit", [P, ET, 3])
    S.q = sb("edge_q", [P, ET])
    S.wh = sb("w_hidden", [128, C])
    S.wm = sb("w_main", [128, 3 * C])
    S.lsc = sb("w_scalar", [C, C])
    S.wd = sb("w_vector", [128, 2, 128])
    S.before = sb("earlier_mask", [P, P])
    S.dump = sb("dump_row", [P, 1])

    S.table1 = nc.dram_tensor("table1", (N, D), F32, kind="Internal").ap()
    S.table2 = nc.dram_tensor("table2", (N, T2), F32, kind="Internal").ap()
    S.acc = [[nc.dram_tensor(f"acc{l}_{i}", (ACC_ROWS, D), F32, kind="Internal").ap() for i in range(GT)]
             for l in range(2)]

    with ExitStack() as loc:
        def tb(name, shape, dt=F32):
            return loc.enter_context(nc.sbuf_tensor(name, shape, dt))

        zero = tb("zero", [128, 26, D])
        ev = tb("edge_vec", [P, ET, 3])
        sq = tb("edge_sq", [P, ET, 3])
        nrm = tb("edge_norm", [P, ET])
        dumpi = tb("dump_int", [P, 1], I32)
        fac = tb("factors", [C, 20, C])
        UT = tb("prod_T", [C, 4, C])
        WT = tb("full_T", [C, 4, C])
        WR = tb("scaled_T", [C, 6, C])
        WDD = tb("wd_twice", [C, 2, C])
        pz = [loc.enter_context(nc.psum_tensor(f"pz{i}", [128, 512], F32)) for i in range(8)]
        s_load, s_zeroed, s_zero, s_out = sem("su_loaded"), sem("su_acc_zeroed"), sem("su_zero_ready"), sem("su_x")
        s_iota, s_link, s_ulink, s_pe, s_cp = sem("su_iota"), sem("su_dve_step"), sem("su_pool_step"), sem("su_product"), sem("su_copied")
        NAMES = ["ls0T", "ls1T", "w00", "w11", "w01", "w10", "lh0", "lh1", "t00", "t11", "t01", "t10"]
        loads = [(S.src[:, :], I["src_pt"]), (S.dst[:, :], I["dst_pt"]), (ev[:, :, :], I["ea3"]), (S.sh0[:, :, :], I["ea4"]),
                 (S.lsc[:, :], I["lsc"])]
        loads += [(fac[:, i, :], I["fac_" + n]) for i, n in enumerate(NAMES)]
        F = {n: fac[:, i, :] for i, n in enumerate(NAMES)}
        s_nrm, s_root = sem("su_norm_sq"), sem("su_norm")
        with nc.Block() as block:
            @block.scalar
            def _(act):
                act.wait_ge(s_nrm, 1)
                act.sem_inc(s_nrm, -1)
                nc.scalar.activation(nrm[:, :], nrm[:, :], ACT.Sqrt).then_inc(s_root, 1)

            @block.sync
            def _(sp):
                for to, fr in loads:
                    sp.dma_start(to, fr).then_inc(s_load, 16)
                sp.dma_start(S.x[:, :, :], I["x"].rearrange("(p t) d -> p t d", t=NT)).then_inc(s_out, 16)
                sp.wait_ge(s_zero, 1)
                for l in range(2):
                    for i in range(GT):
                        sp.dma_start(S.acc[l][i].rearrange("(p t) d -> p t d", t=26), zero[:, :, :]).then_inc(s_zeroed, 16)
                sp.wait_ge(s_zeroed, 16 * 2 * GT)
                sp.wait_ge(s_out, 16)

            @block.gpsimd
            def _(pool):
                link = linker(pool, s_ulink)
                link(nc.gpsimd.memset(S.ident[:, :], 0.0))
                link(nc.gpsimd.affine_select(out=S.ident[:, :], in_=S.ident[:, :], compare_op=ALU.not_equal, fill=1.0,
                                             base=0, pattern=[[-1, 128]], channel_multiplier=1))
                link(nc.gpsimd.memset(S.before[:, :], 1.0))
                link(nc.gpsimd.affine_select(out=S.before[:, :], in_=S.before[:, :], compare_op=ALU.is_gt, fill=0.0,
                                             base=0, pattern=[[-1, P]], channel_multiplier=1))
                nc.gpsimd.iota(dumpi[:, :], pattern=[[0, 1]], base=N, channel_multiplier=1).then_inc(s_iota, 1)

            @block.vector
            def _(dve):
                link = linker(dve, s_link)
                nc.vector.memset(zero[:, :, :], 0.0).then_inc(s_zero, 1)
                nc.vector.memset(S.ones[:, :], 1.0)
                nc.vector.memset(S.wm[0:C, 2 * C:3 * C], 0.0)
                nc.vector.memset(S.wd[:, :, :], 0.0)
                link(nc.vector.memset(WR[:, :, :], 0.0))
                dve.wait_ge(s_iota, 1)
                nc.vector.tensor_copy(S.dump[:, :], dumpi[:, :])
                dve.wait_ge(s_load, 16 * len(loads))
                nc.vector.tensor_copy(S.dstf[:, :], S.dst[:, :])
                link(nc.vector.tensor_tensor(sq[:, :, :], ev[:, :, :], ev[:, :, :], ALU.mult))
                link(nc.vector.tensor_reduce(nrm[:, :], sq[:, :, :], AX, ALU.add))
                dve.sem_inc(s_nrm, 1)
                dve.wait_ge(s_root, 1)
                dve.sem_inc(s_root, -1)
                link(nc.vector.tensor_scalar(nrm[:, :], nrm[:, :], 1e-12, None, ALU.add))
                link(nc.vector.reciprocal(nrm[:, :], nrm[:, :]))
                link(nc.vector.tensor_scalar(nrm[:, :], nrm[:, :], SQ3, None, ALU.mult))
                link(nc.vector.tensor_tensor(S.shn[:, :, :], ev[:, :, :], bc(nrm[:, :], 3, 2), ALU.mult))
                link(nc.vector.tensor_tensor(sq[:, :, :], S.shn[:, :, :], S.shn[:, :, :], ALU.mult))
                link(nc.vector.tensor_reduce(S.q[:, :], sq[:, :, :], AX, ALU.add))
                k = INV_MUL * INV_TP * INV_MUL
                dve.wait_ge(s_pe, 1)
                for i, f in enumerate((k / SQ3, k, k, k)):
                    ins = nc.vector.tensor_scalar(UT[:, i, :], pz[0][0:C, i * C:(i + 1) * C], f, None, ALU.mult)
                ins.then_inc(s_cp, 1)
                dve.wait_ge(s_pe, 2)
                nc.vector.tensor_copy(S.wh[:, :], pz[1][:, 0:C])
                link(nc.vector.tensor_copy(WT[:, :, :].rearrange("p a b -> p (a b)"), pz[2][0:C, 0:4 * C]))
                nc.vector.tensor_scalar(WR[:, 0, :], WT[:, 2, :], 1.0 / SQ3, None, ALU.mult)
                nc.vector.tensor_copy(WR[:, 3, :], WT[:, 3, :])
                nc.vector.tensor_scalar(WR[:, 5, :], WT[:, 3, :], 1.0 / SQ3, None, ALU.mult)
                nc.vector.tensor_copy(WDD[:, 0, :], WT[:, 2, :])
                nc.vector.tensor_copy(WDD[:, 1, :], WT[:, 2, :]).then_inc(s_cp, 1)
                dve.wait_ge(s_pe, 3)
                nc.vector.tensor_scalar(S.wm[:, :], pz[3][:, 0:3 * C], INV_TP, None, ALU.mult)
                for h in range(2):
                    rows = slice(C * h, C * (h + 1))
                    nc.vector.tensor_scalar(S.wd[rows, 1, rows], pz[4][rows, 0:C], INV_TP, None, ALU.mult)
                nc.vector.tensor_scalar(S.wd[C:128, 0, 0:C], pz[4][C:128, 0:C], INV_TP, None, ALU.mult)
                nc.vector.tensor_scalar(S.lsc[:, :], S.lsc[:, :], INV_MUL, None, ALU.mult).then_inc(s_cp, 1)
                dve.wait_ge(s_cp, 3)

            @block.tensor
            def _(pe):
                pe.wait_ge(s_load, 16 * len(loads))
                for i, (a, b) in enumerate((("w11", "ls1T"), ("w00", "ls0T"), ("w10", "ls1T"), ("w01", "ls0T"))):
                    ins = nc.tensor.matmul(pz[0][0:C, i * C:(i + 1) * C], F[a], F[b], start=True, stop=True)
                ins.then_inc(s_pe, 1)
                pe.wait_ge(s_cp, 1)
                nc.tensor.matmul(pz[1][:, 0:C], UT[:, 0:2, :].rearrange("p a b -> p (a b)"), F["lh0"], start=True, stop=True)
                nc.tensor.matmul(pz[2][0:C, 0:2 * C], F["lh0"], UT[:, 0:2, :].rearrange("p a b -> p (a b)"),
                                 start=True, stop=True)
                nc.tensor.matmul(pz[2][0:C, 2 * C:4 * C], F["lh1"], UT[:, 2:4, :].rearrange("p a b -> p (a b)"),
                                 start=True, stop=True).then_inc(s_pe, 1)
                pe.wait_ge(s_cp, 2)
                hT = WT[:, 0:2, :].rearrange("p a b -> p (a b)")

                def pair(i):
                    return WR[:, i:i + 2, :].rearrange("p a b -> p (a b)")
                nc.tensor.matmul(pz[3][:, 0:C], hT, F["t00"], start=True, stop=False)
                nc.tensor.matmul(pz[3][:, 0:C], pair(0), F["t11"], start=False, stop=True)
                nc.tensor.matmul(pz[3][:, C:2 * C], hT, F["t01"], start=True, stop=False)
                nc.tensor.matmul(pz[3][:, C:2 * C], pair(2), F["t10"], start=False, stop=True)
                nc.tensor.matmul(pz[3][:, 2 * C:3 * C], pair(4), F["t11"], start=True, stop=True)
                nc.tensor.matmul(pz[4][:, 0:C], WDD[:, :, :].rearrange("p a b -> p (a b)"), F["t10"],
                                 start=True, stop=True).then_inc(s_pe, 1)



def normalise(nc, dve, link, x, h, st, s_var, s_std):
    for j in range(CT):
        ins = nc.vector.bn_stats(st[:, j, 0:6], x[:, j, :])
    link(ins)
    for j in range(CT):
        ins = nc.vector.bn_aggr(st[:, j, 6:8], st[:, j, 0:6])
    link(ins)
    nc.vector.tensor_scalar(st[:, :, 8:9], st[:, :, 7:8], LN_EPS, None, ALU.add).then_inc(s_var, 1)
    dve.wait_ge(s_std, 1)
    dve.sem_inc(s_std, -1)
    link(nc.vector.reciprocal(st[:, :, 8:9], st[:, :, 8:9]))
    for j in range(CT):
        ins = nc.vector.tensor_scalar(h[:, j, :], x[:, j, :], st[:, j, 6:7], st[:, j, 8:9], ALU.subtract, ALU.mult)
    return ins


def root(nc, act, st, s_var, s_std):
    act.wait_ge(s_var, 1)
    act.sem_inc(s_var, -1)
    nc.scalar.activation(st[:, :, 8:9], st[:, :, 8:9], ACT.Sqrt).then_inc(s_std, 1)


def turn(nc, h, ident, pst):
    for i in range(2 * CT):
        j, k = i // 2, i % 2
        ins = nc.tensor.transpose(pst[:, i // 4, (i % 4) * P:(i % 4 + 1) * P], h[:, j, k * 128:(k + 1) * 128],
                                  ident[0:P, 0:P])
    return ins


def turned(nc, pst, hT):
    for i in range(3):
        n = min(4, 2 * CT - 4 * i) // 2
        o = hT[:, :, 2 * i * P:(2 * i + n) * P].rearrange("p k (j e) -> p j k e", j=n)
        ins = nc.scalar.copy(o, pst[:, i, 0:2 * n * P].rearrange("p (j k e) -> p j k e", j=n, k=2))
    return ins


def linear(nc, hT, w0, w1, pso):
    for j in range(CT):
        for k, w in enumerate((w0, w1)):
            o = (j % 2) * 256 + k * 128
            ins = nc.tensor.matmul(pso[:, j // 2, o:o + 128], hT[:, k, j * P:(j + 1) * P], w, start=True, stop=True)
    return ins


def banks(pso, b):
    n = min(2, CT - 2 * b)
    return pso[:, b, 0:256 * n].rearrange("p (n d) -> p n d", d=256), slice(2 * b, 2 * b + n)



def first_nodes(nc, ctx, I, S):
    def sem(name):
        return S.signals.get("fn", name)

    with ExitStack() as loc:
        def tb(name, shape, dt=F32):
            return loc.enter_context(nc.sbuf_tensor(name, shape, dt))
        h, st, hT = tb("fn_h", [P, CT, D]), tb("fn_st", [P, CT, 9]), tb("fn_hT", [128, 2, CN])
        up = tb("fn_up", [P, CT, D])
        bd = tb("fn_bd", [128, 4, 128])
        pst = loc.enter_context(nc.psum_tensor("fn_pst", [128, 3, 512], F32))
        pso = loc.enter_context(nc.psum_tensor("fn_pso", [P, 3, 512], F32))
        s_bz, s_w, s_link, s_h, s_t, s_hT = sem("bd_zero"), sem("weights"), sem("dve_step"), sem("h_ready"), sem("turned"), sem("hT_ready")
        s_hfree, s_own = sem("h_free"), sem("act_step")
        s_var, s_std = sem("variance"), sem("deviation")
        s_up, s_upc, s_sc, s_scc, s_upd, s_upg = sem("up"), sem("up_copied"), sem("skip"), sem("skip_copied"), sem("table"), sem("table_ok")
        with nc.Block() as block:
            @block.sync
            def _(sp):
                sp.wait_ge(s_bz, 1)
                sp.sem_inc(s_bz, -1)
                for i, (a, b) in enumerate(((I["Wup0"], I["Wup1"]), (I["Wup1"], I["Wup1"]), (I["Wsc0"], I["Wsc1"]), (I["Wsc1"], I["Wsc1"]))):
                    sp.dma_start(bd[0:C, i, 0:C], a).then_inc(s_w, 16)
                    sp.dma_start(bd[C:128, i, C:128], b).then_inc(s_w, 16)
                rows = S.table1.rearrange("(p t) d -> p t d", t=NT)
                with sp.Fori(0, CHUNKS) as c:
                    sp.wait_ge(s_upc, 1)
                    sp.sem_inc(s_upc, -1)
                    sp.dma_start(rows[:, bass.ds(c * CT, CT), :], up[:, :, :]).then_inc(s_upd, 16)
                    sp.wait_ge(s_upd, 16 * c + 16)
                    sp.sem_inc(s_upg, 1)

            @block.vector
            def _(dve):
                link = linker(dve, s_link)
                nc.vector.memset(bd[:, :, :], 0.0).then_inc(s_bz, 1)
                with dve.Fori(0, CHUNKS) as c:
                    normalise(nc, dve, link, S.x[:, bass.ds(c * CT, CT), :], h, st, s_var, s_std).then_inc(s_h, 1)
                    dve.wait_ge(s_hfree, 1)
                    dve.sem_inc(s_hfree, -1)

            @block.tensor
            def _(pe):
                pe.wait_ge(s_w, 16 * 8)
                with pe.Fori(0, CHUNKS) as c:
                    pe.wait_ge(s_h, 1)
                    pe.sem_inc(s_h, -1)
                    turn(nc, h, S.ident, pst).then_inc(s_t, 1)
                    pe.wait_ge(s_hT, 1)
                    pe.sem_inc(s_hT, -1)
                    linear(nc, hT, bd[:, 0, :], bd[:, 1, :], pso).then_inc(s_up, 1)
                    pe.wait_ge(s_scc, 1)
                    pe.sem_inc(s_scc, -1)
                    linear(nc, hT, bd[:, 2, :], bd[:, 3, :], pso).then_inc(s_sc, 1)
                    pe.wait_ge(s_scc, 1)
                    pe.sem_inc(s_scc, -1)

            @block.scalar
            def _(act):
                act.sem_inc(s_upg, 1)
                with act.Fori(0, CHUNKS) as c:
                    root(nc, act, st, s_var, s_std)
                    act.wait_ge(s_t, 1)
                    act.sem_inc(s_t, -1)
                    act.sem_inc(s_hfree, 1)
                    turned(nc, pst, hT).then_inc(s_hT, 1)
                    act.wait_ge(s_up, 1)
                    act.sem_inc(s_up, -1)
                    act.wait_ge(s_upg, 1)
                    act.sem_inc(s_upg, -1)
                    for b in range(3):
                        v, r = banks(pso, b)
                        ins = nc.scalar.copy(up[:, r, :], v)
                    tell(act, ins, s_own, s_scc, s_upc)
                    act.wait_ge(s_sc, 1)
                    act.sem_inc(s_sc, -1)
                    for b in range(3):
                        v, r = banks(pso, b)
                        ins = nc.scalar.copy(S.skip[:, bass.ds(c * CT + r.start, r.stop - r.start), :], v)
                    ins.then_inc(s_scc, 1)



class Edge:
    def __init__(self, it, c):
        self.g = it * 2 + c
        self.slot = c % 2
        self.use = it + (c // 2 + 1)


def edge_buffers(nc, loc, S, name):
    def tb(n, shape, dt=F32):
        return loc.enter_context(nc.sbuf_tensor(f"{name}_{n}", shape, dt))

    def sem(n):
        return S.signals.get(name, n)
    B = Buffers()
    B.take_i = [tb(f"gather_idx{s}", [P, GT], I32) for s in range(2)]
    B.put_i = [tb(f"scatter_idx{s}", [P, GT], I32) for s in range(2)]
    B.row = [tb(f"dst_row{s}", [128, GE], I32) for s in range(2)]
    B.same = [tb(f"same{s}", [P, GT, P]) for s in range(2)]
    B.msg = [tb(f"msg{s}", [P, GT, D]) for s in range(2)]
    B.sum = [tb(f"sum{s}", [P, GT, D]) for s in range(2)]
    B.got = [sem(f"gathered{s}") for s in range(2)]
    B.put = [sem(f"scattered{s}") for s in range(2)]
    B.row_in = [sem(f"dst_row_in{s}") for s in range(2)]
    B.row_free = sem("dst_row_free")
    B.idx_ready = sem("gather_index_ready")
    B.got_free = sem("gathered_free")
    B.msg_ready = sem("messages_ready")
    B.msg_free = sem("messages_used")
    B.sum_ps = sem("sums_in_psum")
    B.sum_ps_free = sem("sums_psum_free")
    B.sum_ready = sem("sums_ready")
    B.sum_free = sem("sums_scattered")
    B.put_free = sem("scatter_index_free")
    B.own = sem("act_step")
    B.passed = sem("dma_waits_passed")
    return B


def edge_pool(nc, pool, B, table, got, acc):
    def gather(e):
        pool.wait_ge(B.idx_ready, 1)
        pool.sem_inc(B.idx_ready, -1)
        pool.wait_ge(B.got_free, 1)
        pool.sem_inc(B.got_free, -1)
        for j in range(GT):
            pool.indirect_dma_start(got(e.slot, j), None, table,
                                    bass.IndirectOffsetOnAxis(B.take_i[e.slot][:, j:j + 1], 0)).then_inc(B.got[e.slot], 16)

    def scatter(e, before):
        if before is not None:
            pool.wait_ge(B.put[before.slot], 16 * GT * before.use)
            pool.sem_inc(B.sum_free, 1)
            pool.sem_inc(B.put_free, 1)
        pool.wait_ge(B.sum_ready, 1)
        pool.sem_inc(B.sum_ready, -1)
        for j in range(GT):
            pool.indirect_dma_start(acc[j], bass.IndirectOffsetOnAxis(B.put_i[e.slot][:, j:j + 1], 0),
                                    B.sum[e.slot][:, j, :], None, compute_op=ALU.add).then_inc(B.put[e.slot], 16)
    gather(Edge(0, 0))
    gather(Edge(0, 1))
    gather(Edge(0, 2))
    scatter(Edge(0, 0), None)

    def body(it, c):
        gather(Edge(it, c + 2))
        scatter(Edge(it, c), Edge(it, c - 1))
    pairs = (G - 4) // 2
    with pool.Fori(0, pairs) as it:
        body(it, 1)
        body(it, 2)
    body(pairs, 1)
    scatter(Edge(pairs, 2), Edge(pairs, 1))
    scatter(Edge(pairs, 3), Edge(pairs, 2))
    for s in range(2):
        pool.wait_ge(B.put[s], 16 * GT * (G // 2))


def load_row(sp, I, B, e):
    sp.wait_ge(B.row_free, 1)
    sp.sem_inc(B.row_free, -1)
    sp.dma_start(B.row[e.slot][:, :], I["dst_row"][:, bass.ds(e.g * GE, GE)].broadcast_to([128, GE])).then_inc(
        B.row_in[e.slot], 16)


def make_same(nc, dve, link, S, B, e):
    dve.wait_ge(B.msg_free, 1)
    dve.sem_inc(B.msg_free, -1)
    dve.wait_ge(B.row_in[e.slot], 16 * e.use)
    dve.sem_inc(B.passed, 1)
    link(nc.vector.tensor_tensor(B.same[e.slot][:, :, :],
                                 B.row[e.slot][0:P, :].rearrange("p (t f) -> p t f", t=GT),
                                 bc(S.dstf[:, bass.ds(e.g * GT, GT)], P, 2), ALU.is_equal))


def sum_matmuls(nc, pe, B, e, pss):
    pe.wait_ge(B.msg_ready, 1)
    pe.sem_inc(B.msg_ready, -1)
    pe.wait_ge(B.sum_ps_free, 1)
    pe.sem_inc(B.sum_ps_free, -1)
    for j in range(GT):
        ins = nc.tensor.matmul(pss[:, j // 2, (j % 2) * D:(j % 2 + 1) * D], B.same[e.slot][:, j, :],
                               B.msg[e.slot][:, j, :], start=True, stop=True)
    ins.then_inc(B.sum_ps, 1)


def sum_copy(nc, act, B, e, pss):
    act.wait_ge(B.sum_ps, 1)
    act.sem_inc(B.sum_ps, -1)
    act.sem_inc(B.msg_free, 1)
    act.wait_ge(B.sum_free, 1)
    act.sem_inc(B.sum_free, -1)
    for b in range(2):
        ins = nc.scalar.copy(B.sum[e.slot][:, 2 * b:2 * b + 2, :],
                             pss[:, b, :].rearrange("p (n d) -> p n d", d=D))
    tell(act, ins, B.own, B.sum_ready, B.sum_ps_free)


def first_edges(nc, ctx, I, S):
    with ExitStack() as loc:
        def tb(name, shape, dt=F32):
            return loc.enter_context(nc.sbuf_tensor(f"e1_{name}", shape, dt))

        def sem(n):
            return S.signals.get("e1", n)
        B = edge_buffers(nc, loc, S, "e1")
        got = [tb(f"got{s}", [P, GT, D]) for s in range(2)]
        rbf = [tb(f"rbf{s}", [R, GE]) for s in range(2)]
        r = [tb(f"r{i}", [HID, GE]) for i in range(3)]
        w = [tb(f"tpw{s}", [P, GT, D]) for s in range(2)]
        prod = tb("prod", [P, GT, 3, C])
        q = tb("q", [P, GT, C])
        q3 = tb("q3", [P, GT, C])
        a = tb("a", [P, GT, C])
        count = tb("count", [P, GT])
        junk = tb("junk", [P, GT, P])
        putf = tb("putf", [P, GT])
        sh3 = tb("sh3", [P, ET, 3])
        M1, M2, M3, M4 = tb("M1", [R, HID]), tb("M2", [HID, HID]), tb("M3", [HID, HID]), tb("M4", [HID, D])
        ps_m = [loc.enter_context(nc.psum_tensor(f"e1_psm{i}", [HID, 512], F32)) for i in range(2)]
        ps_w = loc.enter_context(nc.psum_tensor("e1_psw", [P, 2, 512], F32))
        pss = loc.enter_context(nc.psum_tensor("e1_pss", [P, 2, 512], F32))
        s_w, rbf_in = sem("weights"), [sem(f"rbf_in{s}") for s in range(2)]
        rbf_free, s_m, s_r, s_wp, wp_free, w_ready, w_free = (sem(n) for n in (
            "rbf_free", "hidden_in_psum", "hidden_ready", "tpw_in_psum", "tpw_psum_free", "tpw_ready", "tpw_free"))
        s_link = sem("dve_step")

        def rbf_load(sp, e):
            sp.wait_ge(rbf_free, 1)
            sp.sem_inc(rbf_free, -1)
            sp.dma_start(rbf[e.slot][:, :], I["rbfT"][:, bass.ds(e.g * GE, GE)]).then_inc(rbf_in[e.slot], 16)

        with nc.Block() as block:
            @block.sync
            def _(sp):
                for to, fr in ((M1, I["M1"]), (M2, I["M2"]), (M3, I["M3"]), (M4, I["M4"])):
                    sp.dma_start(to[:, :], fr).then_inc(s_w, 16)
                load_experts(nc, sp, S, 0)
                with sp.Fori(0, G // 2) as it:
                    for c in range(2):
                        rbf_load(sp, Edge(it, c))
                        load_row(sp, I, B, Edge(it, c))

            @block.gpsimd
            def _(pool):
                edge_pool(nc, pool, B, S.table1, lambda s, j: got[s][:, j, :], S.acc[0])

            @block.tensor
            def _(pe):
                pe.sem_inc(rbf_free, 2)
                pe.sem_inc(B.msg_free, 2)
                pe.wait_ge(s_w, 64)

                def mlp1(e):
                    pe.wait_ge(rbf_in[e.slot], 16 * e.use)
                    pe.sem_inc(B.passed, 1)
                    nc.tensor.matmul(ps_m[0][:, 0:GE], M1[:, :], rbf[e.slot][:, :], start=True, stop=True).then_inc(s_m, 1)

                def mlp(w, i):
                    pe.wait_ge(s_r, 1)
                    pe.sem_inc(s_r, -1)
                    nc.tensor.matmul(ps_m[1][:, 0:GE], w[:, :], r[i][:, :], start=True, stop=True).then_inc(s_m, 1)

                def tpw(e):
                    pe.wait_ge(s_r, 1)
                    pe.sem_inc(s_r, -1)
                    pe.wait_ge(wp_free, 1)
                    pe.sem_inc(wp_free, -1)
                    for j in range(GT):
                        ins = nc.tensor.matmul(ps_w[:, j // 2, (j % 2) * D:(j % 2 + 1) * D], r[2][:, j * P:(j + 1) * P],
                                               M4[:, :], start=True, stop=True)
                    ins.then_inc(s_wp, 1)

                def body(it, c, sums=True):
                    mlp1(Edge(it, c + 1))
                    tpw(Edge(it, c))
                    mlp(M2, 0)
                    if sums:
                        sum_matmuls(nc, pe, B, Edge(it, c - 1), pss)
                    mlp(M3, 1)
                mlp1(Edge(0, 0))
                mlp(M2, 0)
                mlp(M3, 1)
                body(0, 0, False)
                with pe.Fori(0, (G - 2) // 2) as it:
                    body(it, 1)
                    body(it, 2)
                last = Edge((G - 2) // 2, 1)
                tpw(last)
                sum_matmuls(nc, pe, B, Edge((G - 2) // 2, 0), pss)
                sum_matmuls(nc, pe, B, last, pss)

            @block.scalar
            def _(act):
                act.sem_inc(B.sum_free, 2)
                act.sem_inc(wp_free, 1)
                act.sem_inc(B.sum_ps_free, 1)

                def silu(i):
                    act.wait_ge(s_m, 1)
                    act.sem_inc(s_m, -1)
                    nc.scalar.activation(r[i][:, :], ps_m[min(i, 1)][:, 0:GE], ACT.Silu).then_inc(s_r, 1)
                    if i == 0:
                        act.sem_inc(rbf_free, 1)

                def tpw(e):
                    act.wait_ge(s_wp, 1)
                    act.sem_inc(s_wp, -1)
                    act.wait_ge(w_free, 1)
                    act.sem_inc(w_free, -1)
                    for j in range(GT):
                        v = ps_w[:, j // 2, (j % 2) * D:(j % 2 + 1) * D]
                        nc.scalar.activation(w[e.slot][:, j, 0:2 * C], v[:, 0:2 * C], ACT.Copy,
                                             scale=S.sh0[:, bass.ds(e.g * GT + j, 1), 0:1].rearrange("p a b -> p (a b)"))
                    for b in range(2):
                        v = ps_w[:, b, :].rearrange("p (n d) -> p n d", d=D)
                        ins = nc.scalar.copy(w[e.slot][:, 2 * b:2 * b + 2, 2 * C:D], v[:, :, 2 * C:D])
                    tell(act, ins, B.own, w_ready, wp_free)

                def sums(e):
                    sum_copy(nc, act, B, e, pss)

                def body(it, c, do_sums=True):
                    silu(0)
                    tpw(Edge(it, c))
                    silu(1)
                    if do_sums:
                        sums(Edge(it, c - 1))
                    silu(2)
                silu(0)
                silu(1)
                silu(2)
                body(0, 0, False)
                with act.Fori(0, (G - 2) // 2) as it:
                    body(it, 1)
                    body(it, 2)
                last = Edge((G - 2) // 2, 1)
                tpw(last)
                sums(Edge((G - 2) // 2, 0))
                sums(last)

            @block.vector
            def _(dve):
                link = linker(dve, s_link)
                dve.sem_inc(B.row_free, 2)
                dve.sem_inc(B.got_free, 2)
                dve.sem_inc(B.put_free, 2)
                dve.sem_inc(w_free, 2)
                link(nc.vector.tensor_scalar(sh3[:, :, :], S.sh0[:, :, 1:4], 1.0 / SQ3, None, ALU.mult))

                def index(e):
                    nc.vector.tensor_copy(B.take_i[e.slot][:, :], S.src[:, bass.ds(e.g * GT, GT)]).then_inc(B.idx_ready, 1)

                def prepare(e):
                    make_same(nc, dve, link, S, B, e)
                    dve.sem_inc(B.row_free, 1)
                    link(nc.vector.tensor_tensor(junk[:, :, :], B.same[e.slot][:, :, :], bc(S.before[:, :], GT, 1), ALU.mult))
                    link(nc.vector.tensor_reduce(count[:, :], junk[:, :, :], AX, ALU.add))
                    link(nc.vector.tensor_scalar(putf[:, :], S.dstf[:, bass.ds(e.g * GT, GT)], S.dump[:, 0:1], -1.0,
                                                 ALU.subtract, ALU.mult))
                    link(nc.vector.scalar_tensor_tensor(out=putf[:, :], in0=count[:, :], scalar=0.5, in1=putf[:, :],
                                                        op0=ALU.is_gt, op1=ALU.mult))
                    dve.wait_ge(B.put_free, 1)
                    dve.sem_inc(B.put_free, -1)
                    nc.vector.tensor_tensor(B.put_i[e.slot][:, :], putf[:, :], S.dstf[:, bass.ds(e.g * GT, GT)], ALU.add)
                    link(nc.vector.tensor_tensor(S.put[:, bass.ds(e.g * GT, GT)], putf[:, :],
                                                 S.dstf[:, bass.ds(e.g * GT, GT)], ALU.add))

                def messages(e):
                    x, m, v = got[e.slot], B.msg[e.slot], w[e.slot]
                    dve.wait_ge(B.got[e.slot], 16 * GT * e.use)
                    dve.sem_inc(B.passed, 1)
                    link(nc.vector.tensor_tensor(prod[:, :, :, :], x[:, :, C:D].rearrange("p t (k c) -> p t k c", k=3),
                                                 bc(sh3[:, bass.ds(e.g * GT, GT), :], C, 3), ALU.mult))
                    link(nc.vector.tensor_tensor(q[:, :, :], prod[:, :, 0, :], prod[:, :, 1, :], ALU.add))
                    link(nc.vector.tensor_tensor(q[:, :, :], q[:, :, :], prod[:, :, 2, :], ALU.add))
                    dve.wait_ge(w_ready, 1)
                    dve.sem_inc(w_ready, -1)
                    nc.vector.tensor_tensor(q3[:, :, :], q[:, :, :], v[:, :, 3 * C:D], ALU.mult)
                    nc.vector.tensor_tensor(a[:, :, :], x[:, :, 0:C], v[:, :, 2 * C:3 * C], ALU.mult)
                    nc.vector.tensor_tensor(m[:, :, 0:C], x[:, :, 0:C], v[:, :, 0:C], ALU.mult)
                    link(nc.vector.tensor_tensor(m[:, :, C:D].rearrange("p t (k c) -> p t k c", k=3),
                                                 x[:, :, C:D].rearrange("p t (k c) -> p t k c", k=3),
                                                 bc(v[:, :, C:2 * C], 3, 2), ALU.mult))
                    dve.sem_inc(B.got_free, 1)
                    dve.sem_inc(w_free, 1)
                    nc.vector.tensor_tensor(m[:, :, 0:C], m[:, :, 0:C], q3[:, :, :], ALU.add)
                    for j in range(GT):
                        for k in range(3):
                            o = m[:, j, (k + 1) * C:(k + 2) * C]
                            ins = nc.vector.scalar_tensor_tensor(
                                out=o, in0=a[:, j, :],
                                scalar=S.sh0[:, bass.ds(e.g * GT + j, 1), k + 1:k + 2].rearrange("p a b -> p (a b)"),
                                in1=o, op0=ALU.mult, op1=ALU.add)
                    ins.then_inc(B.msg_ready, 1)

                index(Edge(0, 0))
                index(Edge(0, 1))
                prepare(Edge(0, 0))

                def body(it, c, more=True):
                    messages(Edge(it, c))
                    if more:
                        index(Edge(it, c + 2))
                    prepare(Edge(it, c + 1))
                with dve.Fori(0, (G - 2) // 2) as it:
                    body(it, 0)
                    body(it, 1)
                body((G - 2) // 2, 0, False)
                messages(Edge((G - 2) // 2, 1))



def load_sums(sp, acc, to, s_in, c):
    for i in range(GT):
        rows = acc[i][0:N, :].rearrange("(p t) d -> p t d", t=NT)
        sp.dma_start(to[:, i, :, :], rows[:, bass.ds(c * CT, CT), :]).then_inc(s_in, 16)


def last_nodes(nc, ctx, I, S):
    def sem(name):
        return S.signals.get("ln", name)

    with ExitStack() as loc:
        def tb(name, shape, dt=F32):
            return loc.enter_context(nc.sbuf_tensor("ln_" + name, shape, dt))
        a4 = tb("acc", [P, GT, CT, D])
        hT = tb("hT", [128, 2, CN])
        A, Bm, sq = tb("A", [P, CT, D]), tb("B", [P, CT, D]), tb("sq", [P, CT, 3, C])
        vv, a2, t1, t2, t3 = (tb(n, [P, CT, C]) for n in ("vv", "a2", "t1", "t2", "t3"))
        big = tb("squares", [P, NT, D])
        bd = tb("bd", [128, 4, 128])
        wc0, wc1 = tb("wc0", [P, 5, C]), tb("wc1", [P, 4, C])
        gam = tb("gam", [P, 3, C])
        mu = tb("mu", [P, C])
        var = tb("var", [P, 2, C])
        fac = tb("fac", [P, 4, C])
        pst = loc.enter_context(nc.psum_tensor("ln_pst", [128, 3, 512], F32))
        pso = loc.enter_context(nc.psum_tensor("ln_pso", [P, 3, 512], F32))
        pstat = loc.enter_context(nc.psum_tensor("ln_pstat", [128, 2, 512], F32))
        (s_bz, s_w, s_in, s_a4free, s_h, s_t, s_hT, s_A, s_Ac, s_B, s_t2, s_o, s_od, s_link, s_st, s_sq, s_var, s_std, s_cent,
         s_pass) = (sem(n) for n in (
             "bd_zero", "weights", "acc_in", "acc_free", "sum_ready", "turned", "hT_ready", "A_in_psum", "A_ready", "B_ready",
             "B_turned", "out_in_psum", "out_used", "dve_step", "stat_in_psum", "squares_ready", "variance", "deviation",
             "centred", "dma_waits_passed"))
        with nc.Block() as block:
            @block.sync
            def _(sp):
                for to, fr in ((wc0, I["Wc0r"]), (wc1, I["Wc1r"]), (gam, I["gam"])):
                    sp.dma_start(to[:, :, :].rearrange("p a b -> p (a b)"), fr.broadcast_to([P, fr.shape[1]])).then_inc(s_w, 16)
                sp.wait_ge(s_bz, 1)
                sp.sem_inc(s_bz, -1)
                for i, (a, b) in enumerate(((I["Wlin0"], I["Wlin1"]), (I["Wlin1"], I["Wlin1"]), (I["WB0"], I["WB1"]), (I["WB1"], I["WB1"]))):
                    sp.dma_start(bd[0:C, i, 0:C], a).then_inc(s_w, 16)
                    sp.dma_start(bd[C:128, i, C:128], b).then_inc(s_w, 16)
                with sp.Fori(0, CHUNKS) as c:
                    sp.wait_ge(s_a4free, 1)
                    sp.sem_inc(s_a4free, -1)
                    load_sums(sp, S.acc[0], a4, s_in, c)

            @block.vector
            def _(dve):
                link = linker(dve, s_link)
                nc.vector.memset(bd[:, :, :], 0.0).then_inc(s_bz, 1)
                dve.sem_inc(s_a4free, 1)
                dve.wait_ge(s_w, 16 * 11)
                TT, TS = nc.vector.tensor_tensor, nc.vector.tensor_scalar

                def w(t, i):
                    return bc(t[:, i, :], CT, 1)
                with dve.Fori(0, CHUNKS) as c:
                    dve.wait_ge(s_in, 16 * GT * c + 16 * GT)
                    dve.sem_inc(s_pass, 1)
                    TT(a4[:, 0, :, :], a4[:, 0, :, :], a4[:, 1, :, :], ALU.add)
                    link(TT(a4[:, 2, :, :], a4[:, 2, :, :], a4[:, 3, :, :], ALU.add))
                    TT(a4[:, 0, :, :], a4[:, 0, :, :], a4[:, 2, :, :], ALU.add).then_inc(s_h, 1)
                    dve.wait_ge(s_Ac, 1)
                    dve.sem_inc(s_Ac, -1)
                    dve.sem_inc(s_a4free, 1)
                    A0, A1 = A[:, :, 0:C], A[:, :, C:D].rearrange("p t (k c) -> p t k c", k=3)
                    TT(a2[:, :, :], A0, A0, ALU.mult)
                    link(TT(sq[:, :, :, :], A1, A1, ALU.mult))
                    link(TT(vv[:, :, :], sq[:, :, 0, :], sq[:, :, 1, :], ALU.add))
                    TT(t1[:, :, :], A0, w(wc0, 3), ALU.mult)
                    link(TT(vv[:, :, :], vv[:, :, :], sq[:, :, 2, :], ALU.add))
                    TT(t2[:, :, :], vv[:, :, :], w(wc0, 4), ALU.mult)
                    TT(t3[:, :, :], vv[:, :, :], w(wc0, 2), ALU.mult)
                    link(TT(t1[:, :, :], t1[:, :, :], w(wc0, 1), ALU.add))
                    link(TT(t2[:, :, :], t2[:, :, :], w(wc0, 0), ALU.add))
                    TT(t1[:, :, :], t1[:, :, :], a2[:, :, :], ALU.mult)
                    link(TT(t2[:, :, :], t2[:, :, :], A0, ALU.mult))
                    link(TT(t1[:, :, :], t1[:, :, :], t2[:, :, :], ALU.add))
                    TT(Bm[:, :, 0:C], t1[:, :, :], t3[:, :, :], ALU.add)
                    TT(t2[:, :, :], A0, w(wc1, 1), ALU.mult)
                    TT(vv[:, :, :], vv[:, :, :], w(wc1, 3), ALU.mult)
                    link(TT(a2[:, :, :], a2[:, :, :], w(wc1, 2), ALU.mult))
                    TT(t2[:, :, :], t2[:, :, :], w(wc1, 0), ALU.add)
                    link(TT(a2[:, :, :], a2[:, :, :], vv[:, :, :], ALU.add))
                    link(TT(t2[:, :, :], t2[:, :, :], a2[:, :, :], ALU.add))
                    TT(Bm[:, :, C:D].rearrange("p t (k c) -> p t k c", k=3), A1, bc(t2[:, :, :], 3, 2), ALU.mult).then_inc(s_B, 1)
                    dve.wait_ge(s_o, 1)
                    dve.sem_inc(s_o, -1)
                    for b in range(3):
                        v, r = banks(pso, b)
                        k = S.skip[:, bass.ds(c * CT + r.start, r.stop - r.start), :]
                        ins = TT(k, k, v, ALU.add)
                    ins.then_inc(s_od, 1)
                dve.wait_ge(s_st, 1)
                dve.sem_inc(s_st, -1)
                link(TS(mu[:, :], pstat[0:P, 0, 0:C], 1.0 / N, None, ALU.mult))
                TT(S.skip[:, :, 0:C], S.skip[:, :, 0:C], bc(mu[:, :], NT, 1), ALU.subtract).then_inc(s_cent, 1)
                dve.wait_ge(s_st, 1)
                dve.sem_inc(s_st, -1)
                link(TS(fac[:, :, :].rearrange("p a b -> p (a b)"), pstat[0:P, 1, 0:D], 1.0 / N, None, ALU.mult))
                link(TT(fac[:, 1, :], fac[:, 1, :], fac[:, 2, :], ALU.add))
                link(TT(fac[:, 1, :], fac[:, 1, :], fac[:, 3, :], ALU.add))
                TS(var[:, 0, :], fac[:, 0, :], LN_EPS, None, ALU.add)
                TS(var[:, 1, :], fac[:, 1, :], 1.0 / 3.0, LN_EPS, ALU.mult, ALU.add).then_inc(s_var, 1)
                dve.wait_ge(s_std, 1)
                dve.sem_inc(s_std, -1)
                link(nc.vector.reciprocal(var[:, :, :], var[:, :, :]))
                TT(fac[:, 0, :], var[:, 0, :], gam[:, 0, :], ALU.mult)
                for k in range(3):
                    ins = TT(fac[:, k + 1, :], var[:, 1, :], gam[:, 2, :], ALU.mult)
                link(ins)
                link(TT(S.skip[:, :, :], S.skip[:, :, :], bc(fac[:, :, :].rearrange("p a b -> p (a b)"), NT, 1), ALU.mult))
                link(TT(S.x[:, :, :], S.x[:, :, :], S.skip[:, :, :], ALU.add))
                link(TT(S.x[:, :, 0:C], S.x[:, :, 0:C], bc(gam[:, 1, :], NT, 1), ALU.add))

            @block.tensor
            def _(pe):
                pe.wait_ge(s_w, 16 * 11)
                with pe.Fori(0, CHUNKS) as c:
                    pe.wait_ge(s_h, 1)
                    pe.sem_inc(s_h, -1)
                    turn(nc, a4[:, 0, :, :], S.ident, pst).then_inc(s_t, 1)
                    pe.wait_ge(s_hT, 1)
                    pe.sem_inc(s_hT, -1)
                    linear(nc, hT, bd[:, 0, :], bd[:, 1, :], pso).then_inc(s_A, 1)
                    pe.wait_ge(s_B, 1)
                    pe.sem_inc(s_B, -1)
                    turn(nc, Bm, S.ident, pst).then_inc(s_t, 1)
                    pe.wait_ge(s_hT, 1)
                    pe.sem_inc(s_hT, -1)
                    linear(nc, hT, bd[:, 2, :], bd[:, 3, :], pso).then_inc(s_o, 1)
                    pe.wait_ge(s_od, 1)
                    pe.sem_inc(s_od, -1)
                for k, src in ((0, S.skip), (1, big)):
                    if k:
                        pe.wait_ge(s_sq, 1)
                        pe.sem_inc(s_sq, -1)
                    for t in range(NT):
                        ins = nc.tensor.matmul(pstat[:, k, 0:D], S.ones[:, :], src[:, t, :], start=(t == 0), stop=(t == NT - 1))
                    ins.then_inc(s_st, 1)

            @block.scalar
            def _(act):
                with act.Fori(0, CHUNKS) as c:
                    act.wait_ge(s_t, 1)
                    act.sem_inc(s_t, -1)
                    turned(nc, pst, hT).then_inc(s_hT, 1)
                    act.wait_ge(s_A, 1)
                    act.sem_inc(s_A, -1)
                    for b in range(3):
                        v, r = banks(pso, b)
                        ins = nc.scalar.copy(A[:, r, :], v)
                    ins.then_inc(s_Ac, 1)
                    act.wait_ge(s_t, 1)
                    act.sem_inc(s_t, -1)
                    turned(nc, pst, hT).then_inc(s_hT, 1)
                act.wait_ge(s_cent, 1)
                act.sem_inc(s_cent, -1)
                nc.scalar.activation(big[:, :, :], S.skip[:, :, :], ACT.Square).then_inc(s_sq, 1)
                act.wait_ge(s_var, 1)
                act.sem_inc(s_var, -1)
                nc.scalar.activation(var[:, :, :], var[:, :, :], ACT.Sqrt).then_inc(s_std, 1)



def mixture(nc, ctx, I, S, layer, out=None):
    pre = f"m{layer}_"
    hid = 2 if layer == 0 else 4
    steps = 2 if layer == 0 else 1

    def sem(name):
        return S.signals.get(pre, name)

    with ExitStack() as loc:
        def tb(name, shape, dt=F32):
            return loc.enter_context(nc.sbuf_tensor(pre + name, shape, dt))
        h, st, hT = tb("h", [P, CT, D]), tb("st", [P, CT, 9]), tb("hT", [128, 2, CN])
        a4 = tb("acc", [P, GT, CT, D]) if layer else None
        hid1 = [tb(f"hid{i}", [128, hid, CN]) for i in range(2)]
        wr, bo = tb("gate_w", [128, 2, NEXP]), tb("out_bias", [NEXP, D])
        br = tb("gate_b", [P, 2, NEXP])
        lg, ex = tb("logits", [P, CT, NEXP]), tb("exps", [P, CT, NEXP])
        m8, i8, i8f = tb("best", [P, CT, 8]), tb("best_i", [P, CT, 8], U32), tb("best_f", [P, CT, 8])
        iota_i, iota = tb("iota_i", [P, NEXP], I32), tb("iota", [P, NEXP])
        s1 = tb("s1", [P, CT, 4])
        wg = tb("weights", [P, CT, NEXP])
        wT = tb("weights_T", [NEXP, CN])
        psh = loc.enter_context(nc.psum_tensor(pre + "psh", [128, 4, 512], F32))
        pso = loc.enter_context(nc.psum_tensor(pre + "pso", [P, 3, 512], F32))
        pst, psg = psh[:, 0:3, :], psh[0:P, 3, 0:CT * NEXP]
        bn = tb("bn", [128, 5, 2, 16]) if layer == 0 else None
        b1 = None if layer == 0 else tb("b1", [128, 32])
        (s_w, s_in, s_free4, s_var, s_std, s_h, s_t, s_hT, s_g, s_lg, s_ex, s_wg, s_wt, s_wT, s_b, s_bd, s_m, s_ev, s_o, s_od,
         s_link, s_bnv, s_bns, s_aff, s_pass, s_iota, s_x, s_out) = (sem(n) for n in (
             "small_weights", "acc_in", "acc_free", "variance", "deviation", "h_ready", "turned", "hT_ready", "gates_in_psum",
             "logits_ready", "exps_ready", "gates_ready", "gates_turned", "gates_T_ready", "bias_in_psum", "bias_added",
             "hidden_in_psum", "hidden_ready", "out_in_psum", "out_added", "dve_step", "bn_variance", "bn_deviation",
             "affine_ready", "dma_waits_passed", "iota", "x_ready", "stored"))
        smalls = [(wr[:, :, :], (I["Wr"] if layer == 0 else I["Wg"]).rearrange("(k p) e -> p k e", p=128)),
                  (bo[:, :], I["bo"] if layer == 0 else I["b2"])]
        if layer == 0:
            smalls += [(br[:, 0, :], I["br"].broadcast_to([P, NEXP])), (bn[:, :, :, :], I["bn"])]
        else:
            smalls += [(br[:, 0, :], I["bg"].broadcast_to([P, NEXP])), (br[:, 1, :], I["bias"].broadcast_to([P, NEXP])), (b1[:, :], I["b1"])]
        with nc.Block() as block:
            @block.sync
            def _(sp):
                for to, fr in smalls:
                    sp.dma_start(to, fr).then_inc(s_w, 16)
                if layer:
                    rows = out.rearrange("(p t) d -> p t d", t=NT)
                    with sp.Fori(0, CHUNKS) as c:
                        sp.wait_ge(s_free4, 1)
                        sp.sem_inc(s_free4, -1)
                        load_sums(sp, S.acc[1], a4, s_in, c)
                    with sp.Fori(0, CHUNKS) as c:
                        sp.wait_ge(s_x, 1)
                        sp.sem_inc(s_x, -1)
                        sp.dma_start(rows[:, bass.ds(c * CT, CT), :], S.x[:, bass.ds(c * CT, CT), :]).then_inc(s_out, 16)
                    sp.wait_ge(s_out, 16 * CHUNKS)

            @block.gpsimd
            def _(pool):
                nc.gpsimd.iota(iota_i[:, :], pattern=[[1, NEXP]], base=0, channel_multiplier=0).then_inc(s_iota, 1)

            @block.vector
            def _(dve):
                link = linker(dve, s_link)
                TT, TS, STT = nc.vector.tensor_tensor, nc.vector.tensor_scalar, nc.vector.scalar_tensor_tensor
                dve.wait_ge(s_iota, 1)
                nc.vector.tensor_copy(iota[:, :], iota_i[:, :])
                dve.wait_ge(s_w, 16 * len(smalls))
                if layer == 0:
                    TS(bn[:, 4, :, :], bn[:, 4, :, :], BN_EPS, None, ALU.add).then_inc(s_bnv, 1)
                    dve.wait_ge(s_bns, 1)
                    dve.sem_inc(s_bns, -1)
                    TT(bn[:, 1, :, :], bn[:, 1, :, :], bn[:, 3, :, :], ALU.subtract)
                    link(nc.vector.reciprocal(bn[:, 4, :, :], bn[:, 4, :, :]))
                    link(TT(bn[:, 0, :, :], bn[:, 0, :, :], bn[:, 4, :, :], ALU.mult))
                    link(TT(bn[:, 1, :, :], bn[:, 1, :, :], bn[:, 0, :, :], ALU.mult))
                    link(TT(bn[:, 2, :, :], bn[:, 2, :, :], bn[:, 1, :, :], ALU.add))
                    dve.sem_inc(s_aff, 1)
                else:
                    link(TT(br[:, 0, :], br[:, 0, :], br[:, 1, :], ALU.add))
                    dve.sem_inc(s_free4, 1)
                with dve.Fori(0, CHUNKS) as c:
                    x = S.x[:, bass.ds(c * CT, CT), :]
                    if layer:
                        dve.wait_ge(s_in, 16 * GT * c + 16 * GT)
                        dve.sem_inc(s_pass, 1)
                        TT(a4[:, 0, :, :], a4[:, 0, :, :], a4[:, 1, :, :], ALU.add)
                        link(TT(a4[:, 2, :, :], a4[:, 2, :, :], a4[:, 3, :, :], ALU.add))
                        link(TT(a4[:, 0, :, :], a4[:, 0, :, :], a4[:, 2, :, :], ALU.add))
                        link(TT(x, x, a4[:, 0, :, :], ALU.add))
                        dve.sem_inc(s_free4, 1)
                    normalise(nc, dve, link, x, h, st, s_var, s_std).then_inc(s_h, 1)
                    dve.wait_ge(s_g, 1)
                    dve.sem_inc(s_g, -1)
                    link(TT(lg[:, :, :], psg.rearrange("p (t e) -> p t e", e=NEXP), bc(br[:, 0, :], CT, 1), ALU.add))
                    if layer == 0:
                        link(nc.vector.tensor_reduce(s1[:, :, 0], lg[:, :, :], AX, ALU.max))
                        TT(lg[:, :, :], lg[:, :, :], bc(s1[:, :, 0], NEXP, 2), ALU.subtract).then_inc(s_lg, 1)
                        dve.wait_ge(s_ex, 1)
                        dve.sem_inc(s_ex, -1)
                        link(nc.vector.tensor_reduce(s1[:, :, 1], ex[:, :, :], AX, ALU.add))
                        link(nc.vector.reciprocal(s1[:, :, 1], s1[:, :, 1]))
                        TT(wg[:, :, :], ex[:, :, :], bc(s1[:, :, 1], NEXP, 2), ALU.mult).then_inc(s_wg, 1)
                    else:
                        for j in range(CT):
                            ins = nc.vector.max(m8[:, j, :], lg[:, j, :])
                        link(ins)
                        for j in range(CT):
                            ins = nc.vector.max_index(i8[:, j, :], m8[:, j, :], lg[:, j, :])
                        link(ins)
                        nc.vector.tensor_copy(i8f[:, :, :], i8[:, :, :])
                        TT(s1[:, :, 0], m8[:, :, 1], m8[:, :, 0], ALU.subtract).then_inc(s_lg, 1)
                        dve.wait_ge(s_ex, 1)
                        dve.sem_inc(s_ex, -1)
                        link(TS(s1[:, :, 2], s1[:, :, 1], 1.0, None, ALU.add))
                        link(nc.vector.reciprocal(s1[:, :, 2], s1[:, :, 2]))
                        link(TT(s1[:, :, 3], s1[:, :, 2], s1[:, :, 1], ALU.mult))
                        for j in range(CT):
                            TS(wg[:, j, :], iota[:, :], i8f[:, j, 0:1], s1[:, j, 2:3], ALU.is_equal, ALU.mult)
                            ins = TS(ex[:, j, :], iota[:, :], i8f[:, j, 1:2], s1[:, j, 3:4], ALU.is_equal, ALU.mult)
                        link(ins)
                        TT(wg[:, :, :], wg[:, :, :], ex[:, :, :], ALU.add).then_inc(s_wg, 1)
                    dve.wait_ge(s_b, 1)
                    dve.sem_inc(s_b, -1)
                    for b in range(3):
                        v, r = banks(pso, b)
                        xk = S.x[:, bass.ds(c * CT + r.start, r.stop - r.start), :]
                        ins = TT(xk, xk, v, ALU.add)
                    link(ins)
                    dve.sem_inc(s_od, 1)
                    for e in range(NEXP):
                        dve.wait_ge(s_o, 1)
                        dve.sem_inc(s_o, -1)
                        for j in range(CT):
                            xk = S.x[:, bass.ds(c * CT + j, 1), :].rearrange("p a d -> p (a d)")
                            ins = STT(out=xk, in0=pso[:, j // 2, (j % 2) * D:(j % 2 + 1) * D], scalar=wg[:, j, e:e + 1],
                                      in1=xk, op0=ALU.mult, op1=ALU.add)
                        link(ins)
                        dve.sem_inc(s_od, 1)
                    if layer:
                        dve.sem_inc(s_x, 1)

            @block.scalar
            def _(act):
                if layer == 0:
                    act.wait_ge(s_bnv, 1)
                    act.sem_inc(s_bnv, -1)
                    nc.scalar.activation(bn[:, 4, :, :], bn[:, 4, :, :], ACT.Sqrt).then_inc(s_bns, 1)
                    act.wait_ge(s_aff, 1)
                    act.sem_inc(s_aff, -1)
                else:
                    act.wait_ge(s_w, 16 * len(smalls))
                with act.Fori(0, CHUNKS) as c:
                    root(nc, act, st, s_var, s_std)
                    act.wait_ge(s_t, 1)
                    act.sem_inc(s_t, -1)
                    turned(nc, pst, hT).then_inc(s_hT, 1)
                    act.wait_ge(s_lg, 1)
                    act.sem_inc(s_lg, -1)
                    if layer == 0:
                        nc.scalar.activation(ex[:, :, :], lg[:, :, :], ACT.Exp).then_inc(s_ex, 1)
                    else:
                        nc.scalar.activation(s1[:, :, 1], s1[:, :, 0], ACT.Exp).then_inc(s_ex, 1)
                    act.wait_ge(s_wt, 1)
                    act.sem_inc(s_wt, -1)
                    nc.scalar.copy(wT[:, 0:4 * P], pst[0:NEXP, 0, 0:4 * P])
                    nc.scalar.copy(wT[:, 4 * P:CN], pst[0:NEXP, 1, 0:P]).then_inc(s_wT, 1)

                    def evacuate(e, step, m):
                        act.wait_ge(s_m, 1)
                        act.sem_inc(s_m, -1)
                        for i in range(2):
                            lo, hi = SPLIT[i], SPLIT[i + 1]
                            v = psh[:, 2 * (m % 2) + i, 0:hi - lo]
                            k = e * 2 + m
                            if layer == 0:
                                ins = nc.scalar.activation(hid1[step][:, m, lo:hi], v, ACT.Relu, bias=bn[:, 2, step, k:k + 1],
                                                           scale=bn[:, 0, step, k:k + 1])
                            else:
                                ins = nc.scalar.activation(hid1[e % 2][:, m, lo:hi], v, ACT.Relu,
                                                           bias=b1[:, 4 * e + m:4 * e + m + 1])
                        ins.then_inc(s_ev, 1)

                    for e in range(NEXP):
                        for step in range(steps):
                            for m in range(hid):
                                evacuate(e, step, m)

            @block.tensor
            def _(pe):
                pe.wait_ge(s_w, 16 * len(smalls))
                for s, n in S.mw_in[layer]:
                    pe.wait_ge(s, n)

                def hidden(w, e, src, m):
                    for i in range(2):
                        lo, hi = SPLIT[i], SPLIT[i + 1]
                        for k in range(2):
                            ins = nc.tensor.matmul(psh[:, 2 * (m % 2) + i, 0:hi - lo], w[:, e, k, m * 128:(m + 1) * 128],
                                                   src[:, k, lo:hi], start=(k == 0), stop=(k == 1))
                    ins.then_inc(s_m, 1)

                def output(w, e, src):
                    pe.wait_ge(s_od, 1)
                    pe.sem_inc(s_od, -1)
                    for j in range(CT):
                        for k in range(hid):
                            ins = nc.tensor.matmul(pso[:, j // 2, (j % 2) * D:(j % 2 + 1) * D], src[:, k, j * P:(j + 1) * P],
                                                   w[:, e, k, :], start=(k == 0), stop=(k == hid - 1))
                    ins.then_inc(s_o, 1)

                with pe.Fori(0, CHUNKS) as c:
                    pe.wait_ge(s_h, 1)
                    pe.sem_inc(s_h, -1)
                    turn(nc, h, S.ident, pst).then_inc(s_t, 1)
                    pe.wait_ge(s_hT, 1)
                    pe.sem_inc(s_hT, -1)
                    for j in range(CT):
                        for k in range(2):
                            ins = nc.tensor.matmul(psg[:, j * NEXP:(j + 1) * NEXP], hT[:, k, j * P:(j + 1) * P], wr[:, k, :],
                                                   start=(k == 0), stop=(k == 1))
                    ins.then_inc(s_g, 1)
                    pe.wait_ge(s_wg, 1)
                    pe.sem_inc(s_wg, -1)
                    for j in range(CT):
                        ins = nc.tensor.transpose(pst[0:NEXP, j // 4, (j % 4) * P:(j % 4 + 1) * P], wg[:, j, :], S.ident[0:P, 0:P])
                    ins.then_inc(s_wt, 1)
                    pe.wait_ge(s_wT, 1)
                    pe.sem_inc(s_wT, -1)
                    for j in range(CT):
                        ins = nc.tensor.matmul(pso[:, j // 2, (j % 2) * D:(j % 2 + 1) * D], wT[:, j * P:(j + 1) * P], bo[:, :],
                                               start=True, stop=True)
                    ins.then_inc(s_b, 1)
                    W = S.mw[layer]
                    if layer == 0:
                        hidden(W[0], 0, hT, 0)
                        hidden(W[0], 0, hT, 1)
                        for e in range(NEXP):
                            pe.wait_ge(s_ev, 2)
                            pe.sem_inc(s_ev, -2)
                            hidden(W[1], e, hid1[0], 0)
                            hidden(W[1], e, hid1[0], 1)
                            if e + 1 < NEXP:
                                pe.wait_ge(s_ev, 1)
                                pe.sem_inc(s_ev, -1)
                                hidden(W[0], e + 1, hT, 0)
                                pe.wait_ge(s_ev, 1)
                                pe.sem_inc(s_ev, -1)
                                hidden(W[0], e + 1, hT, 1)
                            else:
                                pe.wait_ge(s_ev, 2)
                                pe.sem_inc(s_ev, -2)
                            output(W[2], e, hid1[1])
                    else:
                        for e in range(NEXP):
                            for m in range(hid):
                                if e or m > 1:
                                    pe.wait_ge(s_ev, 1)
                                    pe.sem_inc(s_ev, -1)
                                hidden(W[0], e, hT, m)
                            if e:
                                output(W[1], e - 1, hid1[(e - 1) % 2])
                        pe.wait_ge(s_ev, 2)
                        pe.sem_inc(s_ev, -2)
                        output(W[1], NEXP - 1, hid1[(NEXP - 1) % 2])
                    pe.wait_ge(s_od, 1)
                    pe.sem_inc(s_od, -1)



def second_nodes(nc, ctx, I, S):
    def sem(name):
        return S.signals.get("sn", name)

    with ExitStack() as loc:
        def tb(name, shape, dt=F32):
            return loc.enter_context(nc.sbuf_tensor("sn_" + name, shape, dt))
        row, st, hT = tb("row", [P, CT, T2]), tb("st", [P, CT, 9]), tb("hT", [128, 2, CN])
        pst = loc.enter_context(nc.psum_tensor("sn_pst", [128, 3, 512], F32))
        pso = loc.enter_context(nc.psum_tensor("sn_pso", [P, 3, 512], F32))
        s_link, s_var, s_std, s_h, s_t, s_hT, s_d, s_row, s_tab, s_rowfree = (sem(n) for n in (
            "dve_step", "variance", "deviation", "h_ready", "turned", "hT_ready", "vectors_in_psum", "row_ready", "table",
            "row_free"))
        with nc.Block() as block:
            @block.sync
            def _(sp):
                rows = S.table2.rearrange("(p t) d -> p t d", t=NT)
                with sp.Fori(0, CHUNKS) as c:
                    sp.wait_ge(s_row, 1)
                    sp.sem_inc(s_row, -1)
                    sp.dma_start(rows[:, bass.ds(c * CT, CT), :], row[:, :, :]).then_inc(s_tab, 16)
                    sp.wait_ge(s_tab, 16 * c + 16)
                    sp.sem_inc(s_rowfree, 1)

            @block.vector
            def _(dve):
                link = linker(dve, s_link)
                dve.sem_inc(s_rowfree, 1)
                with dve.Fori(0, CHUNKS) as c:
                    x = S.x[:, bass.ds(c * CT, CT), :]
                    dve.wait_ge(s_rowfree, 1)
                    dve.sem_inc(s_rowfree, -1)
                    link(normalise(nc, dve, link, x, row[:, :, 0:D], st, s_var, s_std))
                    dve.sem_inc(s_h, 1)
                    link(nc.vector.tensor_tensor(x, x, row[:, :, 0:D], ALU.add))

            @block.tensor
            def _(pe):
                with pe.Fori(0, CHUNKS) as c:
                    pe.wait_ge(s_h, 1)
                    pe.sem_inc(s_h, -1)
                    turn(nc, row, S.ident, pst).then_inc(s_t, 1)
                    pe.wait_ge(s_hT, 1)
                    pe.sem_inc(s_hT, -1)
                    for j in range(CT):
                        o = (j % 2) * 256
                        nc.tensor.matmul(pso[:, j // 2, o:o + C], hT[:, 0, j * P:(j + 1) * P], S.wd[:, 0, 0:C], start=True, stop=True)
                        ins = nc.tensor.matmul(pso[:, j // 2, o + C:o + 3 * C], hT[:, 1, j * P:(j + 1) * P], S.wd[:, 1, :],
                                               start=True, stop=True)
                    ins.then_inc(s_d, 1)

            @block.scalar
            def _(act):
                with act.Fori(0, CHUNKS) as c:
                    root(nc, act, st, s_var, s_std)
                    act.wait_ge(s_t, 1)
                    act.sem_inc(s_t, -1)
                    turned(nc, pst, hT).then_inc(s_hT, 1)
                    act.wait_ge(s_d, 1)
                    act.sem_inc(s_d, -1)
                    for b in range(3):
                        v, r = banks(pso, b)
                        ins = nc.scalar.copy(row[:, r, D:T2], v[:, :, 0:3 * C])
                    ins.then_inc(s_row, 1)



def second_edges(nc, ctx, I, S):
    with ExitStack() as loc:
        def tb(name, shape, dt=F32):
            return loc.enter_context(nc.sbuf_tensor(f"e2_{name}", shape, dt))

        def sem(n):
            return S.signals.get("e2", n)
        B = edge_buffers(nc, loc, S, "e2")
        got = [tb(f"got{s}", [P, GT, C + T2]) for s in range(2)]
        yx = tb("yx", [128, GE])
        lk = tb("leaky", [C, GE])
        cs = [tb(f"c{s}", [P, GT, D]) for s in range(2)]
        ex = tb("exp", [P, GT, C])
        mx, nm, Z, ez, az = (tb(n, [P, GT]) for n in ("max", "neg_max", "Z", "ez", "az"))
        shz = tb("shz", [P, GT, 3])
        t = tb("t", [P, GT, C])
        p_t = loc.enter_context(nc.psum_tensor("e2_pt", [128, 512], F32))
        p_h = loc.enter_context(nc.psum_tensor("e2_ph", [C, 512], F32))
        p_c = loc.enter_context(nc.psum_tensor("e2_pc", [P, 2, 512], F32))
        pss = loc.enter_context(nc.psum_tensor("e2_pss", [P, 2, 512], F32))
        (y_ready, yx_ps, yx_ready, h_ps, lk_ready, c_ps, c_ps_free, c_ready, c_free, nm_ready, e_ready, az_ready, dz_ready,
         s_link) = (sem(n) for n in (
             "y_ready", "yx_in_psum", "yx_ready", "hidden_in_psum", "leaky_ready", "main_in_psum", "main_psum_free",
             "main_ready", "main_free", "neg_max_ready", "exp_ready", "weights_ready", "vectors_weighted", "dve_step"))
        LAST = (G - 2) // 2

        with nc.Block() as block:
            @block.sync
            def _(sp):
                load_experts(nc, sp, S, 1)
                with sp.Fori(0, G // 2) as it:
                    for c in range(2):
                        load_row(sp, I, B, Edge(it, c))

            @block.gpsimd
            def _(pool):
                edge_pool(nc, pool, B, S.table2, lambda s, j: got[s][:, j, C:C + T2], S.acc[1])

            @block.tensor
            def _(pe):
                pe.sem_inc(B.msg_free, 2)

                def turn_in(e):
                    pe.wait_ge(y_ready, 1)
                    pe.sem_inc(y_ready, -1)
                    for j in range(GT):
                        ins = nc.tensor.transpose(p_t[:, j * P:(j + 1) * P], got[e.slot][:, j, 0:128], S.ident[0:P, 0:P])
                    ins.then_inc(yx_ps, 1)

                def main(e):
                    pe.wait_ge(yx_ready, 1)
                    pe.sem_inc(yx_ready, -1)
                    nc.tensor.matmul(p_h[:, 0:GE], S.wh[:, :], yx[:, :], start=True, stop=True).then_inc(h_ps, 1)
                    pe.wait_ge(c_ps_free, 1)
                    pe.sem_inc(c_ps_free, -1)
                    for j in range(GT):
                        o = (j % 2) * D
                        nc.tensor.matmul(p_c[:, j // 2, o:o + 3 * C], yx[:, j * P:(j + 1) * P], S.wm[:, :], start=True, stop=True)
                    pe.wait_ge(lk_ready, 1)
                    pe.sem_inc(lk_ready, -1)
                    for j in range(GT):
                        o = (j % 2) * D
                        ins = nc.tensor.matmul(p_c[:, j // 2, o + 3 * C:o + D], lk[:, j * P:(j + 1) * P], S.lsc[:, :],
                                               start=True, stop=True)
                    ins.then_inc(c_ps, 1)

                def body(it, c, sums=True):
                    turn_in(Edge(it, c + 1))
                    if sums:
                        sum_matmuls(nc, pe, B, Edge(it, c - 1), pss)
                    main(Edge(it, c + 1))
                turn_in(Edge(0, 0))
                main(Edge(0, 0))
                body(0, 0, False)
                with pe.Fori(0, LAST) as it:
                    body(it, 1)
                    body(it, 2)
                sum_matmuls(nc, pe, B, Edge(LAST, 0), pss)
                sum_matmuls(nc, pe, B, Edge(LAST, 1), pss)

            @block.scalar
            def _(act):
                act.sem_inc(B.sum_free, 2)
                act.sem_inc(B.sum_ps_free, 1)
                act.sem_inc(c_ps_free, 1)

                def yx_copy():
                    act.wait_ge(yx_ps, 1)
                    act.sem_inc(yx_ps, -1)
                    nc.scalar.copy(yx[:, :], p_t[:, 0:GE]).then_inc(yx_ready, 1)

                def c_copy(e):
                    act.wait_ge(c_ps, 1)
                    act.sem_inc(c_ps, -1)
                    act.wait_ge(c_free, 1)
                    act.sem_inc(c_free, -1)
                    for b in range(2):
                        ins = nc.scalar.copy(cs[e.slot][:, 2 * b:2 * b + 2, :], p_c[:, b, :].rearrange("p (n d) -> p n d", d=D))
                    tell(act, ins, B.own, c_ready, c_ps_free)

                def exps(e):
                    act.wait_ge(nm_ready, 1)
                    act.sem_inc(nm_ready, -1)
                    nc.scalar.activation(ez[:, :], nm[:, :], ACT.Exp)
                    for j in range(GT):
                        ins = nc.scalar.activation(ex[:, j, :], cs[e.slot][:, j, 3 * C:D], ACT.Exp, bias=nm[:, j:j + 1],
                                                   accum_out=Z[:, j:j + 1])
                    ins.then_inc(e_ready, 1)

                def vectors(e):
                    act.wait_ge(az_ready, 1)
                    act.sem_inc(az_ready, -1)
                    for j in range(GT):
                        ins = nc.scalar.activation(B.msg[e.slot][:, j, C:D], got[e.slot][:, j, C + D:C + T2], ACT.Copy,
                                                   scale=az[:, j:j + 1])
                    ins.then_inc(dz_ready, 1)

                def body(it, c, sums=True):
                    exps(Edge(it, c))
                    yx_copy()
                    vectors(Edge(it, c))
                    if sums:
                        sum_copy(nc, act, B, Edge(it, c - 1), pss)
                    c_copy(Edge(it, c + 1))
                yx_copy()
                c_copy(Edge(0, 0))
                body(0, 0, False)
                with act.Fori(0, LAST) as it:
                    body(it, 1)
                    body(it, 2)
                exps(Edge(LAST, 1))
                vectors(Edge(LAST, 1))
                sum_copy(nc, act, B, Edge(LAST, 0), pss)
                sum_copy(nc, act, B, Edge(LAST, 1), pss)

            @block.vector
            def _(dve):
                link = linker(dve, s_link)
                TT, TS, STT = nc.vector.tensor_tensor, nc.vector.tensor_scalar, nc.vector.scalar_tensor_tensor
                dve.sem_inc(B.row_free, 2)
                dve.sem_inc(B.got_free, 2)
                dve.sem_inc(B.put_free, 2)
                dve.sem_inc(c_free, 2)

                def col(a, e, j):
                    return a[:, bass.ds(e.g * GT + j, 1)]

                def sh(e, j, k):
                    return S.shn[:, bass.ds(e.g * GT + j, 1), k:k + 1].rearrange("p a b -> p (a b)")

                def index(e):
                    nc.vector.tensor_copy(B.take_i[e.slot][:, :], S.src[:, bass.ds(e.g * GT, GT)]).then_inc(B.idx_ready, 1)

                def prepare(e):
                    make_same(nc, dve, link, S, B, e)
                    dve.sem_inc(B.row_free, 1)
                    dve.wait_ge(B.put_free, 1)
                    dve.sem_inc(B.put_free, -1)
                    link(nc.vector.tensor_copy(B.put_i[e.slot][:, :], S.put[:, bass.ds(e.g * GT, GT)]))

                def contract(e):
                    x = got[e.slot]
                    dve.wait_ge(B.got[e.slot], 16 * GT * e.use)
                    dve.sem_inc(B.passed, 1)
                    for j in range(GT):
                        ins = TS(x[:, j, 0:C], x[:, j, 2 * C:3 * C], sh(e, j, 0), None, ALU.mult)
                    link(ins)
                    for k in (1, 2):
                        for j in range(GT):
                            ins = STT(out=x[:, j, 0:C], in0=x[:, j, (2 + k) * C:(3 + k) * C], scalar=sh(e, j, k), in1=x[:, j, 0:C],
                                      op0=ALU.mult, op1=ALU.add)
                        if k == 1:
                            link(ins)
                    ins.then_inc(y_ready, 1)

                def maximum(e):
                    dve.wait_ge(c_ready, 1)
                    dve.sem_inc(c_ready, -1)
                    link(nc.vector.tensor_reduce(mx[:, :], cs[e.slot][:, :, 3 * C:D], AX, ALU.max))
                    TS(nm[:, :], mx[:, :], -1.0, 0.0, ALU.mult, ALU.min).then_inc(nm_ready, 1)

                def leaky():
                    dve.wait_ge(h_ps, 1)
                    dve.sem_inc(h_ps, -1)
                    link(TS(lk[:, :], p_h[:, 0:GE], 0.01, None, ALU.mult))
                    TT(lk[:, :], lk[:, :], p_h[:, 0:GE], ALU.max).then_inc(lk_ready, 1)

                def messages(e):
                    v, m = cs[e.slot], B.msg[e.slot]
                    for j in range(GT):
                        ins = STT(out=t[:, j, :], in0=v[:, j, 2 * C:3 * C], scalar=col(S.q, e, j), in1=v[:, j, 0:C],
                                  op0=ALU.mult, op1=ALU.add)
                    dve.wait_ge(e_ready, 1)
                    dve.sem_inc(e_ready, -1)
                    link(STT(out=Z[:, :], in0=ez[:, :], scalar=float(3 * C), in1=Z[:, :], op0=ALU.mult, op1=ALU.add))
                    link(nc.vector.reciprocal(Z[:, :], Z[:, :]))
                    link(TT(az[:, :], ez[:, :], Z[:, :], ALU.mult))
                    dve.sem_inc(az_ready, 1)
                    TT(shz[:, :, :], S.shn[:, bass.ds(e.g * GT, GT), :], bc(az[:, :], 3, 2), ALU.mult)
                    for j in range(GT):
                        ins = STT(out=m[:, j, 0:C], in0=t[:, j, :], scalar=Z[:, j:j + 1], in1=ex[:, j, :], op0=ALU.mult, op1=ALU.mult)
                    link(ins)
                    dve.wait_ge(dz_ready, 1)
                    dve.sem_inc(dz_ready, -1)
                    dve.sem_inc(B.got_free, 1)
                    for j in range(GT):
                        for k in range(3):
                            o = m[:, j, (k + 1) * C:(k + 2) * C]
                            ins = STT(out=o, in0=v[:, j, C:2 * C], scalar=shz[:, j, k:k + 1], in1=o, op0=ALU.mult, op1=ALU.add)
                    link(ins)
                    dve.sem_inc(c_free, 1)
                    dve.sem_inc(B.msg_ready, 1)

                index(Edge(0, 0))
                index(Edge(0, 1))
                contract(Edge(0, 0))
                prepare(Edge(0, 0))
                leaky()

                def body(it, c, more=True):
                    maximum(Edge(it, c))
                    contract(Edge(it, c + 1))
                    messages(Edge(it, c))
                    if more:
                        index(Edge(it, c + 2))
                    leaky()
                    prepare(Edge(it, c + 1))
                with dve.Fori(0, LAST) as it:
                    body(it, 0)
                    body(it, 1)
                body(LAST, 0, False)
                maximum(Edge(LAST, 1))
                messages(Edge(LAST, 1))



def expert_weights(nc, ctx, S, layer, shapes, arrays):
    S.mw[layer] = [ctx.enter_context(nc.sbuf_tensor(f"mw{layer}_{i}", s, F32)) for i, s in enumerate(shapes)]
    S.mw_loads[layer] = [(t[:, :, :, :].rearrange("p e k h -> p (e k) h"), a.rearrange("e (k p) h -> p (e k) h", p=128))
                         for t, a in zip(S.mw[layer], arrays)]


def load_experts(nc, sp, S, layer):
    for to, fr in S.mw_loads[layer]:
        sp.dma_start(to, fr).then_inc(S.s_mw[layer], 16)


def program(nc, I, out):
    S = State()
    with ExitStack() as ctx:
        S.signals = Signals(nc, ctx)
        for layer in range(2):
            S.s_mw[layer] = ctx.enter_context(nc.semaphore(f"experts{layer}_in"))
        S.mw_in = {0: [(S.s_mw[0], 48)], 1: [(S.s_mw[1], 32)]}
        setup(nc, ctx, I, S)
        with ExitStack() as experts:
            expert_weights(nc, experts, S, 0, [[128, NEXP, 2, H1]] * 3, [I["eW1"], I["eW2"], I["eWo"]])
            with ExitStack() as skips:
                S.skip = skips.enter_context(nc.sbuf_tensor("skip", [P, NT, D], F32))
                first_nodes(nc, ctx, I, S)
                first_edges(nc, ctx, I, S)
                last_nodes(nc, ctx, I, S)
            mixture(nc, ctx, I, S, 0)
        with ExitStack() as experts:
            expert_weights(nc, experts, S, 1, [[128, NEXP, 2, H2], [128, NEXP, 4, D]], [I["fW1"], I["fW2"]])
            second_nodes(nc, ctx, I, S)
            second_edges(nc, ctx, I, S)
            mixture(nc, ctx, I, S, 1, out)


def planar(a, axis):
    a = np.moveaxis(np.asarray(a), axis, -1)
    v = a[..., C:].reshape(a.shape[:-1] + (C, 3))
    v = np.swapaxes(v, -1, -2).reshape(a.shape[:-1] + (3 * C,))
    return np.ascontiguousarray(np.moveaxis(np.concatenate([a[..., :C], v], axis=-1), -1, axis))


def kernel(**inputs):
    import concourse.bacc as bacc
    from concourse.bass_utils import run_bass_kernel_spmd as run

    a = {k: np.asarray(v) for k, v in inputs.items()}
    g0, g1, f0, f1 = "L0_gnn_", "L1_gnn_", "L0_ffn_", "L1_ffn_"

    def tiled(v):
        return np.swapaxes(v.reshape((ET, P) + v.shape[1:]), 0, 1)

    def columns(v):
        return v.reshape(-1, 128).T

    m4 = a[g0 + "M4"].reshape(HID, 4, C)
    arrays = {
        "x": planar(a["x"], 1),
        "src_pt": tiled(a["src"]), "dst_pt": tiled(a["dst"]), "dst_row": a["dst"].reshape(1, E),
        "ea3": tiled(a["edge_attr_3"]), "ea4": tiled(a["edge_attr_4"]), "rbfT": a["edge_attr_16"].T,
        "M1": a[g0 + "M1"], "M2": a[g0 + "M2"], "M3": a[g0 + "M3"],
        "M4": np.concatenate([m4[:, 0], m4[:, 2], m4[:, 1], m4[:, 3]], axis=1),
        "Wup0": a[g0 + "W_up0"], "Wup1": a[g0 + "W_up1"], "Wsc0": a[g0 + "Wsc0"], "Wsc1": a[g0 + "Wsc1"],
        "Wlin0": a[g0 + "W_lin0"], "Wlin1": a[g0 + "W_lin1"], "WB0": a[g0 + "WB0"], "WB1": a[g0 + "WB1"],
        "Wc0r": a[g0 + "Wc0"].T.reshape(1, 5 * C), "Wc1r": a[g0 + "Wc1"].T.reshape(1, 4 * C),
        "gam": np.concatenate([a[g0 + "gamma0"], a[g0 + "beta0"], a[g0 + "gamma1"]]).reshape(1, 3 * C),
        "lsc": a[g1 + "lin_scalar_w"],
        "Wr": planar(a[f0 + "Wr"], 0), "br": a[f0 + "br"].reshape(1, NEXP), "bo": planar(a[f0 + "bo"], 1),
        "bn": np.stack([np.stack([columns(a[f0 + n + s]) for s in "12"], 1) for n in ("g", "b", "be", "m", "v")], 1),
        "eW1": planar(a[f0 + "W1"], 1), "eW2": a[f0 + "W2"], "eWo": planar(a[f0 + "Wo"], 2),
        "Wg": planar(a[f1 + "Wg"], 0), "bg": a[f1 + "bg"].reshape(1, NEXP), "bias": a[f1 + "bias"].reshape(1, NEXP),
        "fW1": planar(a[f1 + "W1"], 1), "b1": columns(a[f1 + "b1"]), "fW2": planar(a[f1 + "W2"], 2),
        "b2": planar(a[f1 + "b2"], 1),
    }
    fac = {"ls0T": a[g1 + "lin_src_w0"].T, "ls1T": a[g1 + "lin_src_w1"].T,
           "w00": a[g1 + "tp1_w00"], "w11": a[g1 + "tp1_w11"], "w01": a[g1 + "tp1_w01"], "w10": a[g1 + "tp1_w10"],
           "lh0": a[g1 + "lin_hidden_w0"], "lh1": a[g1 + "lin_hidden_w1"],
           "t00": a[g1 + "tp2_w00"], "t11": a[g1 + "tp2_w11"], "t01": a[g1 + "tp2_w01"], "t10": a[g1 + "tp2_w10"]}
    nc = bacc.Bacc("TRN2", target_bir_lowering=False, num_devices=1)
    feed = {}

    def given(name, v):
        v = np.ascontiguousarray(v)
        feed["in_" + name] = v
        return nc.dram_tensor("in_" + name, v.shape, mybir.dt.from_np(v.dtype), kind="ExternalInput").ap()
    I = {name: given(name, v) for name, v in arrays.items()}
    I.update({"fac_" + name: given("fac_" + name, v) for name, v in fac.items()})
    out = nc.dram_tensor("out", (N, D), F32, kind="ExternalOutput").ap()
    program(nc, I, out)
    y = run(nc, [feed], core_ids=[0]).results[0]["out"]
    return np.concatenate([y[:, :C], np.swapaxes(y[:, C:].reshape(N, 3, C), 1, 2).reshape(N, 3 * C)], axis=1)
```

```python
from contextlib import ExitStack

import numpy as np

import concourse.bass as bass
from concourse import mybir

F32 = mybir.dt.float32
I32 = mybir.dt.int32
U32 = mybir.dt.uint32
ALU = mybir.AluOpType
ACT = mybir.ActivationFunctionType
AX = mybir.AxisListType.X

N, D, C, E = 3125, 256, 64, 50000
P = 125
NT = N // P
CT = 5
CHUNKS = NT // CT
CN = CT * P
ET = E // P
GT = 4
G = ET // GT
GE = GT * P
HE = GE // 2
R, HID = 16, 64
UNROLL = 4
PASSES = (G - 4) // UNROLL
ACC_ROWS = 26 * 128
T2 = 448
NEXP = 8
H1 = 256
H2 = 512
SPLIT = (0, 375, 625)
LN_EPS, BN_EPS = 1e-5, 1e-3
SQ3 = float(np.sqrt(3.0))
INV_TP = float(1.0 / np.sqrt(2 * C))
INV_MUL = float(1.0 / np.sqrt(C))


class State:
    def __init__(self):
        self.mw, self.mw_loads, self.mw_in, self.s_mw = {}, {}, {}, {}


class Buffers:
    pass


def bc(ap, n, axis):
    v = ap.unsqueeze(axis)
    shape = list(v.shape)
    shape[axis] = n
    return v.broadcast_to(shape)


def linker(eng, sem):
    def link(ins):
        ins.then_inc(sem, 1)
        eng.wait_ge(sem, 1)
        eng.sem_inc(sem, -1)
    return link


def tell(eng, ins, own, *sems):
    ins.then_inc(own, 1)
    eng.wait_ge(own, 1)
    eng.sem_inc(own, -1)
    for s in sems:
        eng.sem_inc(s, 1)


class Signals:
    SHARED = {"dve_step", "act_step", "variance", "deviation", "h_ready", "turned", "hT_ready", "h_free",
              "gates_in_psum", "logits_ready", "exps_ready", "gates_ready", "gates_turned", "gates_T_ready",
              "bias_in_psum", "hidden_in_psum", "hidden_ready", "out_in_psum", "out_added"}

    def __init__(self, nc, ctx):
        self.nc, self.ctx, self.shared = nc, ctx, {}

    def get(self, phase, name):
        if name not in self.SHARED:
            return self.ctx.enter_context(self.nc.semaphore(f"{phase}_{name}"))
        if name not in self.shared:
            self.shared[name] = self.ctx.enter_context(self.nc.semaphore(name))
        return self.shared[name]



def setup(nc, ctx, I, S):
    def sb(name, shape, dt=F32):
        return ctx.enter_context(nc.sbuf_tensor(name, shape, dt))

    def sem(name):
        return S.signals.get("su", name)

    S.x = sb("x_nodes", [P, NT, D])
    S.ident = sb("ident", [128, 128])
    S.ones = sb("ones", [P, 128])
    S.src = sb("src_idx", [P, ET], I32)
    S.dst = sb("dst_idx", [P, ET], I32)
    S.dstf = sb("dst_float", [P, ET])
    S.put = sb("scatter_idx", [P, ET], I32)
    S.sh0 = sb("edge_sh", [P, ET, 4])
    S.shn = sb("edge_unit", [P, ET, 3])
    S.q = sb("edge_q", [P, ET])
    S.wh = sb("w_hidden", [128, C])
    S.wm = sb("w_main", [128, D])
    S.lsc = sb("w_scalar", [C, C])
    S.wd = sb("w_vector", [128, 2, 128])
    S.before = sb("earlier_mask", [P, P])
    S.dump = sb("dump_row", [P, 1])

    S.table1 = nc.dram_tensor("table1", (N, D), F32, kind="Internal").ap()
    S.table2 = nc.dram_tensor("table2", (N, T2), F32, kind="Internal").ap()
    S.acc = [[nc.dram_tensor(f"acc{l}_{i}", (ACC_ROWS, D), F32, kind="Internal").ap() for i in range(GT)]
             for l in range(2)]

    with ExitStack() as loc:
        def tb(name, shape, dt=F32):
            return loc.enter_context(nc.sbuf_tensor(name, shape, dt))

        zero = tb("zero", [128, 26, D])
        ev = tb("edge_vec", [P, ET, 3])
        sq = tb("edge_sq", [P, ET, 3])
        nrm = tb("edge_norm", [P, ET])
        dumpi = tb("dump_int", [P, 1], I32)
        fac = tb("factors", [C, 20, C])
        UT = tb("prod_T", [C, 4, C])
        WT = tb("full_T", [C, 4, C])
        WR = tb("scaled_T", [C, 6, C])
        WDD = tb("wd_twice", [C, 2, C])
        pz = [loc.enter_context(nc.psum_tensor(f"pz{i}", [128, 512], F32)) for i in range(8)]
        s_load, s_zeroed, s_zero, s_out = sem("su_loaded"), sem("su_acc_zeroed"), sem("su_zero_ready"), sem("su_x")
        s_iota, s_link, s_ulink, s_pe, s_cp = sem("su_iota"), sem("su_dve_step"), sem("su_pool_step"), sem("su_product"), sem("su_copied")
        NAMES = ["ls0T", "ls1T", "w00", "w11", "w01", "w10", "lh0", "lh1", "t00", "t11", "t01", "t10"]
        loads = [(S.src[:, :], I["src_pt"]), (S.dst[:, :], I["dst_pt"]), (ev[:, :, :], I["ea3"]), (S.sh0[:, :, :], I["ea4"]),
                 (S.lsc[:, :], I["lsc"])]
        loads += [(fac[:, i, :], I["fac_" + n]) for i, n in enumerate(NAMES)]
        F = {n: fac[:, i, :] for i, n in enumerate(NAMES)}
        s_nrm, s_root = sem("su_norm_sq"), sem("su_norm")
        with nc.Block() as block:
            @block.scalar
            def _(act):
                act.wait_ge(s_nrm, 1)
                act.sem_inc(s_nrm, -1)
                nc.scalar.activation(nrm[:, :], nrm[:, :], ACT.Sqrt).then_inc(s_root, 1)

            @block.sync
            def _(sp):
                for to, fr in loads:
                    sp.dma_start(to, fr).then_inc(s_load, 16)
                sp.dma_start(S.x[:, :, :], I["x"].rearrange("(p t) d -> p t d", t=NT)).then_inc(s_out, 16)
                sp.wait_ge(s_zero, 1)
                for l in range(2):
                    for i in range(GT):
                        sp.dma_start(S.acc[l][i].rearrange("(p t) d -> p t d", t=26), zero[:, :, :]).then_inc(s_zeroed, 16)
                sp.wait_ge(s_zeroed, 16 * 2 * GT)
                sp.wait_ge(s_out, 16)

            @block.gpsimd
            def _(pool):
                link = linker(pool, s_ulink)
                link(nc.gpsimd.memset(S.ident[:, :], 0.0))
                link(nc.gpsimd.affine_select(out=S.ident[:, :], in_=S.ident[:, :], compare_op=ALU.not_equal, fill=1.0,
                                             base=0, pattern=[[-1, 128]], channel_multiplier=1))
                link(nc.gpsimd.memset(S.before[:, :], 1.0))
                link(nc.gpsimd.affine_select(out=S.before[:, :], in_=S.before[:, :], compare_op=ALU.is_gt, fill=0.0,
                                             base=0, pattern=[[-1, P]], channel_multiplier=1))
                nc.gpsimd.iota(dumpi[:, :], pattern=[[0, 1]], base=N, channel_multiplier=1).then_inc(s_iota, 1)

            @block.vector
            def _(dve):
                link = linker(dve, s_link)
                nc.vector.memset(zero[:, :, :], 0.0).then_inc(s_zero, 1)
                nc.vector.memset(S.ones[:, :], 1.0)
                nc.vector.memset(S.wm[0:C, 2 * C:3 * C], 0.0)
                nc.vector.memset(S.wd[:, :, :], 0.0)
                link(nc.vector.memset(WR[:, :, :], 0.0))
                dve.wait_ge(s_iota, 1)
                nc.vector.tensor_copy(S.dump[:, :], dumpi[:, :])
                dve.wait_ge(s_load, 16 * len(loads))
                nc.vector.tensor_copy(S.dstf[:, :], S.dst[:, :])
                link(nc.vector.tensor_tensor(sq[:, :, :], ev[:, :, :], ev[:, :, :], ALU.mult))
                link(nc.vector.tensor_reduce(nrm[:, :], sq[:, :, :], AX, ALU.add))
                dve.sem_inc(s_nrm, 1)
                dve.wait_ge(s_root, 1)
                dve.sem_inc(s_root, -1)
                link(nc.vector.tensor_scalar(nrm[:, :], nrm[:, :], 1e-12, None, ALU.add))
                link(nc.vector.reciprocal(nrm[:, :], nrm[:, :]))
                link(nc.vector.tensor_scalar(nrm[:, :], nrm[:, :], SQ3, None, ALU.mult))
                link(nc.vector.tensor_tensor(S.shn[:, :, :], ev[:, :, :], bc(nrm[:, :], 3, 2), ALU.mult))
                link(nc.vector.tensor_tensor(sq[:, :, :], S.shn[:, :, :], S.shn[:, :, :], ALU.mult))
                link(nc.vector.tensor_reduce(S.q[:, :], sq[:, :, :], AX, ALU.add))
                k = INV_MUL * INV_TP * INV_MUL
                dve.wait_ge(s_pe, 1)
                for i, f in enumerate((k / SQ3, k, k, k)):
                    ins = nc.vector.tensor_scalar(UT[:, i, :], pz[0][0:C, i * C:(i + 1) * C], f, None, ALU.mult)
                ins.then_inc(s_cp, 1)
                dve.wait_ge(s_pe, 2)
                nc.vector.tensor_copy(S.wh[:, :], pz[1][:, 0:C])
                link(nc.vector.tensor_copy(WT[:, :, :].rearrange("p a b -> p (a b)"), pz[2][0:C, 0:4 * C]))
                nc.vector.tensor_scalar(WR[:, 0, :], WT[:, 2, :], 1.0 / SQ3, None, ALU.mult)
                nc.vector.tensor_copy(WR[:, 3, :], WT[:, 3, :])
                nc.vector.tensor_scalar(WR[:, 5, :], WT[:, 3, :], 1.0 / SQ3, None, ALU.mult)
                nc.vector.tensor_copy(WDD[:, 0, :], WT[:, 2, :])
                nc.vector.tensor_copy(WDD[:, 1, :], WT[:, 2, :]).then_inc(s_cp, 1)
                dve.wait_ge(s_pe, 3)
                nc.vector.tensor_scalar(S.wm[:, 0:3 * C], pz[3][:, 0:3 * C], INV_TP, None, ALU.mult)
                nc.vector.tensor_scalar(S.wm[:, 3 * C:D], pz[5][:, 0:C], 0.01 * INV_MUL, None, ALU.mult)
                for h in range(2):
                    rows = slice(C * h, C * (h + 1))
                    nc.vector.tensor_scalar(S.wd[rows, 1, rows], pz[4][rows, 0:C], INV_TP, None, ALU.mult)
                nc.vector.tensor_scalar(S.wd[C:128, 0, 0:C], pz[4][C:128, 0:C], INV_TP, None, ALU.mult)
                nc.vector.tensor_scalar(S.lsc[:, :], S.lsc[:, :], 0.99 * INV_MUL, None, ALU.mult).then_inc(s_cp, 1)
                dve.wait_ge(s_cp, 3)

            @block.tensor
            def _(pe):
                pe.wait_ge(s_load, 16 * len(loads))
                for i, (a, b) in enumerate((("w11", "ls1T"), ("w00", "ls0T"), ("w10", "ls1T"), ("w01", "ls0T"))):
                    ins = nc.tensor.matmul(pz[0][0:C, i * C:(i + 1) * C], F[a], F[b], start=True, stop=True)
                ins.then_inc(s_pe, 1)
                pe.wait_ge(s_cp, 1)
                nc.tensor.matmul(pz[1][:, 0:C], UT[:, 0:2, :].rearrange("p a b -> p (a b)"), F["lh0"], start=True, stop=True)
                nc.tensor.matmul(pz[2][0:C, 0:2 * C], F["lh0"], UT[:, 0:2, :].rearrange("p a b -> p (a b)"),
                                 start=True, stop=True)
                nc.tensor.matmul(pz[2][0:C, 2 * C:4 * C], F["lh1"], UT[:, 2:4, :].rearrange("p a b -> p (a b)"),
                                 start=True, stop=True).then_inc(s_pe, 1)
                pe.wait_ge(s_cp, 2)
                hT = WT[:, 0:2, :].rearrange("p a b -> p (a b)")

                def pair(i):
                    return WR[:, i:i + 2, :].rearrange("p a b -> p (a b)")
                nc.tensor.matmul(pz[3][:, 0:C], hT, F["t00"], start=True, stop=False)
                nc.tensor.matmul(pz[3][:, 0:C], pair(0), F["t11"], start=False, stop=True)
                nc.tensor.matmul(pz[3][:, C:2 * C], hT, F["t01"], start=True, stop=False)
                nc.tensor.matmul(pz[3][:, C:2 * C], pair(2), F["t10"], start=False, stop=True)
                nc.tensor.matmul(pz[3][:, 2 * C:3 * C], pair(4), F["t11"], start=True, stop=True)
                nc.tensor.matmul(pz[5][:, 0:C], hT, S.lsc[:, :], start=True, stop=True)
                nc.tensor.matmul(pz[4][:, 0:C], WDD[:, :, :].rearrange("p a b -> p (a b)"), F["t10"],
                                 start=True, stop=True).then_inc(s_pe, 1)



def statistics(nc, link, x, st):
    for j in range(CT):
        ins = nc.vector.bn_stats(st[:, j, 0:6], x[:, j, :])
    link(ins)
    for j in range(CT):
        ins = nc.vector.bn_aggr(st[:, j, 6:8], st[:, j, 0:6])
    link(ins)
    return nc.vector.tensor_scalar(st[:, :, 8:9], st[:, :, 7:8], LN_EPS, None, ALU.add)


def normed(nc, link, x, h, st):
    link(nc.vector.reciprocal(st[:, :, 8:9], st[:, :, 8:9]))
    for j in range(CT):
        ins = nc.vector.tensor_scalar(h[:, j, :], x[:, j, :], st[:, j, 6:7], st[:, j, 8:9], ALU.subtract, ALU.mult)
    return ins


def normalise(nc, dve, link, x, h, st, s_var, s_std):
    statistics(nc, link, x, st).then_inc(s_var, 1)
    dve.wait_ge(s_std, 1)
    dve.sem_inc(s_std, -1)
    return normed(nc, link, x, h, st)


def root(nc, act, st, s_var, s_std):
    act.wait_ge(s_var, 1)
    act.sem_inc(s_var, -1)
    nc.scalar.activation(st[:, :, 8:9], st[:, :, 8:9], ACT.Sqrt).then_inc(s_std, 1)


def turn(nc, h, ident, pst):
    for i in range(2 * CT):
        j, k = i // 2, i % 2
        ins = nc.tensor.transpose(pst[:, i // 4, (i % 4) * P:(i % 4 + 1) * P], h[:, j, k * 128:(k + 1) * 128],
                                  ident[0:P, 0:P])
    return ins


def turned(nc, pst, hT):
    for i in range(3):
        n = min(4, 2 * CT - 4 * i) // 2
        o = hT[:, :, 2 * i * P:(2 * i + n) * P].rearrange("p k (j e) -> p j k e", j=n)
        ins = nc.scalar.copy(o, pst[:, i, 0:2 * n * P].rearrange("p (j k e) -> p j k e", j=n, k=2))
    return ins


def linear(nc, hT, w0, w1, pso):
    for j in range(CT):
        for k, w in enumerate((w0, w1)):
            o = (j % 2) * 256 + k * 128
            ins = nc.tensor.matmul(pso[:, j // 2, o:o + 128], hT[:, k, j * P:(j + 1) * P], w, start=True, stop=True)
    return ins


def banks(pso, b):
    n = min(2, CT - 2 * b)
    return pso[:, b, 0:256 * n].rearrange("p (n d) -> p n d", d=256), slice(2 * b, 2 * b + n)



def first_nodes(nc, ctx, I, S):
    def sem(name):
        return S.signals.get("fn", name)

    with ExitStack() as loc:
        def tb(name, shape, dt=F32):
            return loc.enter_context(nc.sbuf_tensor(name, shape, dt))
        h, st, hT = tb("fn_h", [P, CT, D]), tb("fn_st", [P, CT, 9]), tb("fn_hT", [128, 2, CN])
        up = tb("fn_up", [P, CT, D])
        bd = tb("fn_bd", [128, 4, 128])
        pst = loc.enter_context(nc.psum_tensor("fn_pst", [128, 3, 512], F32))
        pso = loc.enter_context(nc.psum_tensor("fn_pso", [P, 3, 512], F32))
        s_bz, s_w, s_link, s_h, s_t, s_hT = sem("bd_zero"), sem("weights"), sem("dve_step"), sem("h_ready"), sem("turned"), sem("hT_ready")
        s_hfree, s_own = sem("h_free"), sem("act_step")
        s_var, s_std = sem("variance"), sem("deviation")
        s_up, s_upc, s_sc, s_scc, s_upd, s_upg = sem("up"), sem("up_copied"), sem("skip"), sem("skip_copied"), sem("table"), sem("table_ok")
        with nc.Block() as block:
            @block.sync
            def _(sp):
                sp.wait_ge(s_bz, 1)
                sp.sem_inc(s_bz, -1)
                for i, (a, b) in enumerate(((I["Wup0"], I["Wup1"]), (I["Wup1"], I["Wup1"]), (I["Wsc0"], I["Wsc1"]), (I["Wsc1"], I["Wsc1"]))):
                    sp.dma_start(bd[0:C, i, 0:C], a).then_inc(s_w, 16)
                    sp.dma_start(bd[C:128, i, C:128], b).then_inc(s_w, 16)
                rows = S.table1.rearrange("(p t) d -> p t d", t=NT)
                with sp.Fori(0, CHUNKS) as c:
                    sp.wait_ge(s_upc, 1)
                    sp.sem_inc(s_upc, -1)
                    sp.dma_start(rows[:, bass.ds(c * CT, CT), :], up[:, :, :]).then_inc(s_upd, 16)
                    sp.wait_ge(s_upd, 16 * c + 16)
                    sp.sem_inc(s_upg, 1)

            @block.vector
            def _(dve):
                link = linker(dve, s_link)
                nc.vector.memset(bd[:, :, :], 0.0).then_inc(s_bz, 1)
                with dve.Fori(0, CHUNKS) as c:
                    normalise(nc, dve, link, S.x[:, bass.ds(c * CT, CT), :], h, st, s_var, s_std).then_inc(s_h, 1)
                    dve.wait_ge(s_hfree, 1)
                    dve.sem_inc(s_hfree, -1)

            @block.tensor
            def _(pe):
                pe.wait_ge(s_w, 16 * 8)
                with pe.Fori(0, CHUNKS) as c:
                    pe.wait_ge(s_h, 1)
                    pe.sem_inc(s_h, -1)
                    turn(nc, h, S.ident, pst).then_inc(s_t, 1)
                    pe.wait_ge(s_hT, 1)
                    pe.sem_inc(s_hT, -1)
                    linear(nc, hT, bd[:, 0, :], bd[:, 1, :], pso).then_inc(s_up, 1)
                    pe.wait_ge(s_scc, 1)
                    pe.sem_inc(s_scc, -1)
                    linear(nc, hT, bd[:, 2, :], bd[:, 3, :], pso).then_inc(s_sc, 1)
                    pe.wait_ge(s_scc, 1)
                    pe.sem_inc(s_scc, -1)

            @block.scalar
            def _(act):
                act.sem_inc(s_upg, 1)
                with act.Fori(0, CHUNKS) as c:
                    root(nc, act, st, s_var, s_std)
                    act.wait_ge(s_t, 1)
                    act.sem_inc(s_t, -1)
                    act.sem_inc(s_hfree, 1)
                    turned(nc, pst, hT).then_inc(s_hT, 1)
                    act.wait_ge(s_up, 1)
                    act.sem_inc(s_up, -1)
                    act.wait_ge(s_upg, 1)
                    act.sem_inc(s_upg, -1)
                    for b in range(3):
                        v, r = banks(pso, b)
                        ins = nc.scalar.copy(up[:, r, :], v)
                    tell(act, ins, s_own, s_scc, s_upc)
                    act.wait_ge(s_sc, 1)
                    act.sem_inc(s_sc, -1)
                    for b in range(3):
                        v, r = banks(pso, b)
                        ins = nc.scalar.copy(S.skip[:, bass.ds(c * CT + r.start, r.stop - r.start), :], v)
                    ins.then_inc(s_scc, 1)



class Edge:
    def __init__(self, it, c):
        self.g = it * UNROLL + c
        self.slot = c % 2
        self.use = it * (UNROLL // 2) + (c // 2 + 1)
        self.deep = c % UNROLL
        self.deep_use = it + (c // UNROLL + 1)


def edge_buffers(nc, loc, S, name):
    def tb(n, shape, dt=F32):
        return loc.enter_context(nc.sbuf_tensor(f"{name}_{n}", shape, dt))

    def sem(n):
        return S.signals.get(name, n)
    B = Buffers()
    B.take_i = [tb(f"gather_idx{s}", [P, GT], I32) for s in range(UNROLL)]
    B.put_i = [tb(f"scatter_idx{s}", [P, GT], I32) for s in range(2)]
    B.row = [tb(f"dst_row{s}", [128, GE], I32) for s in range(2)]
    B.same = [tb(f"same{s}", [P, GT, P]) for s in range(2)]
    B.msg = [tb(f"msg{s}", [P, GT, D]) for s in range(2)]
    B.sum = [tb(f"sum{s}", [P, GT, D]) for s in range(2)]
    B.got = [sem(f"gathered{s}") for s in range(UNROLL)]
    B.put = [sem(f"scattered{s}") for s in range(2)]
    B.row_in = [sem(f"dst_row_in{s}") for s in range(2)]
    B.row_free = sem("dst_row_free")
    B.idx_ready = sem("gather_index_ready")
    B.got_free = sem("gathered_free")
    B.msg_ready = sem("messages_ready")
    B.msg_free = sem("messages_used")
    B.sum_ps = sem("sums_in_psum")
    B.sum_ps_free = sem("sums_psum_free")
    B.sum_ready = sem("sums_ready")
    B.sum_free = sem("sums_scattered")
    B.put_free = sem("scatter_index_free")
    B.put_ready = sem("scatter_index_ready")
    B.own = sem("act_step")
    B.passed = sem("dma_waits_passed")
    return B


def edge_pool(nc, pool, B, table, got, acc):
    def gather(e):
        pool.wait_ge(B.idx_ready, 1)
        pool.sem_inc(B.idx_ready, -1)
        pool.wait_ge(B.got_free, 1)
        pool.sem_inc(B.got_free, -1)
        for j in range(GT):
            pool.indirect_dma_start(got(e.deep, j), None, table,
                                    bass.IndirectOffsetOnAxis(B.take_i[e.deep][:, j:j + 1], 0)).then_inc(B.got[e.deep], 16)

    def scatter(e, before):
        if before is not None:
            pool.wait_ge(B.put[before.slot], 16 * GT * before.use)
            pool.sem_inc(B.sum_free, 1)
            pool.sem_inc(B.put_free, 1)
        pool.wait_ge(B.put_ready, 1)
        pool.sem_inc(B.put_ready, -1)
        pool.wait_ge(B.sum_ready, 1)
        pool.sem_inc(B.sum_ready, -1)
        for j in range(GT):
            pool.indirect_dma_start(acc[j], bass.IndirectOffsetOnAxis(B.put_i[e.slot][:, j:j + 1], 0),
                                    B.sum[e.slot][:, j, :], None, compute_op=ALU.add).then_inc(B.put[e.slot], 16)
    for c in range(UNROLL):
        gather(Edge(0, c))

    def body(it, c):
        gather(Edge(it, c + 3))
        scatter(Edge(it, c - 1), Edge(it, c - 2) if c > 1 else None)
    for c in range(1, UNROLL + 1):
        body(0, c)
    with pool.Fori(0, PASSES - 1) as it:
        for c in range(1, UNROLL + 1):
            body(it, UNROLL + c)
    for c in range(G - 4, G):
        scatter(Edge(0, c), Edge(0, c - 1))
    for s in range(2):
        pool.wait_ge(B.put[s], 16 * GT * (G // 2))


def load_row(sp, I, B, e):
    sp.wait_ge(B.row_free, 1)
    sp.sem_inc(B.row_free, -1)
    sp.dma_start(B.row[e.slot][:, :], I["dst_row"][:, bass.ds(e.g * GE, GE)].broadcast_to([128, GE])).then_inc(
        B.row_in[e.slot], 16)


def make_same(nc, dve, S, B, e):
    dve.wait_ge(B.msg_free, 1)
    dve.sem_inc(B.msg_free, -1)
    dve.wait_ge(B.row_in[e.slot], 16 * e.use)
    dve.sem_inc(B.passed, 1)
    return nc.vector.tensor_tensor(B.same[e.slot][:, :, :],
                                   B.row[e.slot][0:P, :].rearrange("p (t f) -> p t f", t=GT),
                                   bc(S.dstf[:, bass.ds(e.g * GT, GT)], P, 2), ALU.is_equal)


def target(nc, dve, S, B, e):
    dve.wait_ge(B.put_free, 1)
    dve.sem_inc(B.put_free, -1)
    nc.vector.tensor_copy(B.put_i[e.slot][:, :], S.put[:, bass.ds(e.g * GT, GT)]).then_inc(B.put_ready, 1)


def sum_matmuls(nc, pe, B, e, pss):
    pe.wait_ge(B.msg_ready, 1)
    pe.sem_inc(B.msg_ready, -1)
    pe.wait_ge(B.sum_ps_free, 1)
    pe.sem_inc(B.sum_ps_free, -1)
    for j in range(GT):
        ins = nc.tensor.matmul(pss[:, j // 2, (j % 2) * D:(j % 2 + 1) * D], B.same[e.slot][:, j, :],
                               B.msg[e.slot][:, j, :], start=True, stop=True)
    ins.then_inc(B.sum_ps, 1)


def sums_done(act, B):
    act.wait_ge(B.sum_ps, 1)
    act.sem_inc(B.sum_ps, -1)
    act.sem_inc(B.msg_free, 1)


def sum_copy(nc, act, B, e, pss):
    act.wait_ge(B.sum_free, 1)
    act.sem_inc(B.sum_free, -1)
    for b in range(2):
        ins = nc.scalar.copy(B.sum[e.slot][:, 2 * b:2 * b + 2, :],
                             pss[:, b, :].rearrange("p (n d) -> p n d", d=D))
    tell(act, ins, B.own, B.sum_ready, B.sum_ps_free)


def first_edges(nc, ctx, I, S):
    with ExitStack() as loc:
        def tb(name, shape, dt=F32):
            return loc.enter_context(nc.sbuf_tensor(f"e1_{name}", shape, dt))

        def sem(n):
            return S.signals.get("e1", n)
        B = edge_buffers(nc, loc, S, "e1")
        got = [tb(f"got{s}", [P, GT, D]) for s in range(UNROLL)]
        rbf = [tb(f"rbf{s}", [2 * R, HE]) for s in range(2)]
        r = [tb(f"r{i}", [2 * HID, HE]) for i in range(3)]
        w = [tb(f"tpw{s}", [P, GT, D]) for s in range(2)]
        prod = tb("prod", [P, GT, 3, C])
        ash = tb("ash", [P, GT, 3, C])
        q = tb("q", [P, GT, C])
        q3 = tb("q3", [P, GT, C])
        a = tb("a", [P, GT, C])
        count = tb("count", [P, GT])
        repeat = tb("repeat", [P, GT, P])
        junk = tb("junk", [P, GT, P])
        putf = tb("putf", [P, GT])
        sh3 = tb("sh3", [P, ET, 3])
        M1, M2, M3 = tb("M1", [2 * R, 2, HID]), tb("M2", [2 * HID, 2, HID]), tb("M3", [2 * HID, 2, HID])
        M4 = tb("M4", [2 * HID, D])
        ps_m = [loc.enter_context(nc.psum_tensor(f"e1_psm{i}", [2 * HID, 512], F32)) for i in range(2)]
        ps_w = loc.enter_context(nc.psum_tensor("e1_psw", [P, 2, 512], F32))
        pss = loc.enter_context(nc.psum_tensor("e1_pss", [P, 2, 512], F32))
        s_w, rbf_in = sem("weights"), [sem(f"rbf_in{s}") for s in range(2)]
        rbf_free, s_m, s_r, s_wp, wp_free, w_ready, w_free = (sem(n) for n in (
            "rbf_free", "hidden_in_psum", "hidden_ready", "tpw_in_psum", "tpw_psum_free", "tpw_ready", "tpw_free"))
        s_link, s_zeroed = sem("dve_step"), sem("blocks_zeroed")
        repeat_ready, count_ready = sem("repeats_ready"), sem("counts_ready")

        def rbf_load(sp, e):
            sp.wait_ge(rbf_free, 1)
            sp.sem_inc(rbf_free, -1)
            sp.dma_start(rbf[e.slot][:, :], I["rbfT"][:, bass.ds(e.g * HE, HE)]).then_inc(rbf_in[e.slot], 16)

        with nc.Block() as block:
            @block.sync
            def _(sp):
                sp.wait_ge(s_zeroed, 1)
                for h in range(2):
                    for to, n in ((M1, "M1"), (M2, "M2"), (M3, "M3")):
                        k = to.shape[0] // 2
                        sp.dma_start(to[h * k:(h + 1) * k, h, :], I[n]).then_inc(s_w, 16)
                    sp.dma_start(M4[h * HID:(h + 1) * HID, :], I["M4"]).then_inc(s_w, 16)
                load_experts(nc, sp, S, 0)
                with sp.Fori(0, G // UNROLL) as it:
                    for c in range(UNROLL):
                        rbf_load(sp, Edge(it, c))
                        load_row(sp, I, B, Edge(it, c))

            @block.gpsimd
            def _(pool):
                edge_pool(nc, pool, B, S.table1, lambda s, j: got[s][:, j, :], S.acc[0])

            @block.tensor
            def _(pe):
                pe.sem_inc(rbf_free, 2)
                pe.sem_inc(B.msg_free, 2)
                pe.wait_ge(s_w, 16 * 8)

                def mlp1(e):
                    pe.wait_ge(rbf_in[e.slot], 16 * e.use)
                    pe.sem_inc(B.passed, 1)
                    nc.tensor.matmul(ps_m[0][:, 0:HE], M1[:, :, :].rearrange("p a b -> p (a b)"), rbf[e.slot][:, :], start=True, stop=True).then_inc(s_m, 1)

                def mlp(w, i):
                    pe.wait_ge(s_r, 1)
                    pe.sem_inc(s_r, -1)
                    nc.tensor.matmul(ps_m[1][:, 0:HE], w[:, :, :].rearrange("p a b -> p (a b)"), r[i][:, :], start=True, stop=True).then_inc(s_m, 1)

                def tpw(e):
                    pe.wait_ge(s_r, 1)
                    pe.sem_inc(s_r, -1)
                    pe.wait_ge(wp_free, 1)
                    pe.sem_inc(wp_free, -1)
                    for j in range(GT):
                        half = slice(j // 2 * HID, (j // 2 + 1) * HID)
                        ins = nc.tensor.matmul(ps_w[:, j // 2, (j % 2) * D:(j % 2 + 1) * D],
                                               r[2][half, (j % 2) * P:(j % 2 + 1) * P], M4[half, :], start=True, stop=True)
                    ins.then_inc(s_wp, 1)

                def body(it, c, sums=True):
                    mlp1(Edge(it, c + 1))
                    tpw(Edge(it, c))
                    mlp(M2, 0)
                    if sums:
                        sum_matmuls(nc, pe, B, Edge(it, c - 1), pss)
                    mlp(M3, 1)
                mlp1(Edge(0, 0))
                mlp(M2, 0)
                mlp(M3, 1)
                body(0, 0, False)
                with pe.Fori(0, PASSES) as it:
                    for c in range(1, UNROLL + 1):
                        body(it, c)
                body(0, G - 3)
                body(0, G - 2)
                last = Edge(0, G - 1)
                tpw(last)
                sum_matmuls(nc, pe, B, Edge(0, G - 2), pss)
                sum_matmuls(nc, pe, B, last, pss)

            @block.scalar
            def _(act):
                act.sem_inc(B.sum_free, 2)
                act.sem_inc(wp_free, 1)
                act.sem_inc(B.sum_ps_free, 1)

                def silu(i):
                    act.wait_ge(s_m, 1)
                    act.sem_inc(s_m, -1)
                    nc.scalar.activation(r[i][:, :], ps_m[min(i, 1)][:, 0:HE], ACT.Silu).then_inc(s_r, 1)
                    if i == 0:
                        act.sem_inc(rbf_free, 1)

                def tpw(e):
                    act.wait_ge(s_wp, 1)
                    act.sem_inc(s_wp, -1)
                    act.wait_ge(w_free, 1)
                    act.sem_inc(w_free, -1)
                    for j in range(GT):
                        v = ps_w[:, j // 2, (j % 2) * D:(j % 2 + 1) * D]
                        nc.scalar.activation(w[e.slot][:, j, 0:2 * C], v[:, 0:2 * C], ACT.Copy,
                                             scale=S.sh0[:, bass.ds(e.g * GT + j, 1), 0:1].rearrange("p a b -> p (a b)"))
                    for b in range(2):
                        v = ps_w[:, b, :].rearrange("p (n d) -> p n d", d=D)
                        ins = nc.scalar.copy(w[e.slot][:, 2 * b:2 * b + 2, 2 * C:D], v[:, :, 2 * C:D])
                    tell(act, ins, B.own, w_ready, wp_free)

                def counts():
                    act.wait_ge(repeat_ready, 1)
                    act.sem_inc(repeat_ready, -1)
                    for j in range(GT):
                        ins = nc.scalar.activation(junk[:, j, :], repeat[:, j, :], ACT.Copy, accum_out=count[:, j:j + 1])
                    ins.then_inc(count_ready, 1)

                def sums(e):
                    sums_done(act, B)
                    sum_copy(nc, act, B, e, pss)

                def body(it, c, do_sums=True):
                    silu(0)
                    counts()
                    tpw(Edge(it, c))
                    silu(1)
                    if do_sums:
                        sums(Edge(it, c - 1))
                    silu(2)
                silu(0)
                silu(1)
                silu(2)
                body(0, 0, False)
                with act.Fori(0, PASSES) as it:
                    for c in range(1, UNROLL + 1):
                        body(it, c)
                body(0, G - 3)
                body(0, G - 2)
                last = Edge(0, G - 1)
                counts()
                tpw(last)
                sums(Edge(0, G - 2))
                sums(last)

            @block.vector
            def _(dve):
                link = linker(dve, s_link)
                nc.vector.memset(M1[:, :, :], 0.0)
                nc.vector.memset(M2[:, :, :], 0.0)
                link(nc.vector.memset(M3[:, :, :], 0.0))
                dve.sem_inc(s_zeroed, 1)
                dve.sem_inc(B.row_free, 2)
                dve.sem_inc(B.got_free, UNROLL)
                dve.sem_inc(B.put_free, 2)
                dve.sem_inc(w_free, 2)
                link(nc.vector.tensor_scalar(sh3[:, :, :], S.sh0[:, :, 1:4], 1.0 / SQ3, None, ALU.mult))

                def index(e):
                    nc.vector.tensor_copy(B.take_i[e.deep][:, :], S.src[:, bass.ds(e.g * GT, GT)]).then_inc(B.idx_ready, 1)

                def body(it, c, more=True, first=False, same=True):
                    TT = nc.vector.tensor_tensor
                    e, n = Edge(it, c), Edge(it, c + 1)
                    x, m, v = got[e.deep], B.msg[e.slot], w[e.slot]
                    xv = x[:, :, C:D].rearrange("p t (k c) -> p t k c", k=3)
                    mv = m[:, :, C:D].rearrange("p t (k c) -> p t k c", k=3)
                    dst = S.dstf[:, bass.ds(e.g * GT, GT)]
                    dve.wait_ge(B.got[e.deep], 16 * GT * e.deep_use)
                    dve.sem_inc(B.passed, 1)
                    TT(prod[:, :, :, :], xv, bc(sh3[:, bass.ds(e.g * GT, GT), :], C, 3), ALU.mult)
                    dve.wait_ge(w_ready, 1)
                    dve.sem_inc(w_ready, -1)
                    link(TT(m[:, :, 0:C], x[:, :, 0:C], v[:, :, 0:C], ALU.mult))
                    TT(q[:, :, :], prod[:, :, 0, :], prod[:, :, 1, :], ALU.add)
                    TT(a[:, :, :], x[:, :, 0:C], v[:, :, 2 * C:3 * C], ALU.mult)
                    dve.wait_ge(count_ready, 1)
                    dve.sem_inc(count_ready, -1)
                    nc.vector.scalar_tensor_tensor(out=putf[:, :], in0=count[:, :], scalar=0.5, in1=putf[:, :],
                                                   op0=ALU.is_gt, op1=ALU.mult)
                    link(TT(mv, xv, bc(v[:, :, C:2 * C], 3, 2), ALU.mult))
                    dve.sem_inc(B.got_free, 1)
                    TT(S.put[:, bass.ds(e.g * GT, GT)], putf[:, :], dst, ALU.add)
                    ins = TT(q[:, :, :], q[:, :, :], prod[:, :, 2, :], ALU.add)
                    if same:
                        ins = make_same(nc, dve, S, B, n)
                    link(ins)
                    if same:
                        dve.sem_inc(B.row_free, 1)
                        repeats(n)
                    TT(q3[:, :, :], q[:, :, :], v[:, :, 3 * C:D], ALU.mult)
                    link(TT(ash[:, :, :, :], bc(a[:, :, :], 3, 2), bc(S.sh0[:, bass.ds(e.g * GT, GT), 1:4], C, 3), ALU.mult))
                    dve.sem_inc(w_free, 1)
                    if more:
                        index(Edge(it, c + 3))
                    if not first:
                        target(nc, dve, S, B, Edge(it, c - 1))
                    TT(m[:, :, 0:C], m[:, :, 0:C], q3[:, :, :], ALU.add)
                    TT(mv, mv, ash[:, :, :, :], ALU.add).then_inc(B.msg_ready, 1)

                def repeats(e):
                    nc.vector.tensor_scalar(putf[:, :], S.dstf[:, bass.ds(e.g * GT, GT)], S.dump[:, 0:1], -1.0,
                                            ALU.subtract, ALU.mult)
                    nc.vector.tensor_tensor(repeat[:, :, :], B.same[e.slot][:, :, :], bc(S.before[:, :], GT, 1),
                                            ALU.mult).then_inc(repeat_ready, 1)

                for c in range(3):
                    index(Edge(0, c))
                link(make_same(nc, dve, S, B, Edge(0, 0)))
                dve.sem_inc(B.row_free, 1)
                repeats(Edge(0, 0))
                body(0, 0, first=True)
                with dve.Fori(0, PASSES) as it:
                    for c in range(1, UNROLL + 1):
                        body(it, c)
                body(0, G - 3, more=False)
                body(0, G - 2, more=False)
                body(0, G - 1, more=False, same=False)
                target(nc, dve, S, B, Edge(0, G - 1))



def load_sums(sp, acc, to, s_in, c):
    for i in range(GT):
        rows = acc[i][0:N, :].rearrange("(p t) d -> p t d", t=NT)
        sp.dma_start(to[:, i, :, :], rows[:, bass.ds(c * CT, CT), :]).then_inc(s_in, 16)


def last_nodes(nc, ctx, I, S):
    def sem(name):
        return S.signals.get("ln", name)

    with ExitStack() as loc:
        def tb(name, shape, dt=F32):
            return loc.enter_context(nc.sbuf_tensor("ln_" + name, shape, dt))
        a4 = tb("acc", [P, GT, CT, D])
        hT = tb("hT", [128, 2, CN])
        A, Bm, sq = tb("A", [P, CT, D]), tb("B", [P, CT, D]), tb("sq", [P, CT, 3, C])
        vv, a2, t1, t2, t3 = (tb(n, [P, CT, C]) for n in ("vv", "a2", "t1", "t2", "t3"))
        big = tb("squares", [P, NT, D])
        bd = tb("bd", [128, 4, 128])
        wc0, wc1 = tb("wc0", [P, 5, C]), tb("wc1", [P, 4, C])
        gam = tb("gam", [P, 3, C])
        mu = tb("mu", [P, C])
        var = tb("var", [P, 2, C])
        fac = tb("fac", [P, 4, C])
        pst = loc.enter_context(nc.psum_tensor("ln_pst", [128, 3, 512], F32))
        pso = loc.enter_context(nc.psum_tensor("ln_pso", [P, 3, 512], F32))
        pstat = loc.enter_context(nc.psum_tensor("ln_pstat", [128, 2, 512], F32))
        (s_bz, s_w, s_in, s_a4free, s_h, s_t, s_hT, s_A, s_Ac, s_B, s_t2, s_o, s_od, s_link, s_st, s_sq, s_var, s_std, s_cent,
         s_pass) = (sem(n) for n in (
             "bd_zero", "weights", "acc_in", "acc_free", "sum_ready", "turned", "hT_ready", "A_in_psum", "A_ready", "B_ready",
             "B_turned", "out_in_psum", "out_used", "dve_step", "stat_in_psum", "squares_ready", "variance", "deviation",
             "centred", "dma_waits_passed"))
        with nc.Block() as block:
            @block.sync
            def _(sp):
                for to, fr in ((wc0, I["Wc0r"]), (wc1, I["Wc1r"]), (gam, I["gam"])):
                    sp.dma_start(to[:, :, :].rearrange("p a b -> p (a b)"), fr.broadcast_to([P, fr.shape[1]])).then_inc(s_w, 16)
                sp.wait_ge(s_bz, 1)
                sp.sem_inc(s_bz, -1)
                for i, (a, b) in enumerate(((I["Wlin0"], I["Wlin1"]), (I["Wlin1"], I["Wlin1"]), (I["WB0"], I["WB1"]), (I["WB1"], I["WB1"]))):
                    sp.dma_start(bd[0:C, i, 0:C], a).then_inc(s_w, 16)
                    sp.dma_start(bd[C:128, i, C:128], b).then_inc(s_w, 16)
                with sp.Fori(0, CHUNKS) as c:
                    sp.wait_ge(s_a4free, 1)
                    sp.sem_inc(s_a4free, -1)
                    load_sums(sp, S.acc[0], a4, s_in, c)

            @block.vector
            def _(dve):
                link = linker(dve, s_link)
                nc.vector.memset(bd[:, :, :], 0.0).then_inc(s_bz, 1)
                dve.sem_inc(s_a4free, 1)
                dve.wait_ge(s_w, 16 * 11)
                TT, TS = nc.vector.tensor_tensor, nc.vector.tensor_scalar

                def w(t, i):
                    return bc(t[:, i, :], CT, 1)
                with dve.Fori(0, CHUNKS) as c:
                    dve.wait_ge(s_in, 16 * GT * c + 16 * GT)
                    dve.sem_inc(s_pass, 1)
                    TT(a4[:, 0, :, :], a4[:, 0, :, :], a4[:, 1, :, :], ALU.add)
                    link(TT(a4[:, 2, :, :], a4[:, 2, :, :], a4[:, 3, :, :], ALU.add))
                    TT(a4[:, 0, :, :], a4[:, 0, :, :], a4[:, 2, :, :], ALU.add).then_inc(s_h, 1)
                    dve.wait_ge(s_Ac, 1)
                    dve.sem_inc(s_Ac, -1)
                    dve.sem_inc(s_a4free, 1)
                    A0, A1 = A[:, :, 0:C], A[:, :, C:D].rearrange("p t (k c) -> p t k c", k=3)
                    TT(a2[:, :, :], A0, A0, ALU.mult)
                    link(TT(sq[:, :, :, :], A1, A1, ALU.mult))
                    link(TT(vv[:, :, :], sq[:, :, 0, :], sq[:, :, 1, :], ALU.add))
                    TT(t1[:, :, :], A0, w(wc0, 3), ALU.mult)
                    link(TT(vv[:, :, :], vv[:, :, :], sq[:, :, 2, :], ALU.add))
                    TT(t2[:, :, :], vv[:, :, :], w(wc0, 4), ALU.mult)
                    TT(t3[:, :, :], vv[:, :, :], w(wc0, 2), ALU.mult)
                    link(TT(t1[:, :, :], t1[:, :, :], w(wc0, 1), ALU.add))
                    link(TT(t2[:, :, :], t2[:, :, :], w(wc0, 0), ALU.add))
                    TT(t1[:, :, :], t1[:, :, :], a2[:, :, :], ALU.mult)
                    link(TT(t2[:, :, :], t2[:, :, :], A0, ALU.mult))
                    link(TT(t1[:, :, :], t1[:, :, :], t2[:, :, :], ALU.add))
                    TT(Bm[:, :, 0:C], t1[:, :, :], t3[:, :, :], ALU.add)
                    TT(t2[:, :, :], A0, w(wc1, 1), ALU.mult)
                    TT(vv[:, :, :], vv[:, :, :], w(wc1, 3), ALU.mult)
                    link(TT(a2[:, :, :], a2[:, :, :], w(wc1, 2), ALU.mult))
                    TT(t2[:, :, :], t2[:, :, :], w(wc1, 0), ALU.add)
                    link(TT(a2[:, :, :], a2[:, :, :], vv[:, :, :], ALU.add))
                    link(TT(t2[:, :, :], t2[:, :, :], a2[:, :, :], ALU.add))
                    TT(Bm[:, :, C:D].rearrange("p t (k c) -> p t k c", k=3), A1, bc(t2[:, :, :], 3, 2), ALU.mult).then_inc(s_B, 1)
                    dve.wait_ge(s_o, 1)
                    dve.sem_inc(s_o, -1)
                    for b in range(3):
                        v, r = banks(pso, b)
                        k = S.skip[:, bass.ds(c * CT + r.start, r.stop - r.start), :]
                        ins = TT(k, k, v, ALU.add)
                    ins.then_inc(s_od, 1)
                dve.wait_ge(s_st, 1)
                dve.sem_inc(s_st, -1)
                link(TS(mu[:, :], pstat[0:P, 0, 0:C], 1.0 / N, None, ALU.mult))
                TT(S.skip[:, :, 0:C], S.skip[:, :, 0:C], bc(mu[:, :], NT, 1), ALU.subtract).then_inc(s_cent, 1)
                dve.wait_ge(s_st, 1)
                dve.sem_inc(s_st, -1)
                link(TS(fac[:, :, :].rearrange("p a b -> p (a b)"), pstat[0:P, 1, 0:D], 1.0 / N, None, ALU.mult))
                link(TT(fac[:, 1, :], fac[:, 1, :], fac[:, 2, :], ALU.add))
                link(TT(fac[:, 1, :], fac[:, 1, :], fac[:, 3, :], ALU.add))
                TS(var[:, 0, :], fac[:, 0, :], LN_EPS, None, ALU.add)
                TS(var[:, 1, :], fac[:, 1, :], 1.0 / 3.0, LN_EPS, ALU.mult, ALU.add).then_inc(s_var, 1)
                dve.wait_ge(s_std, 1)
                dve.sem_inc(s_std, -1)
                link(nc.vector.reciprocal(var[:, :, :], var[:, :, :]))
                TT(fac[:, 0, :], var[:, 0, :], gam[:, 0, :], ALU.mult)
                for k in range(3):
                    ins = TT(fac[:, k + 1, :], var[:, 1, :], gam[:, 2, :], ALU.mult)
                link(ins)
                link(TT(S.skip[:, :, :], S.skip[:, :, :], bc(fac[:, :, :].rearrange("p a b -> p (a b)"), NT, 1), ALU.mult))
                link(TT(S.x[:, :, :], S.x[:, :, :], S.skip[:, :, :], ALU.add))
                link(TT(S.x[:, :, 0:C], S.x[:, :, 0:C], bc(gam[:, 1, :], NT, 1), ALU.add))

            @block.tensor
            def _(pe):
                pe.wait_ge(s_w, 16 * 11)
                with pe.Fori(0, CHUNKS) as c:
                    pe.wait_ge(s_h, 1)
                    pe.sem_inc(s_h, -1)
                    turn(nc, a4[:, 0, :, :], S.ident, pst).then_inc(s_t, 1)
                    pe.wait_ge(s_hT, 1)
                    pe.sem_inc(s_hT, -1)
                    linear(nc, hT, bd[:, 0, :], bd[:, 1, :], pso).then_inc(s_A, 1)
                    pe.wait_ge(s_B, 1)
                    pe.sem_inc(s_B, -1)
                    turn(nc, Bm, S.ident, pst).then_inc(s_t, 1)
                    pe.wait_ge(s_hT, 1)
                    pe.sem_inc(s_hT, -1)
                    linear(nc, hT, bd[:, 2, :], bd[:, 3, :], pso).then_inc(s_o, 1)
                    pe.wait_ge(s_od, 1)
                    pe.sem_inc(s_od, -1)
                for k, src in ((0, S.skip), (1, big)):
                    if k:
                        pe.wait_ge(s_sq, 1)
                        pe.sem_inc(s_sq, -1)
                    for t in range(NT):
                        ins = nc.tensor.matmul(pstat[:, k, 0:D], S.ones[:, :], src[:, t, :], start=(t == 0), stop=(t == NT - 1))
                    ins.then_inc(s_st, 1)

            @block.scalar
            def _(act):
                with act.Fori(0, CHUNKS) as c:
                    act.wait_ge(s_t, 1)
                    act.sem_inc(s_t, -1)
                    turned(nc, pst, hT).then_inc(s_hT, 1)
                    act.wait_ge(s_A, 1)
                    act.sem_inc(s_A, -1)
                    for b in range(3):
                        v, r = banks(pso, b)
                        ins = nc.scalar.copy(A[:, r, :], v)
                    ins.then_inc(s_Ac, 1)
                    act.wait_ge(s_t, 1)
                    act.sem_inc(s_t, -1)
                    turned(nc, pst, hT).then_inc(s_hT, 1)
                act.wait_ge(s_cent, 1)
                act.sem_inc(s_cent, -1)
                nc.scalar.activation(big[:, :, :], S.skip[:, :, :], ACT.Square).then_inc(s_sq, 1)
                act.wait_ge(s_var, 1)
                act.sem_inc(s_var, -1)
                nc.scalar.activation(var[:, :, :], var[:, :, :], ACT.Sqrt).then_inc(s_std, 1)



def mixture(nc, ctx, I, S, layer, out=None):
    pre = f"m{layer}_"
    hid = 2 if layer == 0 else 4
    steps = 2 if layer == 0 else 1

    def sem(name):
        return S.signals.get(pre, name)

    with ExitStack() as loc:
        def tb(name, shape, dt=F32):
            return loc.enter_context(nc.sbuf_tensor(pre + name, shape, dt))
        h, st, hT = tb("h", [P, CT, D]), tb("st", [P, CT, 9]), tb("hT", [128, 2, CN])
        next_hT = tb("next_hT", [128, 2, CN])
        a4 = tb("acc", [P, GT, CT, D]) if layer else None
        hid1 = [tb(f"hid{i}", [128, hid, CN]) for i in range(2)]
        wr, bo = tb("gate_w", [128, 2, NEXP]), tb("out_bias", [NEXP, D])
        br = tb("gate_b", [P, 2, NEXP])
        lg, ex = tb("logits", [P, CT, NEXP]), tb("exps", [P, CT, NEXP])
        m8, i8, i8f = tb("best", [P, CT, 8]), tb("best_i", [P, CT, 8], U32), tb("best_f", [P, CT, 8])
        iota_i, iota = tb("iota_i", [P, NEXP], I32), tb("iota", [P, NEXP])
        s1 = tb("s1", [P, CT, 4])
        wg = tb("weights", [P, NT, NEXP])
        wgn = tb("next_weights", [P, CT, NEXP])
        wT = tb("weights_T", [NEXP, CN])
        psh = loc.enter_context(nc.psum_tensor(pre + "psh", [128, 4, 512], F32))
        pso = loc.enter_context(nc.psum_tensor(pre + "pso", [P, 3, 512], F32))
        pst = loc.enter_context(nc.psum_tensor(pre + "pst", [128, 512], F32))
        psg = pst[0:P, 0:CT * NEXP]
        bn = tb("bn", [128, 5, 2, 16]) if layer == 0 else None
        b1 = None if layer == 0 else tb("b1", [128, 32])
        (s_w, s_in, s_free4, s_var, s_std, s_h, s_t, s_hT, s_g, s_lg, s_ex, s_wg, s_wt, s_wT, s_b, s_bd, s_m, s_ev, s_o, s_od,
         s_hTc, s_link, s_bnv, s_bns, s_aff, s_pass, s_iota, s_x, s_out) = (sem(n) for n in (
             "small_weights", "acc_in", "acc_free", "variance", "deviation", "h_ready", "turned", "hT_ready", "gates_in_psum",
             "logits_ready", "exps_ready", "gates_ready", "gates_turned", "gates_T_ready", "bias_in_psum", "bias_added",
             "hidden_in_psum", "hidden_ready", "out_in_psum", "out_added", "hT_moved", "dve_step", "bn_variance", "bn_deviation",
             "affine_ready", "dma_waits_passed", "iota", "x_ready", "stored"))
        smalls = [(wr[:, :, :], (I["Wr"] if layer == 0 else I["Wg"]).rearrange("(k p) e -> p k e", p=128)),
                  (bo[:, :], I["bo"] if layer == 0 else I["b2"])]
        if layer == 0:
            smalls += [(br[:, 0, :], I["br"].broadcast_to([P, NEXP])), (bn[:, :, :, :], I["bn"])]
        else:
            smalls += [(br[:, 0, :], I["bg"].broadcast_to([P, NEXP])), (br[:, 1, :], I["bias"].broadcast_to([P, NEXP])), (b1[:, :], I["b1"])]
        with nc.Block() as block:
            @block.sync
            def _(sp):
                for to, fr in smalls:
                    sp.dma_start(to, fr).then_inc(s_w, 16)
                if layer:
                    rows = out.rearrange("(p t) d -> p t d", t=NT)
                    with sp.Fori(0, CHUNKS) as c:
                        sp.wait_ge(s_free4, 1)
                        sp.sem_inc(s_free4, -1)
                        load_sums(sp, S.acc[1], a4, s_in, c)
                    with sp.Fori(0, CHUNKS) as c:
                        sp.wait_ge(s_x, 1)
                        sp.sem_inc(s_x, -1)
                        sp.dma_start(rows[:, bass.ds(c * CT, CT), :], S.x[:, bass.ds(c * CT, CT), :]).then_inc(s_out, 16)
                    sp.wait_ge(s_out, 16 * CHUNKS)

            @block.gpsimd
            def _(pool):
                nc.gpsimd.iota(iota_i[:, :], pattern=[[1, NEXP]], base=0, channel_multiplier=0).then_inc(s_iota, 1)

            @block.vector
            def _(dve):
                link = linker(dve, s_link)
                TT, TS, STT = nc.vector.tensor_tensor, nc.vector.tensor_scalar, nc.vector.scalar_tensor_tensor
                dve.wait_ge(s_iota, 1)
                nc.vector.tensor_copy(iota[:, :], iota_i[:, :])
                dve.wait_ge(s_w, 16 * len(smalls))
                if layer == 0:
                    TS(bn[:, 4, :, :], bn[:, 4, :, :], BN_EPS, None, ALU.add).then_inc(s_bnv, 1)
                    dve.wait_ge(s_bns, 1)
                    dve.sem_inc(s_bns, -1)
                    TT(bn[:, 1, :, :], bn[:, 1, :, :], bn[:, 3, :, :], ALU.subtract)
                    link(nc.vector.reciprocal(bn[:, 4, :, :], bn[:, 4, :, :]))
                    link(TT(bn[:, 0, :, :], bn[:, 0, :, :], bn[:, 4, :, :], ALU.mult))
                    link(TT(bn[:, 1, :, :], bn[:, 1, :, :], bn[:, 0, :, :], ALU.mult))
                    link(TT(bn[:, 2, :, :], bn[:, 2, :, :], bn[:, 1, :, :], ALU.add))
                    dve.sem_inc(s_aff, 1)
                else:
                    link(TT(br[:, 0, :], br[:, 0, :], br[:, 1, :], ALU.add))
                    dve.sem_inc(s_free4, 1)
                dve.sem_inc(s_od, 1)

                def norm_begin(n):
                    x = S.x[:, bass.ds(n * CT, CT), :]
                    if layer:
                        dve.wait_ge(s_in, 16 * GT * n + 16 * GT)
                        dve.sem_inc(s_pass, 1)
                        TT(a4[:, 0, :, :], a4[:, 0, :, :], a4[:, 1, :, :], ALU.add)
                        link(TT(a4[:, 2, :, :], a4[:, 2, :, :], a4[:, 3, :, :], ALU.add))
                        link(TT(a4[:, 0, :, :], a4[:, 0, :, :], a4[:, 2, :, :], ALU.add))
                        link(TT(x, x, a4[:, 0, :, :], ALU.add))
                        dve.sem_inc(s_free4, 1)
                    statistics(nc, link, x, st).then_inc(s_var, 1)

                def norm_end(n):
                    dve.wait_ge(s_std, 1)
                    dve.sem_inc(s_std, -1)
                    normed(nc, link, S.x[:, bass.ds(n * CT, CT), :], h, st).then_inc(s_h, 1)

                def gates_begin(n):
                    dve.wait_ge(s_g, 1)
                    dve.sem_inc(s_g, -1)
                    link(TT(lg[:, :, :], psg.rearrange("p (t e) -> p t e", e=NEXP), bc(br[:, 0, :], CT, 1), ALU.add))
                    if layer == 0:
                        link(nc.vector.tensor_reduce(s1[:, :, 0], lg[:, :, :], AX, ALU.max))
                        TT(lg[:, :, :], lg[:, :, :], bc(s1[:, :, 0], NEXP, 2), ALU.subtract).then_inc(s_lg, 1)
                        return
                    for j in range(CT):
                        ins = nc.vector.max(m8[:, j, :], lg[:, j, :])
                    link(ins)
                    for j in range(CT):
                        ins = nc.vector.max_index(i8[:, j, :], m8[:, j, :], lg[:, j, :])
                    link(ins)
                    nc.vector.tensor_copy(i8f[:, :, :], i8[:, :, :])
                    TT(s1[:, :, 0], m8[:, :, 1], m8[:, :, 0], ALU.subtract).then_inc(s_lg, 1)

                def gates_end(n):
                    weights = wg[:, bass.ds(n * CT, CT), :]
                    dve.wait_ge(s_ex, 1)
                    dve.sem_inc(s_ex, -1)
                    if layer == 0:
                        link(nc.vector.tensor_reduce(s1[:, :, 1], ex[:, :, :], AX, ALU.add))
                        link(nc.vector.reciprocal(s1[:, :, 1], s1[:, :, 1]))
                        link(TT(wgn[:, :, :], ex[:, :, :], bc(s1[:, :, 1], NEXP, 2), ALU.mult))
                    else:
                        link(TS(s1[:, :, 2], s1[:, :, 1], 1.0, None, ALU.add))
                        link(nc.vector.reciprocal(s1[:, :, 2], s1[:, :, 2]))
                        link(TT(s1[:, :, 3], s1[:, :, 2], s1[:, :, 1], ALU.mult))
                        for j in range(CT):
                            TS(wgn[:, j, :], iota[:, :], i8f[:, j, 0:1], s1[:, j, 2:3], ALU.is_equal, ALU.mult)
                            ins = TS(ex[:, j, :], iota[:, :], i8f[:, j, 1:2], s1[:, j, 3:4], ALU.is_equal, ALU.mult)
                        link(ins)
                        link(TT(wgn[:, :, :], wgn[:, :, :], ex[:, :, :], ALU.add))
                    dve.sem_inc(s_wg, 1)
                    nc.vector.tensor_copy(weights, wgn[:, :, :])

                def experts(c, ahead):
                    dve.wait_ge(s_b, 1)
                    dve.sem_inc(s_b, -1)
                    for b in range(3):
                        v, r = banks(pso, b)
                        xk = S.x[:, bass.ds(c * CT + r.start, r.stop - r.start), :]
                        ins = TT(xk, xk, v, ALU.add)
                    link(ins)
                    dve.sem_inc(s_od, 1)
                    for e in range(NEXP):
                        dve.wait_ge(s_o, 1)
                        dve.sem_inc(s_o, -1)
                        for j in range(CT):
                            xk = S.x[:, bass.ds(c * CT + j, 1), :].rearrange("p a d -> p (a d)")
                            weight = wg[:, bass.ds(c * CT + j, 1), e:e + 1].rearrange("p a b -> p (a b)")
                            ins = STT(out=xk, in0=pso[:, j // 2, (j % 2) * D:(j % 2 + 1) * D], scalar=weight,
                                      in1=xk, op0=ALU.mult, op1=ALU.add)
                        link(ins)
                        dve.sem_inc(s_od, 1)
                        if ahead and e == 0:
                            norm_begin(c + 1)
                        elif ahead and e == 1:
                            norm_end(c + 1)
                        elif ahead and e == 5:
                            gates_begin(c + 1)
                        elif ahead and e == 6:
                            gates_end(c + 1)
                    if layer:
                        dve.sem_inc(s_x, 1)

                norm_begin(0)
                norm_end(0)
                gates_begin(0)
                gates_end(0)
                with dve.Fori(0, CHUNKS - 1) as c:
                    experts(c, True)
                experts(CHUNKS - 1, False)

            @block.scalar
            def _(act):
                if layer == 0:
                    act.wait_ge(s_bnv, 1)
                    act.sem_inc(s_bnv, -1)
                    nc.scalar.activation(bn[:, 4, :, :], bn[:, 4, :, :], ACT.Sqrt).then_inc(s_bns, 1)
                    act.wait_ge(s_aff, 1)
                    act.sem_inc(s_aff, -1)
                else:
                    act.wait_ge(s_w, 16 * len(smalls))

                def deviation():
                    root(nc, act, st, s_var, s_std)

                def turned_round(i):
                    act.wait_ge(s_t, 1)
                    act.sem_inc(s_t, -1)
                    n = min(4, 2 * CT - 4 * i) // 2
                    o = next_hT[:, :, 2 * i * P:(2 * i + n) * P].rearrange("p k (j e) -> p j k e", j=n)
                    nc.scalar.copy(o, pst[:, 0:2 * n * P].rearrange("p (j k e) -> p j k e", j=n, k=2)).then_inc(s_hT, 1)

                def exps():
                    act.wait_ge(s_lg, 1)
                    act.sem_inc(s_lg, -1)
                    if layer == 0:
                        nc.scalar.activation(ex[:, :, :], lg[:, :, :], ACT.Exp).then_inc(s_ex, 1)
                    else:
                        nc.scalar.activation(s1[:, :, 1], s1[:, :, 0], ACT.Exp).then_inc(s_ex, 1)
                    nc.scalar.copy(hT[:, :, :], next_hT[:, :, :]).then_inc(s_hTc, 1)

                def weights_round(i):
                    act.wait_ge(s_wt, 1)
                    act.sem_inc(s_wt, -1)
                    lo, hi = (0, 4 * P) if i == 0 else (4 * P, CN)
                    nc.scalar.copy(wT[:, lo:hi], pst[0:NEXP, 0:hi - lo]).then_inc(s_wT, 1)

                def experts(ahead):
                    def evacuate(e, step, m):
                        act.wait_ge(s_m, 1)
                        act.sem_inc(s_m, -1)
                        for i in range(2):
                            lo, hi = SPLIT[i], SPLIT[i + 1]
                            v = psh[:, 2 * (m % 2) + i, 0:hi - lo]
                            k = e * 2 + m
                            if layer == 0:
                                ins = nc.scalar.activation(hid1[step][:, m, lo:hi], v, ACT.Relu, bias=bn[:, 2, step, k:k + 1],
                                                           scale=bn[:, 0, step, k:k + 1])
                            else:
                                ins = nc.scalar.activation(hid1[e % 2][:, m, lo:hi], v, ACT.Relu,
                                                           bias=b1[:, 4 * e + m:4 * e + m + 1])
                        ins.then_inc(s_ev, 1)

                    for e in range(NEXP):
                        for step in range(steps):
                            for m in range(hid):
                                evacuate(e, step, m)
                            if ahead and step == 0:
                                if e == 2:
                                    deviation()
                                elif 4 <= e <= 6:
                                    turned_round(e - 4)
                                elif e == 7:
                                    exps()
                    if ahead:
                        weights_round(0)
                        weights_round(1)

                deviation()
                for i in range(3):
                    turned_round(i)
                exps()
                weights_round(0)
                weights_round(1)
                with act.Fori(0, CHUNKS - 1) as c:
                    experts(True)
                experts(False)


            @block.tensor
            def _(pe):
                pe.wait_ge(s_w, 16 * len(smalls))
                for s, n in S.mw_in[layer]:
                    pe.wait_ge(s, n)

                def hidden(w, e, src, m):
                    for i in range(2):
                        lo, hi = SPLIT[i], SPLIT[i + 1]
                        for k in range(2):
                            ins = nc.tensor.matmul(psh[:, 2 * (m % 2) + i, 0:hi - lo], w[:, e, k, m * 128:(m + 1) * 128],
                                                   src[:, k, lo:hi], start=(k == 0), stop=(k == 1))
                    ins.then_inc(s_m, 1)

                def output(w, e, src):
                    pe.wait_ge(s_od, 1)
                    pe.sem_inc(s_od, -1)
                    for j in range(CT):
                        for k in range(hid):
                            ins = nc.tensor.matmul(pso[:, j // 2, (j % 2) * D:(j % 2 + 1) * D], src[:, k, j * P:(j + 1) * P],
                                                   w[:, e, k, :], start=(k == 0), stop=(k == hid - 1))
                    ins.then_inc(s_o, 1)

                def turn_round(i):
                    if i == 0:
                        pe.wait_ge(s_h, 1)
                        pe.sem_inc(s_h, -1)
                    else:
                        pe.wait_ge(s_hT, 1)
                        pe.sem_inc(s_hT, -1)
                    for b in range(4 * i, min(4 * i + 4, 2 * CT)):
                        ins = nc.tensor.transpose(pst[:, (b % 4) * P:(b % 4 + 1) * P], h[:, b // 2, (b % 2) * 128:(b % 2 + 1) * 128],
                                                  S.ident[0:P, 0:P])
                    ins.then_inc(s_t, 1)

                def logits():
                    pe.wait_ge(s_hT, 1)
                    pe.sem_inc(s_hT, -1)
                    for j in range(CT):
                        for k in range(2):
                            ins = nc.tensor.matmul(psg[:, j * NEXP:(j + 1) * NEXP], next_hT[:, k, j * P:(j + 1) * P], wr[:, k, :],
                                                   start=(k == 0), stop=(k == 1))
                    ins.then_inc(s_g, 1)

                def turn_next(i):
                    if i < 3:
                        turn_round(i)
                    else:
                        logits()

                def turn_weights(i):
                    if i == 0:
                        pe.wait_ge(s_wg, 1)
                        pe.sem_inc(s_wg, -1)
                    else:
                        pe.wait_ge(s_wT, 1)
                        pe.sem_inc(s_wT, -1)
                    for j in (range(4) if i == 0 else (4,)):
                        ins = nc.tensor.transpose(pst[0:NEXP, (j % 4) * P:(j % 4 + 1) * P], wgn[:, j, :], S.ident[0:P, 0:P])
                    ins.then_inc(s_wt, 1)

                def biases():
                    pe.wait_ge(s_wT, 1)
                    pe.sem_inc(s_wT, -1)
                    pe.wait_ge(s_od, 1)
                    pe.sem_inc(s_od, -1)
                    for j in range(CT):
                        ins = nc.tensor.matmul(pso[:, j // 2, (j % 2) * D:(j % 2 + 1) * D], wT[:, j * P:(j + 1) * P], bo[:, :],
                                               start=True, stop=True)
                    ins.then_inc(s_b, 1)

                def experts(ahead):
                    W = S.mw[layer]
                    pe.wait_ge(s_hTc, 1)
                    pe.sem_inc(s_hTc, -1)
                    if layer == 0:
                        hidden(W[0], 0, hT, 0)
                        hidden(W[0], 0, hT, 1)
                        biases()
                        for e in range(NEXP):
                            pe.wait_ge(s_ev, 2)
                            pe.sem_inc(s_ev, -2)
                            hidden(W[1], e, hid1[0], 0)
                            hidden(W[1], e, hid1[0], 1)
                            if e + 1 < NEXP:
                                pe.wait_ge(s_ev, 1)
                                pe.sem_inc(s_ev, -1)
                                hidden(W[0], e + 1, hT, 0)
                                pe.wait_ge(s_ev, 1)
                                pe.sem_inc(s_ev, -1)
                                hidden(W[0], e + 1, hT, 1)
                            else:
                                if ahead:
                                    turn_weights(0)
                                pe.wait_ge(s_ev, 2)
                                pe.sem_inc(s_ev, -2)
                            output(W[2], e, hid1[1])
                            if ahead and 2 <= e <= 5:
                                turn_next(e - 2)
                    else:
                        for e in range(NEXP):
                            for m in range(hid):
                                if e or m > 1:
                                    pe.wait_ge(s_ev, 1)
                                    pe.sem_inc(s_ev, -1)
                                hidden(W[0], e, hT, m)
                            if e:
                                output(W[1], e - 1, hid1[(e - 1) % 2])
                                if ahead and 3 <= e <= 6:
                                    turn_next(e - 3)
                            else:
                                biases()
                        if ahead:
                            turn_weights(0)
                        pe.wait_ge(s_ev, 2)
                        pe.sem_inc(s_ev, -2)
                        output(W[1], NEXP - 1, hid1[(NEXP - 1) % 2])
                    if ahead:
                        turn_weights(1)

                for i in range(3):
                    turn_round(i)
                logits()
                turn_weights(0)
                turn_weights(1)
                with pe.Fori(0, CHUNKS - 1) as c:
                    experts(True)
                experts(False)
                pe.wait_ge(s_od, 1)
                pe.sem_inc(s_od, -1)



def second_nodes(nc, ctx, I, S):
    def sem(name):
        return S.signals.get("sn", name)

    with ExitStack() as loc:
        def tb(name, shape, dt=F32):
            return loc.enter_context(nc.sbuf_tensor("sn_" + name, shape, dt))
        row, st, hT = tb("row", [P, CT, T2]), tb("st", [P, CT, 9]), tb("hT", [128, 2, CN])
        pst = loc.enter_context(nc.psum_tensor("sn_pst", [128, 3, 512], F32))
        pso = loc.enter_context(nc.psum_tensor("sn_pso", [P, 3, 512], F32))
        s_link, s_var, s_std, s_h, s_t, s_hT, s_d, s_row, s_tab, s_rowfree = (sem(n) for n in (
            "dve_step", "variance", "deviation", "h_ready", "turned", "hT_ready", "vectors_in_psum", "row_ready", "table",
            "row_free"))
        with nc.Block() as block:
            @block.sync
            def _(sp):
                rows = S.table2.rearrange("(p t) d -> p t d", t=NT)
                with sp.Fori(0, CHUNKS) as c:
                    sp.wait_ge(s_row, 1)
                    sp.sem_inc(s_row, -1)
                    sp.dma_start(rows[:, bass.ds(c * CT, CT), :], row[:, :, :]).then_inc(s_tab, 16)
                    sp.wait_ge(s_tab, 16 * c + 16)
                    sp.sem_inc(s_rowfree, 1)

            @block.vector
            def _(dve):
                link = linker(dve, s_link)
                dve.sem_inc(s_rowfree, 1)
                with dve.Fori(0, CHUNKS) as c:
                    x = S.x[:, bass.ds(c * CT, CT), :]
                    dve.wait_ge(s_rowfree, 1)
                    dve.sem_inc(s_rowfree, -1)
                    link(normalise(nc, dve, link, x, row[:, :, 0:D], st, s_var, s_std))
                    dve.sem_inc(s_h, 1)
                    link(nc.vector.tensor_tensor(x, x, row[:, :, 0:D], ALU.add))

            @block.tensor
            def _(pe):
                with pe.Fori(0, CHUNKS) as c:
                    pe.wait_ge(s_h, 1)
                    pe.sem_inc(s_h, -1)
                    turn(nc, row, S.ident, pst).then_inc(s_t, 1)
                    pe.wait_ge(s_hT, 1)
                    pe.sem_inc(s_hT, -1)
                    for j in range(CT):
                        o = (j % 2) * 256
                        nc.tensor.matmul(pso[:, j // 2, o:o + C], hT[:, 0, j * P:(j + 1) * P], S.wd[:, 0, 0:C], start=True, stop=True)
                        ins = nc.tensor.matmul(pso[:, j // 2, o + C:o + 3 * C], hT[:, 1, j * P:(j + 1) * P], S.wd[:, 1, :],
                                               start=True, stop=True)
                    ins.then_inc(s_d, 1)

            @block.scalar
            def _(act):
                with act.Fori(0, CHUNKS) as c:
                    root(nc, act, st, s_var, s_std)
                    act.wait_ge(s_t, 1)
                    act.sem_inc(s_t, -1)
                    turned(nc, pst, hT).then_inc(s_hT, 1)
                    act.wait_ge(s_d, 1)
                    act.sem_inc(s_d, -1)
                    for b in range(3):
                        v, r = banks(pso, b)
                        ins = nc.scalar.copy(row[:, r, D:T2], v[:, :, 0:3 * C])
                    ins.then_inc(s_row, 1)



def second_edges(nc, ctx, I, S):
    with ExitStack() as loc:
        def tb(name, shape, dt=F32):
            return loc.enter_context(nc.sbuf_tensor(f"e2_{name}", shape, dt))

        def sem(n):
            return S.signals.get("e2", n)
        B = edge_buffers(nc, loc, S, "e2")
        got = [tb(f"got{s}", [P, GT, C + T2]) for s in range(UNROLL)]
        yx = tb("yx", [128, GE])
        rl = tb("relu", [C, GE])
        cs = [tb(f"c{s}", [P, GT, D]) for s in range(2)]
        ex = tb("exp", [P, GT, C])
        mx, nm, Z, ez, az = (tb(n, [P, GT]) for n in ("max", "neg_max", "Z", "ez", "az"))
        shz = tb("shz", [P, GT, 3])
        t = tb("t", [P, GT, C])
        prod = tb("prod", [P, GT, 3, C])
        p_t = loc.enter_context(nc.psum_tensor("e2_pt", [128, 512], F32))
        p_h = loc.enter_context(nc.psum_tensor("e2_ph", [C, 512], F32))
        p_c = loc.enter_context(nc.psum_tensor("e2_pc", [P, 2, 512], F32))
        pss = loc.enter_context(nc.psum_tensor("e2_pss", [P, 2, 512], F32))
        (y_ready, yx_ps, yx_ready, h_ps, relu_ready, c_ps, c_ps_free, c_ready, c_free, nm_ready, e_ready, az_ready, dz_ready,
         s_link) = (sem(n) for n in (
             "y_ready", "yx_in_psum", "yx_ready", "hidden_in_psum", "relu_ready", "main_in_psum", "main_psum_free",
             "main_ready", "main_free", "neg_max_ready", "exp_ready", "weights_ready", "vectors_weighted", "dve_step"))

        with nc.Block() as block:
            @block.sync
            def _(sp):
                load_experts(nc, sp, S, 1)
                with sp.Fori(0, G // UNROLL) as it:
                    for c in range(UNROLL):
                        load_row(sp, I, B, Edge(it, c))

            @block.gpsimd
            def _(pool):
                edge_pool(nc, pool, B, S.table2, lambda s, j: got[s][:, j, C:C + T2], S.acc[1])

            @block.tensor
            def _(pe):
                pe.sem_inc(B.msg_free, 2)

                def turn_in(e):
                    pe.wait_ge(y_ready, 1)
                    pe.sem_inc(y_ready, -1)
                    for j in range(GT):
                        ins = nc.tensor.transpose(p_t[:, j * P:(j + 1) * P], got[e.deep][:, j, 0:128], S.ident[0:P, 0:P])
                    ins.then_inc(yx_ps, 1)

                def main(e):
                    pe.wait_ge(yx_ready, 1)
                    pe.sem_inc(yx_ready, -1)
                    nc.tensor.matmul(p_h[:, 0:GE], S.wh[:, :], yx[:, :], start=True, stop=True).then_inc(h_ps, 1)
                    pe.wait_ge(c_ps_free, 1)
                    pe.sem_inc(c_ps_free, -1)
                    for j in range(GT):
                        o = (j % 2) * D
                        nc.tensor.matmul(p_c[:, j // 2, o:o + 3 * C], yx[:, j * P:(j + 1) * P], S.wm[:, 0:3 * C],
                                         start=True, stop=True)
                    pe.wait_ge(relu_ready, 1)
                    pe.sem_inc(relu_ready, -1)
                    for j in range(GT):
                        o = (j % 2) * D
                        nc.tensor.matmul(p_c[:, j // 2, o + 3 * C:o + D], yx[:, j * P:(j + 1) * P], S.wm[:, 3 * C:D],
                                         start=True, stop=False)
                        ins = nc.tensor.matmul(p_c[:, j // 2, o + 3 * C:o + D], rl[:, j * P:(j + 1) * P], S.lsc[:, :],
                                               start=False, stop=True)
                    ins.then_inc(c_ps, 1)

                def body(it, c, sums=True):
                    if sums:
                        sum_matmuls(nc, pe, B, Edge(it, c - 1), pss)
                    turn_in(Edge(it, c + 2))
                    main(Edge(it, c + 2))
                for c in range(2):
                    turn_in(Edge(0, c))
                    main(Edge(0, c))
                body(0, 0, False)
                with pe.Fori(0, PASSES) as it:
                    for c in range(1, UNROLL + 1):
                        body(it, c)
                body(0, G - 3)
                for c in range(G - 3, G):
                    sum_matmuls(nc, pe, B, Edge(0, c), pss)

            @block.scalar
            def _(act):
                act.sem_inc(B.sum_free, 2)
                act.sem_inc(B.sum_ps_free, 1)
                act.sem_inc(c_ps_free, 1)

                def yx_copy():
                    act.wait_ge(yx_ps, 1)
                    act.sem_inc(yx_ps, -1)
                    nc.scalar.copy(yx[:, :], p_t[:, 0:GE]).then_inc(yx_ready, 1)

                def relu():
                    act.wait_ge(h_ps, 1)
                    act.sem_inc(h_ps, -1)
                    nc.scalar.activation(rl[:, :], p_h[:, 0:GE], ACT.Relu).then_inc(relu_ready, 1)

                def c_copy(e):
                    act.wait_ge(c_ps, 1)
                    act.sem_inc(c_ps, -1)
                    act.wait_ge(c_free, 1)
                    act.sem_inc(c_free, -1)
                    for b in range(2):
                        ins = nc.scalar.copy(cs[e.slot][:, 2 * b:2 * b + 2, :], p_c[:, b, :].rearrange("p (n d) -> p n d", d=D))
                    tell(act, ins, B.own, c_ready, c_ps_free)

                def exps(e):
                    act.wait_ge(nm_ready, 1)
                    act.sem_inc(nm_ready, -1)
                    nc.scalar.activation(ez[:, :], nm[:, :], ACT.Exp)
                    for j in range(GT):
                        ins = nc.scalar.activation(ex[:, j, :], cs[e.slot][:, j, 3 * C:D], ACT.Exp, bias=nm[:, j:j + 1],
                                                   accum_out=Z[:, j:j + 1])
                    ins.then_inc(e_ready, 1)

                def vectors(e):
                    act.wait_ge(az_ready, 1)
                    act.sem_inc(az_ready, -1)
                    for j in range(GT):
                        ins = nc.scalar.activation(B.msg[e.slot][:, j, C:D], got[e.deep][:, j, C + D:C + T2], ACT.Copy,
                                                   scale=az[:, j:j + 1])
                    ins.then_inc(dz_ready, 1)

                def body(it, c, sums=True, ahead=2):
                    exps(Edge(it, c))
                    vectors(Edge(it, c))
                    if ahead > 1:
                        yx_copy()
                    if sums:
                        sums_done(act, B)
                    if ahead > 0:
                        c_copy(Edge(it, c + 1))
                    if sums:
                        sum_copy(nc, act, B, Edge(it, c - 1), pss)
                    if ahead > 1:
                        relu()
                yx_copy()
                relu()
                c_copy(Edge(0, 0))
                yx_copy()
                relu()
                body(0, 0, False)
                with act.Fori(0, PASSES) as it:
                    for c in range(1, UNROLL + 1):
                        body(it, c)
                body(0, G - 3)
                body(0, G - 2, ahead=1)
                body(0, G - 1, ahead=0)
                sums_done(act, B)
                sum_copy(nc, act, B, Edge(0, G - 1), pss)

            @block.vector
            def _(dve):
                link = linker(dve, s_link)
                TT, TS, STT = nc.vector.tensor_tensor, nc.vector.tensor_scalar, nc.vector.scalar_tensor_tensor
                dve.sem_inc(B.row_free, 2)
                dve.sem_inc(B.got_free, UNROLL)
                dve.sem_inc(B.put_free, 2)
                dve.sem_inc(c_free, 2)

                def col(a, e, j):
                    return a[:, bass.ds(e.g * GT + j, 1)]

                def index(e):
                    nc.vector.tensor_copy(B.take_i[e.deep][:, :], S.src[:, bass.ds(e.g * GT, GT)]).then_inc(B.idx_ready, 1)

                def products(e):
                    dve.wait_ge(B.got[e.deep], 16 * GT * e.deep_use)
                    dve.sem_inc(B.passed, 1)
                    return TT(prod[:, :, :, :], got[e.deep][:, :, 2 * C:5 * C].rearrange("p t (k c) -> p t k c", k=3),
                              bc(S.shn[:, bass.ds(e.g * GT, GT), :], C, 3), ALU.mult)

                def maximum(e):
                    dve.wait_ge(c_ready, 1)
                    dve.sem_inc(c_ready, -1)
                    return nc.vector.tensor_reduce(mx[:, :], cs[e.slot][:, :, 3 * C:D], AX, ALU.max)

                def body(it, c, more=True, first=False, ahead=2):
                    e, n, nn = Edge(it, c), Edge(it, c + 1), Edge(it, c + 2)
                    v, m, y = cs[e.slot], B.msg[e.slot], got[nn.deep][:, :, 0:C]
                    mv = m[:, :, C:D].rearrange("p t (k c) -> p t k c", k=3)
                    TS(nm[:, :], mx[:, :], -1.0, 0.0, ALU.mult, ALU.min).then_inc(nm_ready, 1)
                    if ahead > 1:
                        products(nn)
                    for j in range(GT):
                        ins = STT(out=t[:, j, :], in0=v[:, j, 2 * C:3 * C], scalar=col(S.q, e, j), in1=v[:, j, 0:C],
                                  op0=ALU.mult, op1=ALU.add)
                    link(ins)
                    if ahead > 1:
                        TT(y, prod[:, :, 0, :], prod[:, :, 1, :], ALU.add)
                    if more:
                        index(Edge(it, c + 3))
                    dve.wait_ge(e_ready, 1)
                    dve.sem_inc(e_ready, -1)
                    link(STT(out=Z[:, :], in0=ez[:, :], scalar=float(3 * C), in1=Z[:, :], op0=ALU.mult, op1=ALU.add))
                    if ahead > 1:
                        TT(y, y, prod[:, :, 2, :], ALU.add).then_inc(y_ready, 1)
                    link(nc.vector.reciprocal(Z[:, :], Z[:, :]))
                    link(TT(az[:, :], ez[:, :], Z[:, :], ALU.mult))
                    dve.sem_inc(az_ready, 1)
                    TT(shz[:, :, :], S.shn[:, bass.ds(e.g * GT, GT), :], bc(az[:, :], 3, 2), ALU.mult)
                    for j in range(GT):
                        ins = STT(out=m[:, j, 0:C], in0=t[:, j, :], scalar=Z[:, j:j + 1], in1=ex[:, j, :], op0=ALU.mult, op1=ALU.mult)
                    link(ins)
                    link(TT(prod[:, :, :, :], bc(v[:, :, C:2 * C], 3, 2), bc(shz[:, :, :], C, 3), ALU.mult))
                    dve.sem_inc(c_free, 1)
                    if not first:
                        target(nc, dve, S, B, Edge(it, c - 1))
                    dve.wait_ge(dz_ready, 1)
                    dve.sem_inc(dz_ready, -1)
                    dve.sem_inc(B.got_free, 1)
                    TT(mv, mv, prod[:, :, :, :], ALU.add).then_inc(B.msg_ready, 1)
                    if ahead > 0:
                        make_same(nc, dve, S, B, n).then_inc(B.row_free, 1)
                        link(maximum(n))

                for c in range(3):
                    index(Edge(0, c))
                for c in range(2):
                    y = got[c][:, :, 0:C]
                    link(products(Edge(0, c)))
                    link(TT(y, prod[:, :, 0, :], prod[:, :, 1, :], ALU.add))
                    link(TT(y, y, prod[:, :, 2, :], ALU.add))
                    dve.sem_inc(y_ready, 1)
                make_same(nc, dve, S, B, Edge(0, 0)).then_inc(B.row_free, 1)
                link(maximum(Edge(0, 0)))
                body(0, 0, first=True)
                with dve.Fori(0, PASSES) as it:
                    for c in range(1, UNROLL + 1):
                        body(it, c)
                body(0, G - 3, more=False)
                body(0, G - 2, more=False, ahead=1)
                body(0, G - 1, more=False, ahead=0)
                target(nc, dve, S, B, Edge(0, G - 1))



def expert_weights(nc, ctx, S, layer, shapes, arrays):
    S.mw[layer] = [ctx.enter_context(nc.sbuf_tensor(f"mw{layer}_{i}", s, F32)) for i, s in enumerate(shapes)]
    S.mw_loads[layer] = [(t[:, :, :, :].rearrange("p e k h -> p (e k) h"), a.rearrange("e (k p) h -> p (e k) h", p=128))
                         for t, a in zip(S.mw[layer], arrays)]


def load_experts(nc, sp, S, layer):
    for to, fr in S.mw_loads[layer]:
        sp.dma_start(to, fr).then_inc(S.s_mw[layer], 16)


def program(nc, I, out):
    S = State()
    with ExitStack() as ctx:
        S.signals = Signals(nc, ctx)
        for layer in range(2):
            S.s_mw[layer] = ctx.enter_context(nc.semaphore(f"experts{layer}_in"))
        S.mw_in = {0: [(S.s_mw[0], 48)], 1: [(S.s_mw[1], 32)]}
        setup(nc, ctx, I, S)
        with ExitStack() as experts:
            expert_weights(nc, experts, S, 0, [[128, NEXP, 2, H1]] * 3, [I["eW1"], I["eW2"], I["eWo"]])
            with ExitStack() as skips:
                S.skip = skips.enter_context(nc.sbuf_tensor("skip", [P, NT, D], F32))
                first_nodes(nc, ctx, I, S)
                first_edges(nc, ctx, I, S)
                last_nodes(nc, ctx, I, S)
            mixture(nc, ctx, I, S, 0)
        with ExitStack() as experts:
            expert_weights(nc, experts, S, 1, [[128, NEXP, 2, H2], [128, NEXP, 4, D]], [I["fW1"], I["fW2"]])
            second_nodes(nc, ctx, I, S)
            second_edges(nc, ctx, I, S)
            mixture(nc, ctx, I, S, 1, out)


def planar(a, axis):
    a = np.moveaxis(np.asarray(a), axis, -1)
    v = a[..., C:].reshape(a.shape[:-1] + (C, 3))
    v = np.swapaxes(v, -1, -2).reshape(a.shape[:-1] + (3 * C,))
    return np.ascontiguousarray(np.moveaxis(np.concatenate([a[..., :C], v], axis=-1), -1, axis))


def kernel(**inputs):
    import concourse.bacc as bacc
    from concourse.bass_utils import run_bass_kernel_spmd as run

    a = {k: np.asarray(v) for k, v in inputs.items()}
    g0, g1, f0, f1 = "L0_gnn_", "L1_gnn_", "L0_ffn_", "L1_ffn_"

    def tiled(v):
        return np.swapaxes(v.reshape((ET, P) + v.shape[1:]), 0, 1)

    def columns(v):
        return v.reshape(-1, 128).T

    m4 = a[g0 + "M4"].reshape(HID, 4, C)
    arrays = {
        "x": planar(a["x"], 1),
        "src_pt": tiled(a["src"]), "dst_pt": tiled(a["dst"]), "dst_row": a["dst"].reshape(1, E),
        "ea3": tiled(a["edge_attr_3"]), "ea4": tiled(a["edge_attr_4"]), 
        "rbfT": a["edge_attr_16"].T.reshape(R, G, 2, HE).transpose(2, 0, 1, 3).reshape(2 * R, G * HE),
        "M1": a[g0 + "M1"], "M2": a[g0 + "M2"], "M3": a[g0 + "M3"],
        "M4": np.concatenate([m4[:, 0], m4[:, 2], m4[:, 1], m4[:, 3]], axis=1),
        "Wup0": a[g0 + "W_up0"], "Wup1": a[g0 + "W_up1"], "Wsc0": a[g0 + "Wsc0"], "Wsc1": a[g0 + "Wsc1"],
        "Wlin0": a[g0 + "W_lin0"], "Wlin1": a[g0 + "W_lin1"], "WB0": a[g0 + "WB0"], "WB1": a[g0 + "WB1"],
        "Wc0r": a[g0 + "Wc0"].T.reshape(1, 5 * C), "Wc1r": a[g0 + "Wc1"].T.reshape(1, 4 * C),
        "gam": np.concatenate([a[g0 + "gamma0"], a[g0 + "beta0"], a[g0 + "gamma1"]]).reshape(1, 3 * C),
        "lsc": a[g1 + "lin_scalar_w"],
        "Wr": planar(a[f0 + "Wr"], 0), "br": a[f0 + "br"].reshape(1, NEXP), "bo": planar(a[f0 + "bo"], 1),
        "bn": np.stack([np.stack([columns(a[f0 + n + s]) for s in "12"], 1) for n in ("g", "b", "be", "m", "v")], 1),
        "eW1": planar(a[f0 + "W1"], 1), "eW2": a[f0 + "W2"], "eWo": planar(a[f0 + "Wo"], 2),
        "Wg": planar(a[f1 + "Wg"], 0), "bg": a[f1 + "bg"].reshape(1, NEXP), "bias": a[f1 + "bias"].reshape(1, NEXP),
        "fW1": planar(a[f1 + "W1"], 1), "b1": columns(a[f1 + "b1"]), "fW2": planar(a[f1 + "W2"], 2),
        "b2": planar(a[f1 + "b2"], 1),
    }
    fac = {"ls0T": a[g1 + "lin_src_w0"].T, "ls1T": a[g1 + "lin_src_w1"].T,
           "w00": a[g1 + "tp1_w00"], "w11": a[g1 + "tp1_w11"], "w01": a[g1 + "tp1_w01"], "w10": a[g1 + "tp1_w10"],
           "lh0": a[g1 + "lin_hidden_w0"], "lh1": a[g1 + "lin_hidden_w1"],
           "t00": a[g1 + "tp2_w00"], "t11": a[g1 + "tp2_w11"], "t01": a[g1 + "tp2_w01"], "t10": a[g1 + "tp2_w10"]}
    nc = bacc.Bacc("TRN2", target_bir_lowering=False, num_devices=1)
    feed = {}

    def given(name, v):
        v = np.ascontiguousarray(v)
        feed["in_" + name] = v
        return nc.dram_tensor("in_" + name, v.shape, mybir.dt.from_np(v.dtype), kind="ExternalInput").ap()
    I = {name: given(name, v) for name, v in arrays.items()}
    I.update({"fac_" + name: given("fac_" + name, v) for name, v in fac.items()})
    out = nc.dram_tensor("out", (N, D), F32, kind="ExternalOutput").ap()
    program(nc, I, out)
    y = run(nc, [feed], core_ids=[0]).results[0]["out"]
    return np.concatenate([y[:, :C], np.swapaxes(y[:, C:].reshape(N, 3, C), 1, 2).reshape(N, 3 * C)], axis=1)
```

```python
from contextlib import ExitStack

import numpy as np

import concourse.bass as bass
from concourse import mybir

F32 = mybir.dt.float32
I32 = mybir.dt.int32
U32 = mybir.dt.uint32
ALU = mybir.AluOpType
ACT = mybir.ActivationFunctionType
AX = mybir.AxisListType.X

N, D, C, E = 3125, 256, 64, 50000
P = 125
NT = N // P
CT = 5
CHUNKS = NT // CT
CN = CT * P
ET = E // P
GT = 4
G = ET // GT
GE = GT * P
HE = GE // 2
R, HID = 16, 64
UNROLL = 4
PASSES = (G - 4) // UNROLL
ACC_ROWS = 26 * 128
T2 = 448
NEXP = 8
H1 = 256
H2 = 512
SPLIT = (0, 375, 625)
LN_EPS, BN_EPS = 1e-5, 1e-3
SQ3 = float(np.sqrt(3.0))
INV_TP = float(1.0 / np.sqrt(2 * C))
INV_MUL = float(1.0 / np.sqrt(C))


FACTORS = ("ls0T", "ls1T", "w00", "w11", "w01", "w10", "lh0", "lh1", "t00", "t11", "t01", "t10")


class State:
    def __init__(self):
        self.mw, self.mw_from, self.s_mw = {}, {}, {}


class Buffers:
    pass


def bc(ap, n, axis):
    v = ap.unsqueeze(axis)
    shape = list(v.shape)
    shape[axis] = n
    return v.broadcast_to(shape)


def linker(eng, sem):
    def link(ins):
        ins.then_inc(sem, 1)
        eng.wait_ge(sem, 1)
        eng.sem_inc(sem, -1)
    return link


def tell(eng, ins, own, *sems):
    ins.then_inc(own, 1)
    eng.wait_ge(own, 1)
    eng.sem_inc(own, -1)
    for s in sems:
        eng.sem_inc(s, 1)


class Signals:
    SHARED = {"dve_step", "act_step", "variance", "deviation", "h_ready", "turned", "hT_ready", "h_free",
              "gates_in_psum", "logits_ready", "exps_ready", "gates_ready", "gates_turned", "gates_T_ready",
              "bias_in_psum", "hidden_in_psum", "hidden_ready", "out_in_psum", "out_added"}

    def __init__(self, nc, ctx):
        self.nc, self.ctx, self.shared = nc, ctx, {}

    def get(self, phase, name):
        if name not in self.SHARED:
            return self.ctx.enter_context(self.nc.semaphore(f"{phase}_{name}"))
        if name not in self.shared:
            self.shared[name] = self.ctx.enter_context(self.nc.semaphore(name))
        return self.shared[name]



def zero_sums(sp, S, layer):
    for a in S.acc[layer]:
        sp.dma_start(a.rearrange("(p t) d -> p t d", t=ACC_ROWS // 128), bc(S.zero[:, :], ACC_ROWS // 128, 1)).then_inc(S.zeroed, 16)


def setup(nc, ctx, I, S):
    def sb(name, shape, dt=F32):
        return ctx.enter_context(nc.sbuf_tensor(name, shape, dt))

    def sem(name):
        return S.signals.get("su", name)

    S.x = sb("x_nodes", [P, NT, D])
    S.ident = sb("ident", [128, 128])
    S.ones = sb("ones", [P, 128])
    S.src = sb("src_idx", [P, ET], I32)
    S.dst = sb("dst_idx", [P, ET], I32)
    S.dstf = sb("dst_float", [P, ET])
    S.put = sb("scatter_idx", [P, ET], I32)
    S.sh0 = sb("edge_sh", [P, ET, 4])
    S.shn = sb("edge_unit", [P, ET, 3])
    S.q = sb("edge_q", [P, ET])
    S.wh = sb("w_hidden", [128, C])
    S.wm = sb("w_main", [128, D])
    S.lsc = sb("w_scalar", [C, C])
    S.wd = sb("w_vector", [128, 2, 128])
    S.before = sb("earlier_mask", [P, P])
    S.dump = sb("dump_row", [P, 1])
    S.zero = sb("zero", [128, D])
    S.bd = sb("up_skip", [128, 2, 2, 128])
    S.x_in, S.zeroed, S.bd_in = sem("x_in"), sem("su_acc_zeroed"), sem("bd_in")

    S.table1 = nc.dram_tensor("table1", (N, D), F32, kind="Internal").ap()
    S.table2 = nc.dram_tensor("table2", (N, T2), F32, kind="Internal").ap()
    S.acc = [[nc.dram_tensor(f"acc{l}_{i}", (ACC_ROWS, D), F32, kind="Internal").ap() for i in range(GT)]
             for l in range(2)]

    with ExitStack() as loc:
        def tb(name, shape, dt=F32):
            return loc.enter_context(nc.sbuf_tensor(name, shape, dt))

        ev = tb("edge_vec", [P, ET, 3])
        sq = tb("edge_sq", [P, ET, 3])
        nrm = tb("edge_norm", [P, ET])
        dumpi = tb("dump_int", [P, 1], I32)
        fac = tb("factors", [C, len(FACTORS), C])
        UT = tb("prod_T", [C, 4, C])
        WT = tb("full_T", [C, 4, C])
        WR = tb("scaled_T", [C, 6, C])
        WDD = tb("wd_twice", [C, 2, C])
        pz = [loc.enter_context(nc.psum_tensor(f"pz{i}", [128, 512], F32)) for i in range(8)]
        s_load, s_zero = sem("su_loaded"), sem("su_zero_ready")
        s_iota, s_link, s_ulink, s_pe, s_cp = sem("su_iota"), sem("su_dve_step"), sem("su_pool_step"), sem("su_product"), sem("su_copied")
        loads = [(S.src[:, :], I["src_pt"]), (S.dst[:, :], I["dst_pt"]), (ev[:, :, :], I["ea3"]), (S.sh0[:, :, :], I["ea4"]),
                 (S.lsc[:, :], I["lsc"])]
        loads += [(fac[:, 0:len(FACTORS), :], I["factors"])]
        F = {n: fac[:, i, :] for i, n in enumerate(FACTORS)}
        s_nrm, s_root = sem("su_norm_sq"), sem("su_norm")
        with nc.Block() as block:
            @block.scalar
            def _(act):
                act.wait_ge(s_nrm, 1)
                act.sem_inc(s_nrm, -1)
                nc.scalar.activation(nrm[:, :], nrm[:, :], ACT.Sqrt).then_inc(s_root, 1)

            @block.sync
            def _(sp):
                for to, fr in loads:
                    sp.dma_start(to, fr).then_inc(s_load, 16)
                sp.wait_ge(s_zero, 1)
                for half, kinds in enumerate(((("Wup0", "Wup1"), ("Wsc0", "Wsc1")), (("Wup1", "Wup1"), ("Wsc1", "Wsc1")))):
                    for i, (a, b) in enumerate(kinds):
                        sp.dma_start(S.bd[0:C, half, i, 0:C], I[a]).then_inc(S.bd_in, 16)
                        sp.dma_start(S.bd[C:128, half, i, C:128], I[b]).then_inc(S.bd_in, 16)
                sp.dma_start(S.x[:, :, :], I["x"].rearrange("(p t) d -> p t d", t=NT)).then_inc(S.x_in, 16)
                zero_sums(sp, S, 0)

            @block.gpsimd
            def _(pool):
                link = linker(pool, s_ulink)
                link(nc.gpsimd.memset(S.ident[:, :], 0.0))
                link(nc.gpsimd.affine_select(out=S.ident[:, :], in_=S.ident[:, :], compare_op=ALU.not_equal, fill=1.0,
                                             base=0, pattern=[[-1, 128]], channel_multiplier=1))
                link(nc.gpsimd.memset(S.before[:, :], 1.0))
                link(nc.gpsimd.affine_select(out=S.before[:, :], in_=S.before[:, :], compare_op=ALU.is_gt, fill=0.0,
                                             base=0, pattern=[[-1, P]], channel_multiplier=1))
                nc.gpsimd.iota(dumpi[:, :], pattern=[[0, 1]], base=N, channel_multiplier=1).then_inc(s_iota, 1)

            @block.vector
            def _(dve):
                link = linker(dve, s_link)
                nc.vector.memset(S.bd[:, :, :, :], 0.0)
                nc.vector.memset(S.zero[:, :], 0.0).then_inc(s_zero, 1)
                nc.vector.memset(S.ones[:, :], 1.0)
                nc.vector.memset(S.wm[0:C, 2 * C:3 * C], 0.0)
                nc.vector.memset(S.wd[:, :, :], 0.0)
                link(nc.vector.memset(WR[:, :, :], 0.0))
                dve.wait_ge(s_iota, 1)
                nc.vector.tensor_copy(S.dump[:, :], dumpi[:, :])
                dve.wait_ge(s_load, 16 * len(loads))
                nc.vector.tensor_copy(S.dstf[:, :], S.dst[:, :])
                link(nc.vector.tensor_tensor(sq[:, :, :], ev[:, :, :], ev[:, :, :], ALU.mult))
                link(nc.vector.tensor_reduce(nrm[:, :], sq[:, :, :], AX, ALU.add))
                dve.sem_inc(s_nrm, 1)
                dve.wait_ge(s_root, 1)
                dve.sem_inc(s_root, -1)
                link(nc.vector.tensor_scalar(nrm[:, :], nrm[:, :], 1e-12, None, ALU.add))
                link(nc.vector.reciprocal(nrm[:, :], nrm[:, :]))
                link(nc.vector.tensor_scalar(nrm[:, :], nrm[:, :], SQ3, None, ALU.mult))
                link(nc.vector.tensor_tensor(S.shn[:, :, :], ev[:, :, :], bc(nrm[:, :], 3, 2), ALU.mult))
                link(nc.vector.tensor_tensor(sq[:, :, :], S.shn[:, :, :], S.shn[:, :, :], ALU.mult))
                link(nc.vector.tensor_reduce(S.q[:, :], sq[:, :, :], AX, ALU.add))
                k = INV_MUL * INV_TP * INV_MUL
                dve.wait_ge(s_pe, 1)
                for i, f in enumerate((k / SQ3, k, k, k)):
                    ins = nc.vector.tensor_scalar(UT[:, i, :], pz[0][0:C, i * C:(i + 1) * C], f, None, ALU.mult)
                ins.then_inc(s_cp, 1)
                dve.wait_ge(s_pe, 2)
                nc.vector.tensor_copy(S.wh[:, :], pz[1][:, 0:C])
                link(nc.vector.tensor_copy(WT[:, :, :].rearrange("p a b -> p (a b)"), pz[2][0:C, 0:4 * C]))
                nc.vector.tensor_scalar(WR[:, 0, :], WT[:, 2, :], 1.0 / SQ3, None, ALU.mult)
                nc.vector.tensor_copy(WR[:, 3, :], WT[:, 3, :])
                nc.vector.tensor_scalar(WR[:, 5, :], WT[:, 3, :], 1.0 / SQ3, None, ALU.mult)
                nc.vector.tensor_copy(WDD[:, 0, :], WT[:, 2, :])
                nc.vector.tensor_copy(WDD[:, 1, :], WT[:, 2, :]).then_inc(s_cp, 1)
                dve.wait_ge(s_pe, 3)
                nc.vector.tensor_scalar(S.wm[:, 0:3 * C], pz[3][:, 0:3 * C], INV_TP, None, ALU.mult)
                nc.vector.tensor_scalar(S.wm[:, 3 * C:D], pz[5][:, 0:C], 0.01 * INV_MUL, None, ALU.mult)
                for h in range(2):
                    rows = slice(C * h, C * (h + 1))
                    nc.vector.tensor_scalar(S.wd[rows, 1, rows], pz[4][rows, 0:C], INV_TP, None, ALU.mult)
                nc.vector.tensor_scalar(S.wd[C:128, 0, 0:C], pz[4][C:128, 0:C], INV_TP, None, ALU.mult)
                nc.vector.tensor_scalar(S.lsc[:, :], S.lsc[:, :], 0.99 * INV_MUL, None, ALU.mult).then_inc(s_cp, 1)
                dve.wait_ge(s_cp, 3)

            @block.tensor
            def _(pe):
                pe.wait_ge(s_load, 16 * len(loads))
                for i, (a, b) in enumerate((("w11", "ls1T"), ("w00", "ls0T"), ("w10", "ls1T"), ("w01", "ls0T"))):
                    ins = nc.tensor.matmul(pz[0][0:C, i * C:(i + 1) * C], F[a], F[b], start=True, stop=True)
                ins.then_inc(s_pe, 1)
                pe.wait_ge(s_cp, 1)
                nc.tensor.matmul(pz[1][:, 0:C], UT[:, 0:2, :].rearrange("p a b -> p (a b)"), F["lh0"], start=True, stop=True)
                nc.tensor.matmul(pz[2][0:C, 0:2 * C], F["lh0"], UT[:, 0:2, :].rearrange("p a b -> p (a b)"),
                                 start=True, stop=True)
                nc.tensor.matmul(pz[2][0:C, 2 * C:4 * C], F["lh1"], UT[:, 2:4, :].rearrange("p a b -> p (a b)"),
                                 start=True, stop=True).then_inc(s_pe, 1)
                pe.wait_ge(s_cp, 2)
                hT = WT[:, 0:2, :].rearrange("p a b -> p (a b)")

                def pair(i):
                    return WR[:, i:i + 2, :].rearrange("p a b -> p (a b)")
                nc.tensor.matmul(pz[3][:, 0:C], hT, F["t00"], start=True, stop=False)
                nc.tensor.matmul(pz[3][:, 0:C], pair(0), F["t11"], start=False, stop=True)
                nc.tensor.matmul(pz[3][:, C:2 * C], hT, F["t01"], start=True, stop=False)
                nc.tensor.matmul(pz[3][:, C:2 * C], pair(2), F["t10"], start=False, stop=True)
                nc.tensor.matmul(pz[3][:, 2 * C:3 * C], pair(4), F["t11"], start=True, stop=True)
                nc.tensor.matmul(pz[5][:, 0:C], hT, S.lsc[:, :], start=True, stop=True)
                nc.tensor.matmul(pz[4][:, 0:C], WDD[:, :, :].rearrange("p a b -> p (a b)"), F["t10"],
                                 start=True, stop=True).then_inc(s_pe, 1)



def statistics(nc, link, x, st):
    for j in range(CT):
        ins = nc.vector.bn_stats(st[:, j, 0:6], x[:, j, :])
    link(ins)
    for j in range(CT):
        ins = nc.vector.bn_aggr(st[:, j, 6:8], st[:, j, 0:6])
    link(ins)
    return nc.vector.tensor_scalar(st[:, :, 8:9], st[:, :, 7:8], LN_EPS, None, ALU.add)


def normed(nc, link, x, h, st):
    link(nc.vector.reciprocal(st[:, :, 8:9], st[:, :, 8:9]))
    for j in range(CT):
        ins = nc.vector.tensor_scalar(h[:, j, :], x[:, j, :], st[:, j, 6:7], st[:, j, 8:9], ALU.subtract, ALU.mult)
    return ins


def normalise(nc, dve, link, x, h, st, s_var, s_std):
    statistics(nc, link, x, st).then_inc(s_var, 1)
    dve.wait_ge(s_std, 1)
    dve.sem_inc(s_std, -1)
    return normed(nc, link, x, h, st)


def root(nc, act, st, s_var, s_std):
    act.wait_ge(s_var, 1)
    act.sem_inc(s_var, -1)
    nc.scalar.activation(st[:, :, 8:9], st[:, :, 8:9], ACT.Sqrt).then_inc(s_std, 1)


def turn(nc, h, ident, pst):
    for i in range(2 * CT):
        j, k = i // 2, i % 2
        ins = nc.tensor.transpose(pst[:, i // 4, (i % 4) * P:(i % 4 + 1) * P], h[:, j, k * 128:(k + 1) * 128],
                                  ident[0:P, 0:P])
    return ins


def turned(nc, pst, hT):
    for i in range(3):
        n = min(4, 2 * CT - 4 * i) // 2
        o = hT[:, :, 2 * i * P:(2 * i + n) * P].rearrange("p k (j e) -> p j k e", j=n)
        ins = nc.scalar.copy(o, pst[:, i, 0:2 * n * P].rearrange("p (j k e) -> p j k e", j=n, k=2))
    return ins


def linear(nc, hT, w0, w1, pso):
    for j in range(CT):
        for k, w in enumerate((w0, w1)):
            o = (j % 2) * 256 + k * 128
            ins = nc.tensor.matmul(pso[:, j // 2, o:o + 128], hT[:, k, j * P:(j + 1) * P], w, start=True, stop=True)
    return ins


def banks(pso, b):
    n = min(2, CT - 2 * b)
    return pso[:, b, 0:256 * n].rearrange("p (n d) -> p n d", d=256), slice(2 * b, 2 * b + n)



def first_nodes(nc, ctx, I, S):
    def sem(name):
        return S.signals.get("fn", name)

    with ExitStack() as loc:
        def tb(name, shape, dt=F32):
            return loc.enter_context(nc.sbuf_tensor(name, shape, dt))
        h, st, hT = tb("fn_h", [P, CT, D]), tb("fn_st", [P, CT, 9]), tb("fn_hT", [128, 2, CN])
        up = tb("fn_up", [P, CT, D])
        bd = S.bd
        pst = loc.enter_context(nc.psum_tensor("fn_pst", [128, 3, 512], F32))
        pso = loc.enter_context(nc.psum_tensor("fn_pso", [P, CT, 512], F32))
        s_link, s_h, s_t, s_hT = sem("dve_step"), sem("h_ready"), sem("turned"), sem("hT_ready")
        s_hfree, s_own = sem("h_free"), sem("act_step")
        s_var, s_std = sem("variance"), sem("deviation")
        s_o, s_oc, s_upc, s_upd, s_upg = sem("out_in_psum"), sem("out_copied"), sem("up_copied"), sem("table"), sem("table_ok")
        with nc.Block() as block:
            @block.sync
            def _(sp):
                rows = S.table1.rearrange("(p t) d -> p t d", t=NT)
                with sp.Fori(0, CHUNKS) as c:
                    sp.wait_ge(s_upc, 1)
                    sp.sem_inc(s_upc, -1)
                    sp.dma_start(rows[:, bass.ds(c * CT, CT), :], up[:, :, :]).then_inc(s_upd, 16)
                    sp.wait_ge(s_upd, 16 * c + 16)
                    sp.sem_inc(s_upg, 1)
                sp.wait_ge(S.zeroed, 16 * GT)

            @block.vector
            def _(dve):
                link = linker(dve, s_link)
                dve.wait_ge(S.x_in, 16)
                with dve.Fori(0, CHUNKS) as c:
                    normalise(nc, dve, link, S.x[:, bass.ds(c * CT, CT), :], h, st, s_var, s_std).then_inc(s_h, 1)
                    dve.wait_ge(s_hfree, 1)
                    dve.sem_inc(s_hfree, -1)

            @block.tensor
            def _(pe):
                pe.wait_ge(S.bd_in, 16 * 8)
                def turn_in():
                    pe.wait_ge(s_h, 1)
                    pe.sem_inc(s_h, -1)
                    turn(nc, h, S.ident, pst).then_inc(s_t, 1)

                def out():
                    pe.wait_ge(s_hT, 1)
                    pe.sem_inc(s_hT, -1)
                    pe.wait_ge(s_oc, 1)
                    pe.sem_inc(s_oc, -1)
                    for j in range(CT):
                        for k in range(2):
                            ins = nc.tensor.matmul(pso[:, j, k * 256:(k + 1) * 256], hT[:, k, j * P:(j + 1) * P],
                                                   bd[:, k, :, :].rearrange("p a b -> p (a b)"), start=True, stop=True)
                    ins.then_inc(s_o, 1)
                pe.sem_inc(s_oc, 1)
                turn_in()
                with pe.Fori(0, CHUNKS - 1) as c:
                    out()
                    turn_in()
                out()

            @block.scalar
            def _(act):
                act.sem_inc(s_upg, 1)

                def turned_in():
                    act.wait_ge(s_t, 1)
                    act.sem_inc(s_t, -1)
                    act.sem_inc(s_hfree, 1)
                    turned(nc, pst, hT).then_inc(s_hT, 1)

                def out(c):
                    act.wait_ge(s_o, 1)
                    act.sem_inc(s_o, -1)
                    act.wait_ge(s_upg, 1)
                    act.sem_inc(s_upg, -1)
                    v = pso[:, :, :].rearrange("p j (k i e) -> p j k i e", k=2, i=2)
                    for j in range(CT):
                        nc.scalar.copy(S.skip[:, bass.ds(c * CT + j, 1), :].rearrange("p a (k e) -> p (a k) e", k=2), v[:, j, :, 1, :])
                        ins = nc.scalar.copy(up[:, j, :].rearrange("p (k e) -> p k e", k=2), v[:, j, :, 0, :])
                    tell(act, ins, s_own, s_oc, s_upc)
                root(nc, act, st, s_var, s_std)
                turned_in()
                with act.Fori(0, CHUNKS - 1) as c:
                    root(nc, act, st, s_var, s_std)
                    out(c)
                    turned_in()
                out(CHUNKS - 1)
                act.wait_ge(s_oc, 1)
                act.sem_inc(s_oc, -1)



class Edge:
    def __init__(self, it, c):
        self.g = it * UNROLL + c
        self.slot = c % 2
        self.use = it * (UNROLL // 2) + (c // 2 + 1)
        self.deep = c % UNROLL
        self.deep_use = it + (c // UNROLL + 1)


def edge_buffers(nc, loc, S, name):
    def tb(n, shape, dt=F32):
        return loc.enter_context(nc.sbuf_tensor(f"{name}_{n}", shape, dt))

    def sem(n):
        return S.signals.get(name, n)
    B = Buffers()
    B.take_i = [tb(f"gather_idx{s}", [P, GT], I32) for s in range(UNROLL)]
    B.put_i = [tb(f"scatter_idx{s}", [P, GT], I32) for s in range(2)]
    B.row = [tb(f"dst_row{s}", [128, GE], I32) for s in range(2)]
    B.same = [tb(f"same{s}", [P, GT, P]) for s in range(UNROLL)]
    B.msg = [tb(f"msg{s}", [P, GT, D]) for s in range(UNROLL)]
    B.sum = [tb(f"sum{s}", [P, GT, D]) for s in range(2)]
    B.got = [sem(f"gathered{s}") for s in range(UNROLL)]
    B.put = [sem(f"scattered{s}") for s in range(2)]
    B.row_in = [sem(f"dst_row_in{s}") for s in range(2)]
    B.row_free = sem("dst_row_free")
    B.idx_ready = sem("gather_index_ready")
    B.got_free = sem("gathered_free")
    B.msg_ready = sem("messages_ready")
    B.msg_free = sem("messages_used")
    B.sum_ps = sem("sums_in_psum")
    B.sum_ps_free = sem("sums_psum_free")
    B.sum_ready = sem("sums_ready")
    B.sum_free = sem("sums_scattered")
    B.put_free = sem("scatter_index_free")
    B.put_ready = sem("scatter_index_ready")
    B.own = sem("act_step")
    B.passed = sem("dma_waits_passed")
    return B


def edge_pool(nc, pool, B, table, got, acc):
    def gather(e):
        pool.wait_ge(B.idx_ready, 1)
        pool.sem_inc(B.idx_ready, -1)
        pool.wait_ge(B.got_free, 1)
        pool.sem_inc(B.got_free, -1)
        for j in range(GT):
            pool.indirect_dma_start(got(e.deep, j), None, table,
                                    bass.IndirectOffsetOnAxis(B.take_i[e.deep][:, j:j + 1], 0)).then_inc(B.got[e.deep], 16)

    def scatter(e, before):
        if before is not None:
            pool.wait_ge(B.put[before.slot], 16 * GT * before.use)
            pool.sem_inc(B.sum_free, 1)
            pool.sem_inc(B.put_free, 1)
        pool.wait_ge(B.put_ready, 1)
        pool.sem_inc(B.put_ready, -1)
        pool.wait_ge(B.sum_ready, 1)
        pool.sem_inc(B.sum_ready, -1)
        for j in range(GT):
            pool.indirect_dma_start(acc[j], bass.IndirectOffsetOnAxis(B.put_i[e.slot][:, j:j + 1], 0),
                                    B.sum[e.slot][:, j, :], None, compute_op=ALU.add).then_inc(B.put[e.slot], 16)
    for c in range(UNROLL):
        gather(Edge(0, c))

    def body(it, c):
        gather(Edge(it, c + 3))
        if c > 1:
            scatter(Edge(it, c - 2), Edge(it, c - 3) if c > 2 else None)
    for c in range(1, UNROLL + 1):
        body(0, c)
    with pool.Fori(0, PASSES - 1) as it:
        for c in range(1, UNROLL + 1):
            body(it, UNROLL + c)
    for c in range(G - 5, G):
        scatter(Edge(0, c), Edge(0, c - 1))
    for s in range(2):
        pool.wait_ge(B.put[s], 16 * GT * (G // 2))


def load_row(sp, I, B, e):
    sp.wait_ge(B.row_free, 1)
    sp.sem_inc(B.row_free, -1)
    sp.dma_start(B.row[e.slot][:, :], I["dst_row"][:, bass.ds(e.g * GE, GE)].broadcast_to([128, GE])).then_inc(
        B.row_in[e.slot], 16)


def load_expert(sp, S, layer, e):
    for to, fr in zip(S.mw[layer], S.mw_from[layer]):
        sp.dma_start(to[:, bass.ds(e, 1), :, :].rearrange("p a k h -> p (a k) h"),
                     fr[:, bass.ds(e, 1), :, :].rearrange("p a k h -> p (a k) h")).then_inc(S.s_mw[layer], 16)


def make_same(nc, dve, S, B, e):
    dve.wait_ge(B.msg_free, 1)
    dve.sem_inc(B.msg_free, -1)
    dve.wait_ge(B.row_in[e.slot], 16 * e.use)
    dve.sem_inc(B.passed, 1)
    return nc.vector.tensor_tensor(B.same[e.deep][:, :, :],
                                   B.row[e.slot][0:P, :].rearrange("p (t f) -> p t f", t=GT),
                                   bc(S.dstf[:, bass.ds(e.g * GT, GT)], P, 2), ALU.is_equal)


def target(nc, dve, S, B, e):
    dve.wait_ge(B.put_free, 1)
    dve.sem_inc(B.put_free, -1)
    nc.vector.tensor_copy(B.put_i[e.slot][:, :], S.put[:, bass.ds(e.g * GT, GT)]).then_inc(B.put_ready, 1)


def sum_matmuls(nc, pe, B, e, pss):
    pe.wait_ge(B.msg_ready, 1)
    pe.sem_inc(B.msg_ready, -1)
    pe.wait_ge(B.sum_ps_free, 1)
    pe.sem_inc(B.sum_ps_free, -1)
    for j in range(GT):
        ins = nc.tensor.matmul(pss[:, j // 2, (j % 2) * D:(j % 2 + 1) * D], B.same[e.deep][:, j, :],
                               B.msg[e.deep][:, j, :], start=True, stop=True)
    ins.then_inc(B.sum_ps, 1)


def sums_done(act, B):
    act.wait_ge(B.sum_ps, 1)
    act.sem_inc(B.sum_ps, -1)
    act.sem_inc(B.msg_free, 1)


def sum_copy(nc, act, B, e, pss):
    act.wait_ge(B.sum_free, 1)
    act.sem_inc(B.sum_free, -1)
    for b in range(2):
        ins = nc.scalar.copy(B.sum[e.slot][:, 2 * b:2 * b + 2, :],
                             pss[:, b, :].rearrange("p (n d) -> p n d", d=D))
    tell(act, ins, B.own, B.sum_ready, B.sum_ps_free)


def first_edges(nc, ctx, I, S):
    with ExitStack() as loc:
        def tb(name, shape, dt=F32):
            return loc.enter_context(nc.sbuf_tensor(f"e1_{name}", shape, dt))

        def sem(n):
            return S.signals.get("e1", n)
        B = edge_buffers(nc, loc, S, "e1")
        got = [tb(f"got{s}", [P, GT, D]) for s in range(UNROLL)]
        rbf = [tb(f"rbf{s}", [2 * R, HE]) for s in range(2)]
        r = [tb(f"r{i}", [2 * HID, HE]) for i in range(3)]
        w = [tb(f"tpw{s}", [P, GT, D]) for s in range(2)]
        prod = tb("prod", [P, GT, 3, C])
        ash = tb("ash", [P, GT, 3, C])
        q = tb("q", [P, GT, C])
        q3 = tb("q3", [P, GT, C])
        a = tb("a", [P, GT, C])
        count = tb("count", [P, GT])
        repeat = tb("repeat", [P, GT, P])
        junk = tb("junk", [P, GT, P])
        putf = tb("putf", [P, GT])
        M1, M2, M3 = tb("M1", [2 * R, 2, HID]), tb("M2", [2 * HID, 2, HID]), tb("M3", [2 * HID, 2, HID])
        M4 = tb("M4", [2 * HID, D])
        ps_m = [loc.enter_context(nc.psum_tensor(f"e1_psm{i}", [2 * HID, 512], F32)) for i in range(2)]
        ps_w = loc.enter_context(nc.psum_tensor("e1_psw", [P, 2, 512], F32))
        pss = loc.enter_context(nc.psum_tensor("e1_pss", [P, 2, 512], F32))
        s_w, rbf_in = sem("weights"), [sem(f"rbf_in{s}") for s in range(2)]
        rbf_free, s_m, s_r, s_wp, wp_free, w_ready, w_free = (sem(n) for n in (
            "rbf_free", "hidden_in_psum", "hidden_ready", "tpw_in_psum", "tpw_psum_free", "tpw_ready", "tpw_free"))
        s_link, s_zeroed = sem("dve_step"), sem("blocks_zeroed")
        repeat_ready, count_ready = sem("repeats_ready"), sem("counts_ready")

        def rbf_load(sp, e):
            sp.wait_ge(rbf_free, 1)
            sp.sem_inc(rbf_free, -1)
            sp.dma_start(rbf[e.slot][:, :], I["rbfT"][:, bass.ds(e.g * HE, HE)]).then_inc(rbf_in[e.slot], 16)

        with nc.Block() as block:
            @block.sync
            def _(sp):
                sp.wait_ge(s_zeroed, 1)
                for h in range(2):
                    for to, n in ((M1, "M1"), (M2, "M2"), (M3, "M3")):
                        k = to.shape[0] // 2
                        sp.dma_start(to[h * k:(h + 1) * k, h, :], I[n]).then_inc(s_w, 16)
                    sp.dma_start(M4[h * HID:(h + 1) * HID, :], I["M4"]).then_inc(s_w, 16)
                with sp.Fori(0, NEXP) as it:
                    for c in range(UNROLL):
                        rbf_load(sp, Edge(it, c))
                        load_row(sp, I, B, Edge(it, c))
                    load_expert(sp, S, 0, it)
                with sp.Fori(0, G // UNROLL - NEXP) as it:
                    for c in range(UNROLL):
                        rbf_load(sp, Edge(it, NEXP * UNROLL + c))
                        load_row(sp, I, B, Edge(it, NEXP * UNROLL + c))

            @block.gpsimd
            def _(pool):
                edge_pool(nc, pool, B, S.table1, lambda s, j: got[s][:, j, :], S.acc[0])

            @block.tensor
            def _(pe):
                pe.sem_inc(rbf_free, 2)
                pe.sem_inc(B.msg_free, UNROLL)
                pe.wait_ge(s_w, 16 * 8)

                def mlp1(e):
                    pe.wait_ge(rbf_in[e.slot], 16 * e.use)
                    pe.sem_inc(B.passed, 1)
                    nc.tensor.matmul(ps_m[0][:, 0:HE], M1[:, :, :].rearrange("p a b -> p (a b)"), rbf[e.slot][:, :], start=True, stop=True).then_inc(s_m, 1)

                def mlp(w, i):
                    pe.wait_ge(s_r, 1)
                    pe.sem_inc(s_r, -1)
                    nc.tensor.matmul(ps_m[1][:, 0:HE], w[:, :, :].rearrange("p a b -> p (a b)"), r[i][:, :], start=True, stop=True).then_inc(s_m, 1)

                def tpw(e):
                    pe.wait_ge(s_r, 1)
                    pe.sem_inc(s_r, -1)
                    pe.wait_ge(wp_free, 1)
                    pe.sem_inc(wp_free, -1)
                    for j in range(GT):
                        half = slice(j // 2 * HID, (j // 2 + 1) * HID)
                        ins = nc.tensor.matmul(ps_w[:, j // 2, (j % 2) * D:(j % 2 + 1) * D],
                                               r[2][half, (j % 2) * P:(j % 2 + 1) * P], M4[half, :], start=True, stop=True)
                    ins.then_inc(s_wp, 1)

                def body(it, c, sums=True):
                    mlp1(Edge(it, c + 1))
                    tpw(Edge(it, c))
                    mlp(M2, 0)
                    if sums:
                        sum_matmuls(nc, pe, B, Edge(it, c - 2), pss)
                    mlp(M3, 1)
                mlp1(Edge(0, 0))
                mlp(M2, 0)
                mlp(M3, 1)
                body(0, 0, False)
                body(0, 1, False)
                with pe.Fori(0, PASSES) as it:
                    for c in range(2, UNROLL + 2):
                        body(it, c)
                body(0, G - 2)
                tpw(Edge(0, G - 1))
                for c in range(G - 3, G):
                    sum_matmuls(nc, pe, B, Edge(0, c), pss)

            @block.scalar
            def _(act):
                act.sem_inc(B.sum_free, 2)
                act.sem_inc(wp_free, 1)
                act.sem_inc(B.sum_ps_free, 1)

                def silu(i):
                    act.wait_ge(s_m, 1)
                    act.sem_inc(s_m, -1)
                    nc.scalar.activation(r[i][:, :], ps_m[min(i, 1)][:, 0:HE], ACT.Silu).then_inc(s_r, 1)
                    if i == 0:
                        act.sem_inc(rbf_free, 1)

                def tpw(e):
                    act.wait_ge(s_wp, 1)
                    act.sem_inc(s_wp, -1)
                    act.wait_ge(w_free, 1)
                    act.sem_inc(w_free, -1)
                    for j in range(GT):
                        v = ps_w[:, j // 2, (j % 2) * D:(j % 2 + 1) * D]
                        nc.scalar.activation(w[e.slot][:, j, 0:2 * C], v[:, 0:2 * C], ACT.Copy,
                                             scale=S.sh0[:, bass.ds(e.g * GT + j, 1), 0:1].rearrange("p a b -> p (a b)"))
                    for b in range(2):
                        v = ps_w[:, b, :].rearrange("p (n d) -> p n d", d=D)
                        ins = nc.scalar.copy(w[e.slot][:, 2 * b:2 * b + 2, 2 * C:D], v[:, :, 2 * C:D])
                    tell(act, ins, B.own, w_ready, wp_free)

                def counts():
                    act.wait_ge(repeat_ready, 1)
                    act.sem_inc(repeat_ready, -1)
                    for j in range(GT):
                        ins = nc.scalar.activation(junk[:, j, :], repeat[:, j, :], ACT.Copy, accum_out=count[:, j:j + 1])
                    ins.then_inc(count_ready, 1)

                def sums(e):
                    sums_done(act, B)
                    sum_copy(nc, act, B, e, pss)

                def body(it, c, do_sums=True):
                    silu(0)
                    tpw(Edge(it, c))
                    counts()
                    silu(1)
                    if do_sums:
                        sums(Edge(it, c - 2))
                    silu(2)
                silu(0)
                silu(1)
                silu(2)
                body(0, 0, False)
                body(0, 1, False)
                with act.Fori(0, PASSES) as it:
                    for c in range(2, UNROLL + 2):
                        body(it, c)
                body(0, G - 2)
                tpw(Edge(0, G - 1))
                counts()
                for c in range(G - 3, G):
                    sums(Edge(0, c))

            @block.vector
            def _(dve):
                link = linker(dve, s_link)
                nc.vector.memset(M1[:, :, :], 0.0)
                nc.vector.memset(M2[:, :, :], 0.0)
                link(nc.vector.memset(M3[:, :, :], 0.0))
                dve.sem_inc(s_zeroed, 1)
                dve.sem_inc(B.row_free, 2)
                dve.sem_inc(B.got_free, UNROLL)
                dve.sem_inc(B.put_free, 2)
                dve.sem_inc(w_free, 2)

                def index(e):
                    nc.vector.tensor_copy(B.take_i[e.deep][:, :], S.src[:, bass.ds(e.g * GT, GT)]).then_inc(B.idx_ready, 1)

                def body(it, c, more=True, first=False, same=True):
                    TT = nc.vector.tensor_tensor
                    e, n = Edge(it, c), Edge(it, c + 1)
                    x, m, v = got[e.deep], B.msg[e.deep], w[e.slot]
                    xv = x[:, :, C:D].rearrange("p t (k c) -> p t k c", k=3)
                    mv = m[:, :, C:D].rearrange("p t (k c) -> p t k c", k=3)
                    dst = S.dstf[:, bass.ds(e.g * GT, GT)]
                    if more:
                        index(Edge(it, c + 3))
                    dve.wait_ge(B.got[e.deep], 16 * GT * e.deep_use)
                    dve.sem_inc(B.passed, 1)
                    TT(prod[:, :, :, :], xv, bc(S.sh0[:, bass.ds(e.g * GT, GT), 1:4], C, 3), ALU.mult)
                    dve.wait_ge(w_ready, 1)
                    dve.sem_inc(w_ready, -1)
                    link(TT(m[:, :, 0:C], x[:, :, 0:C], v[:, :, 0:C], ALU.mult))
                    TT(q[:, :, :], prod[:, :, 0, :], prod[:, :, 1, :], ALU.add)
                    TT(a[:, :, :], x[:, :, 0:C], v[:, :, 2 * C:3 * C], ALU.mult)
                    dve.wait_ge(count_ready, 1)
                    dve.sem_inc(count_ready, -1)
                    nc.vector.scalar_tensor_tensor(out=putf[:, :], in0=count[:, :], scalar=0.5, in1=putf[:, :],
                                                   op0=ALU.is_gt, op1=ALU.mult)
                    link(TT(mv, xv, bc(v[:, :, C:2 * C], 3, 2), ALU.mult))
                    dve.sem_inc(B.got_free, 1)
                    TT(S.put[:, bass.ds(e.g * GT, GT)], putf[:, :], dst, ALU.add)
                    ins = TT(q[:, :, :], q[:, :, :], prod[:, :, 2, :], ALU.add)
                    if same:
                        ins = make_same(nc, dve, S, B, n)
                    link(ins)
                    if same:
                        dve.sem_inc(B.row_free, 1)
                        repeats(n)
                    nc.vector.scalar_tensor_tensor(out=q3[:, :, :], in0=q[:, :, :], scalar=1.0 / SQ3, in1=v[:, :, 3 * C:D],
                                                   op0=ALU.mult, op1=ALU.mult)
                    link(TT(ash[:, :, :, :], bc(a[:, :, :], 3, 2), bc(S.sh0[:, bass.ds(e.g * GT, GT), 1:4], C, 3), ALU.mult))
                    dve.sem_inc(w_free, 1)
                    if not first:
                        target(nc, dve, S, B, Edge(it, c - 1))
                    TT(m[:, :, 0:C], m[:, :, 0:C], q3[:, :, :], ALU.add)
                    TT(mv, mv, ash[:, :, :, :], ALU.add).then_inc(B.msg_ready, 1)

                def repeats(e):
                    nc.vector.tensor_scalar(putf[:, :], S.dstf[:, bass.ds(e.g * GT, GT)], S.dump[:, 0:1], -1.0,
                                            ALU.subtract, ALU.mult)
                    nc.vector.tensor_tensor(repeat[:, :, :], B.same[e.deep][:, :, :], bc(S.before[:, :], GT, 1),
                                            ALU.mult).then_inc(repeat_ready, 1)

                for c in range(3):
                    index(Edge(0, c))
                link(make_same(nc, dve, S, B, Edge(0, 0)))
                dve.sem_inc(B.row_free, 1)
                repeats(Edge(0, 0))
                body(0, 0, first=True)
                with dve.Fori(0, PASSES) as it:
                    for c in range(1, UNROLL + 1):
                        body(it, c)
                body(0, G - 3, more=False)
                body(0, G - 2, more=False)
                body(0, G - 1, more=False, same=False)
                target(nc, dve, S, B, Edge(0, G - 1))



def load_sums(sp, acc, to, s_in, c):
    for i in range(GT):
        rows = acc[i][0:N, :].rearrange("(p t) d -> p t d", t=NT)
        sp.dma_start(to[:, i, :, :], rows[:, bass.ds(c * CT, CT), :]).then_inc(s_in, 16)


def last_nodes(nc, ctx, I, S):
    def sem(name):
        return S.signals.get("ln", name)

    with ExitStack() as loc:
        def tb(name, shape, dt=F32):
            return loc.enter_context(nc.sbuf_tensor("ln_" + name, shape, dt))
        room = tb("acc", [P, 2 * GT * CT, D])
        a4 = [room[:, i * GT * CT:(i + 1) * GT * CT, :].rearrange("p (g t) d -> p g t d", t=CT) for i in range(2)]
        big = room[:, 0:NT, :]
        h = tb("sum", [P, CT, D])
        hT = [tb(f"hT{i}", [128, 2, CN]) for i in range(2)]
        A, Bm, sq = tb("A", [P, CT, D]), tb("B", [P, CT, D]), tb("sq", [P, CT, 3, C])
        vv, a2, t1, t2, t3 = (tb(n, [P, CT, C]) for n in ("vv", "a2", "t1", "t2", "t3"))
        bd = tb("bd", [128, 4, 128])
        wc0, wc1 = tb("wc0", [P, 5, C]), tb("wc1", [P, 4, C])
        mu = tb("mu", [P, C])
        var = tb("var", [P, 2, C])
        fac, gam = S.fac, S.gam
        pst = loc.enter_context(nc.psum_tensor("ln_pst", [128, 3, 512], F32))
        pso = loc.enter_context(nc.psum_tensor("ln_pso", [P, 3, 512], F32))
        pstat = loc.enter_context(nc.psum_tensor("ln_pstat", [128, 2, 512], F32))
        s_in = [sem(f"acc_in{i}") for i in range(2)]
        (s_bz, s_w, s_a4free, s_h, s_t, s_hT, s_A, s_Ac, s_B, s_t2, s_o, s_od, s_link, s_st, s_sq, s_var, s_std, s_cent,
         s_pass) = (sem(n) for n in (
             "bd_zero", "weights", "acc_free", "sum_ready", "turned", "hT_ready", "A_in_psum", "A_ready", "B_ready",
             "B_turned", "out_in_psum", "out_used", "dve_step", "stat_in_psum", "squares_ready", "variance", "deviation",
             "centred", "dma_waits_passed"))
        s_sqv, s_all = sem("vector_squares_ready"), sem("all_added")
        with nc.Block() as block:
            @block.sync
            def _(sp):
                load_sums(sp, S.acc[0], a4[0], s_in[0], 0)
                load_sums(sp, S.acc[0], a4[1], s_in[1], 1)
                for to, fr in ((wc0, I["Wc0r"]), (wc1, I["Wc1r"]), (gam, I["gam"])):
                    sp.dma_start(to[:, :, :].rearrange("p a b -> p (a b)"), fr.broadcast_to([P, fr.shape[1]])).then_inc(s_w, 16)
                sp.wait_ge(s_bz, 1)
                sp.sem_inc(s_bz, -1)
                for i, (a, b) in enumerate(((I["Wlin0"], I["Wlin1"]), (I["Wlin1"], I["Wlin1"]), (I["WB0"], I["WB1"]), (I["WB1"], I["WB1"]))):
                    sp.dma_start(bd[0:C, i, 0:C], a).then_inc(s_w, 16)
                    sp.dma_start(bd[C:128, i, C:128], b).then_inc(s_w, 16)
                for c in range(2, CHUNKS):
                    sp.wait_ge(s_a4free, 1)
                    sp.sem_inc(s_a4free, -1)
                    load_sums(sp, S.acc[0], a4[c % 2], s_in[c % 2], c)

            @block.vector
            def _(dve):
                link = linker(dve, s_link)
                nc.vector.memset(bd[:, :, :], 0.0).then_inc(s_bz, 1)
                dve.wait_ge(s_w, 16 * 11)
                TT, TS = nc.vector.tensor_tensor, nc.vector.tensor_scalar

                def w(t, i):
                    return bc(t[:, i, :], CT, 1)

                def sums(it, slot, freed=True):
                    a = a4[slot]
                    dve.wait_ge(s_in[slot], 16 * GT * it + 16 * GT)
                    dve.sem_inc(s_pass, 1)
                    TT(a[:, 0, :, :], a[:, 0, :, :], a[:, 1, :, :], ALU.add)
                    link(TT(a[:, 2, :, :], a[:, 2, :, :], a[:, 3, :, :], ALU.add))
                    link(TT(h[:, :, :], a[:, 0, :, :], a[:, 2, :, :], ALU.add))
                    if freed:
                        dve.sem_inc(s_a4free, 1)
                    dve.sem_inc(s_h, 1)

                def basis():
                    dve.wait_ge(s_Ac, 1)
                    dve.sem_inc(s_Ac, -1)
                    A0, A1 = A[:, :, 0:C], A[:, :, C:D].rearrange("p t (k c) -> p t k c", k=3)
                    TT(a2[:, :, :], A0, A0, ALU.mult)
                    link(TT(sq[:, :, :, :], A1, A1, ALU.mult))
                    link(TT(vv[:, :, :], sq[:, :, 0, :], sq[:, :, 1, :], ALU.add))
                    TT(t1[:, :, :], A0, w(wc0, 3), ALU.mult)
                    link(TT(vv[:, :, :], vv[:, :, :], sq[:, :, 2, :], ALU.add))
                    TT(t2[:, :, :], vv[:, :, :], w(wc0, 4), ALU.mult)
                    TT(t3[:, :, :], vv[:, :, :], w(wc0, 2), ALU.mult)
                    link(TT(t1[:, :, :], t1[:, :, :], w(wc0, 1), ALU.add))
                    link(TT(t2[:, :, :], t2[:, :, :], w(wc0, 0), ALU.add))
                    TT(t1[:, :, :], t1[:, :, :], a2[:, :, :], ALU.mult)
                    link(TT(t2[:, :, :], t2[:, :, :], A0, ALU.mult))
                    link(TT(t1[:, :, :], t1[:, :, :], t2[:, :, :], ALU.add))
                    TT(Bm[:, :, 0:C], t1[:, :, :], t3[:, :, :], ALU.add)
                    TT(t2[:, :, :], A0, w(wc1, 1), ALU.mult)
                    TT(vv[:, :, :], vv[:, :, :], w(wc1, 3), ALU.mult)
                    link(TT(a2[:, :, :], a2[:, :, :], w(wc1, 2), ALU.mult))
                    TT(t2[:, :, :], t2[:, :, :], w(wc1, 0), ALU.add)
                    link(TT(a2[:, :, :], a2[:, :, :], vv[:, :, :], ALU.add))
                    link(TT(t2[:, :, :], t2[:, :, :], a2[:, :, :], ALU.add))
                    TT(Bm[:, :, C:D].rearrange("p t (k c) -> p t k c", k=3), A1, bc(t2[:, :, :], 3, 2), ALU.mult).then_inc(s_B, 1)

                def to_skip(c):
                    dve.wait_ge(s_o, 1)
                    dve.sem_inc(s_o, -1)
                    for b in range(3):
                        v, r = banks(pso, b)
                        k = S.skip[:, bass.ds(c * CT + r.start, r.stop - r.start), :]
                        ins = TT(k, k, v, ALU.add)
                    ins.then_inc(s_od, 1)

                sums(0, 0)
                with dve.Fori(0, CHUNKS // 2 - 1) as it:
                    for slot in range(2):
                        basis()
                        sums(it + slot, 1 - slot)
                        to_skip(it * 2 + slot)
                for c in range(CHUNKS - 3, CHUNKS - 1):
                    basis()
                    sums((c + 1) // 2, (c + 1) % 2, freed=False)
                    to_skip(c)
                basis()
                to_skip(CHUNKS - 1)
                dve.wait_ge(s_st, 1)
                dve.sem_inc(s_st, -1)
                link(TS(mu[:, :], pstat[0:P, 0, 0:C], 1.0 / N, None, ALU.mult))
                TT(S.skip[:, :, 0:C], S.skip[:, :, 0:C], bc(mu[:, :], NT, 1), ALU.subtract).then_inc(s_cent, 1)
                dve.wait_ge(s_st, 2)
                dve.sem_inc(s_st, -2)
                TS(fac[:, 0, :], pstat[0:P, 0, C:2 * C], 1.0 / N, None, ALU.mult)
                link(TS(fac[:, 1:4, :].rearrange("p a b -> p (a b)"), pstat[0:P, 1, 0:3 * C], 1.0 / N, None, ALU.mult))
                link(TT(fac[:, 1, :], fac[:, 1, :], fac[:, 2, :], ALU.add))
                link(TT(fac[:, 1, :], fac[:, 1, :], fac[:, 3, :], ALU.add))
                TS(var[:, 0, :], fac[:, 0, :], LN_EPS, None, ALU.add)
                TS(var[:, 1, :], fac[:, 1, :], 1.0 / 3.0, LN_EPS, ALU.mult, ALU.add).then_inc(s_var, 1)
                dve.wait_ge(s_std, 1)
                dve.sem_inc(s_std, -1)
                link(nc.vector.reciprocal(var[:, :, :], var[:, :, :]))
                TT(fac[:, 0, :], var[:, 0, :], gam[:, 0, :], ALU.mult)
                for k in range(3):
                    ins = TT(fac[:, k + 1, :], var[:, 1, :], gam[:, 2, :], ALU.mult)
                link(ins)

            @block.tensor
            def _(pe):
                def sums_turned():
                    pe.wait_ge(s_h, 1)
                    pe.sem_inc(s_h, -1)
                    turn(nc, h, S.ident, pst).then_inc(s_t, 1)
                    pe.wait_ge(s_hT, 1)
                    pe.sem_inc(s_hT, -1)

                def basis_out():
                    pe.wait_ge(s_B, 1)
                    pe.sem_inc(s_B, -1)
                    turn(nc, Bm, S.ident, pst).then_inc(s_t, 1)
                    pe.wait_ge(s_hT, 1)
                    pe.sem_inc(s_hT, -1)
                    linear(nc, hT[1], bd[:, 2, :], bd[:, 3, :], pso).then_inc(s_o, 1)
                pe.wait_ge(s_w, 16 * 11)
                sums_turned()
                linear(nc, hT[0], bd[:, 0, :], bd[:, 1, :], pso).then_inc(s_A, 1)
                with pe.Fori(0, CHUNKS - 1) as c:
                    basis_out()
                    sums_turned()
                    pe.wait_ge(s_od, 1)
                    pe.sem_inc(s_od, -1)
                    linear(nc, hT[0], bd[:, 0, :], bd[:, 1, :], pso).then_inc(s_A, 1)
                basis_out()
                pe.wait_ge(s_od, 1)
                pe.sem_inc(s_od, -1)
                pe.sem_inc(s_all, 1)

                def over_nodes(to, v):
                    for t in range(NT):
                        ins = nc.tensor.matmul(to, S.ones[:, :], v(t), start=(t == 0), stop=(t == NT - 1))
                    ins.then_inc(s_st, 1)
                over_nodes(pstat[:, 0, 0:C], lambda t: S.skip[:, t, 0:C])
                pe.wait_ge(s_sqv, 1)
                pe.sem_inc(s_sqv, -1)
                over_nodes(pstat[:, 1, 0:3 * C], lambda t: big[:, t, C:D])
                pe.wait_ge(s_sq, 1)
                pe.sem_inc(s_sq, -1)
                over_nodes(pstat[:, 0, C:2 * C], lambda t: big[:, t, 0:C])

            @block.scalar
            def _(act):
                def copy_turned(to):
                    act.wait_ge(s_t, 1)
                    act.sem_inc(s_t, -1)
                    turned(nc, pst, to).then_inc(s_hT, 1)

                def copy_A():
                    act.wait_ge(s_A, 1)
                    act.sem_inc(s_A, -1)
                    for b in range(3):
                        v, r = banks(pso, b)
                        ins = nc.scalar.copy(A[:, r, :], v)
                    ins.then_inc(s_Ac, 1)
                copy_turned(hT[0])
                with act.Fori(0, CHUNKS - 1) as c:
                    copy_A()
                    copy_turned(hT[1])
                    copy_turned(hT[0])
                copy_A()
                copy_turned(hT[1])
                act.wait_ge(s_all, 1)
                nc.scalar.activation(big[:, :, C:D], S.skip[:, :, C:D], ACT.Square).then_inc(s_sqv, 1)
                act.wait_ge(s_cent, 1)
                act.sem_inc(s_cent, -1)
                nc.scalar.activation(big[:, :, 0:C], S.skip[:, :, 0:C], ACT.Square).then_inc(s_sq, 1)
                act.wait_ge(s_var, 1)
                act.sem_inc(s_var, -1)
                nc.scalar.activation(var[:, :, :], var[:, :, :], ACT.Sqrt).then_inc(s_std, 1)



def mixture(nc, ctx, I, S, layer, out=None):
    pre = f"m{layer}_"
    hid = 2 if layer == 0 else 4
    steps = 2 if layer == 0 else 1

    def sem(name):
        return S.signals.get(pre, name)

    with ExitStack() as loc:
        def tb(name, shape, dt=F32):
            return loc.enter_context(nc.sbuf_tensor(pre + name, shape, dt))
        h, st, hT = tb("h", [P, CT, D]), tb("st", [P, CT, 9]), tb("hT", [128, 2, CN])
        next_hT = tb("next_hT", [128, 2, CN])
        a4 = tb("acc", [P, GT, CT, D]) if layer else None
        hid1 = [tb(f"hid{i}", [128, hid, CN]) for i in range(2)]
        wr, bo = tb("gate_w", [128, 2, NEXP]), tb("out_bias", [NEXP, D])
        br = tb("gate_b", [P, 2, NEXP])
        lg, ex = tb("logits", [P, CT, NEXP]), tb("exps", [P, CT, NEXP])
        m8, i8, i8f = tb("best", [P, CT, 8]), tb("best_i", [P, CT, 8], U32), tb("best_f", [P, CT, 8])
        iota_i, iota = tb("iota_i", [P, NEXP], I32), tb("iota", [P, NEXP])
        s1 = tb("s1", [P, CT, 4])
        wg = tb("weights", [P, NT, NEXP])
        wgn = tb("next_weights", [P, CT, NEXP])
        wT = tb("weights_T", [NEXP, CN])
        psh = loc.enter_context(nc.psum_tensor(pre + "psh", [128, 4, 512], F32))
        pso = loc.enter_context(nc.psum_tensor(pre + "pso", [P, 3, 512], F32))
        pst = loc.enter_context(nc.psum_tensor(pre + "pst", [128, 512], F32))
        psg = pst[0:P, 0:CT * NEXP]
        s_own = sem("act_step")
        bn = tb("bn", [128, 5, 2, 16]) if layer == 0 else None
        b1 = None if layer == 0 else tb("b1", [128, 32])
        (s_w, s_in, s_free4, s_var, s_std, s_h, s_t, s_hT, s_g, s_lg, s_ex, s_wg, s_wt, s_wT, s_b, s_bd, s_m, s_ev, s_o, s_od,
         s_hTc, s_link, s_bnv, s_bns, s_aff, s_pass, s_iota, s_x, s_out) = (sem(n) for n in (
             "small_weights", "acc_in", "acc_free", "variance", "deviation", "h_ready", "turned", "hT_ready", "gates_in_psum",
             "logits_ready", "exps_ready", "gates_ready", "gates_turned", "gates_T_ready", "bias_in_psum", "bias_added",
             "hidden_in_psum", "hidden_ready", "out_in_psum", "out_added", "hT_moved", "dve_step", "bn_variance", "bn_deviation",
             "affine_ready", "dma_waits_passed", "iota", "x_ready", "stored"))
        smalls = [(wr[:, :, :], (I["Wr"] if layer == 0 else I["Wg"]).rearrange("(k p) e -> p k e", p=128)),
                  (bo[:, :], I["bo"] if layer == 0 else I["b2"])]
        if layer == 0:
            smalls += [(br[:, 0, :], I["br"].broadcast_to([P, NEXP])), (bn[:, :, :, :], I["bn"])]
        else:
            smalls += [(br[:, 0, :], I["bg"].broadcast_to([P, NEXP])), (br[:, 1, :], I["bias"].broadcast_to([P, NEXP])), (b1[:, :], I["b1"])]
        with nc.Block() as block:
            @block.sync
            def _(sp):
                for to, fr in smalls:
                    sp.dma_start(to, fr).then_inc(s_w, 16)
                if layer == 0:
                    zero_sums(sp, S, 1)
                    sp.wait_ge(S.zeroed, 16 * 2 * GT)
                if layer:
                    rows = out.rearrange("(p t) d -> p t d", t=NT)
                    with sp.Fori(0, CHUNKS) as c:
                        sp.wait_ge(s_free4, 1)
                        sp.sem_inc(s_free4, -1)
                        load_sums(sp, S.acc[1], a4, s_in, c)
                    with sp.Fori(0, CHUNKS) as c:
                        sp.wait_ge(s_x, 1)
                        sp.sem_inc(s_x, -1)
                        sp.dma_start(rows[:, bass.ds(c * CT, CT), :], S.x[:, bass.ds(c * CT, CT), :]).then_inc(s_out, 16)
                    sp.wait_ge(s_out, 16 * CHUNKS)

            @block.gpsimd
            def _(pool):
                nc.gpsimd.iota(iota_i[:, :], pattern=[[1, NEXP]], base=0, channel_multiplier=0).then_inc(s_iota, 1)

            @block.vector
            def _(dve):
                link = linker(dve, s_link)
                TT, TS, STT = nc.vector.tensor_tensor, nc.vector.tensor_scalar, nc.vector.scalar_tensor_tensor
                dve.sem_inc(s_od, 1)
                if layer:
                    dve.sem_inc(s_free4, 1)

                def norm_begin(n):
                    x = S.x[:, bass.ds(n * CT, CT), :]
                    if layer == 0:
                        k = S.skip[:, bass.ds(n * CT, CT), :]
                        link(TT(k, k, bc(S.fac[:, :, :].rearrange("p a b -> p (a b)"), CT, 1), ALU.mult))
                        link(TT(x, x, k, ALU.add))
                        link(TT(x[:, :, 0:C], x[:, :, 0:C], bc(S.gam[:, 1, :], CT, 1), ALU.add))
                    if layer:
                        dve.wait_ge(s_in, 16 * GT * n + 16 * GT)
                        dve.sem_inc(s_pass, 1)
                        TT(a4[:, 0, :, :], a4[:, 0, :, :], a4[:, 1, :, :], ALU.add)
                        link(TT(a4[:, 2, :, :], a4[:, 2, :, :], a4[:, 3, :, :], ALU.add))
                        link(TT(a4[:, 0, :, :], a4[:, 0, :, :], a4[:, 2, :, :], ALU.add))
                        link(TT(x, x, a4[:, 0, :, :], ALU.add))
                        dve.sem_inc(s_free4, 1)
                    statistics(nc, link, x, st).then_inc(s_var, 1)

                def norm_end(n):
                    dve.wait_ge(s_std, 1)
                    dve.sem_inc(s_std, -1)
                    normed(nc, link, S.x[:, bass.ds(n * CT, CT), :], h, st).then_inc(s_h, 1)

                def gates_begin(n):
                    dve.wait_ge(s_g, 1)
                    dve.sem_inc(s_g, -1)
                    link(TT(lg[:, :, :], psg.rearrange("p (t e) -> p t e", e=NEXP), bc(br[:, 0, :], CT, 1), ALU.add))
                    if layer == 0:
                        link(nc.vector.tensor_reduce(s1[:, :, 0], lg[:, :, :], AX, ALU.max))
                        TT(lg[:, :, :], lg[:, :, :], bc(s1[:, :, 0], NEXP, 2), ALU.subtract).then_inc(s_lg, 1)
                        return
                    for j in range(CT):
                        ins = nc.vector.max(m8[:, j, :], lg[:, j, :])
                    link(ins)
                    for j in range(CT):
                        ins = nc.vector.max_index(i8[:, j, :], m8[:, j, :], lg[:, j, :])
                    link(ins)
                    nc.vector.tensor_copy(i8f[:, :, :], i8[:, :, :])
                    TT(s1[:, :, 0], m8[:, :, 1], m8[:, :, 0], ALU.subtract).then_inc(s_lg, 1)

                def gates_end(n):
                    weights = wg[:, bass.ds(n * CT, CT), :]
                    dve.wait_ge(s_ex, 1)
                    dve.sem_inc(s_ex, -1)
                    if layer == 0:
                        link(nc.vector.tensor_reduce(s1[:, :, 1], ex[:, :, :], AX, ALU.add))
                        link(nc.vector.reciprocal(s1[:, :, 1], s1[:, :, 1]))
                        link(TT(wgn[:, :, :], ex[:, :, :], bc(s1[:, :, 1], NEXP, 2), ALU.mult))
                    else:
                        link(TS(s1[:, :, 2], s1[:, :, 1], 1.0, None, ALU.add))
                        link(nc.vector.reciprocal(s1[:, :, 2], s1[:, :, 2]))
                        link(TT(s1[:, :, 3], s1[:, :, 2], s1[:, :, 1], ALU.mult))
                        for j in range(CT):
                            TS(wgn[:, j, :], iota[:, :], i8f[:, j, 0:1], s1[:, j, 2:3], ALU.is_equal, ALU.mult)
                            ins = TS(ex[:, j, :], iota[:, :], i8f[:, j, 1:2], s1[:, j, 3:4], ALU.is_equal, ALU.mult)
                        link(ins)
                        link(TT(wgn[:, :, :], wgn[:, :, :], ex[:, :, :], ALU.add))
                    dve.sem_inc(s_wg, 1)
                    nc.vector.tensor_copy(weights, wgn[:, :, :])

                def experts(c, ahead):
                    dve.wait_ge(s_b, 1)
                    dve.sem_inc(s_b, -1)
                    for b in range(3):
                        v, r = banks(pso, b)
                        xk = S.x[:, bass.ds(c * CT + r.start, r.stop - r.start), :]
                        ins = TT(xk, xk, v, ALU.add)
                    link(ins)
                    dve.sem_inc(s_od, 1)
                    for e in range(NEXP):
                        dve.wait_ge(s_o, 1)
                        dve.sem_inc(s_o, -1)
                        for j in range(CT):
                            xk = S.x[:, bass.ds(c * CT + j, 1), :].rearrange("p a d -> p (a d)")
                            weight = wg[:, bass.ds(c * CT + j, 1), e:e + 1].rearrange("p a b -> p (a b)")
                            ins = STT(out=xk, in0=pso[:, j // 2, (j % 2) * D:(j % 2 + 1) * D], scalar=weight,
                                      in1=xk, op0=ALU.mult, op1=ALU.add)
                        link(ins)
                        dve.sem_inc(s_od, 1)
                        if ahead and e == 0:
                            norm_begin(c + 1)
                        elif ahead and e == 1:
                            norm_end(c + 1)
                        elif ahead and e == 5:
                            gates_begin(c + 1)
                        elif ahead and e == 6:
                            gates_end(c + 1)
                    if layer:
                        dve.sem_inc(s_x, 1)

                norm_begin(0)
                norm_end(0)
                dve.wait_ge(s_iota, 1)
                nc.vector.tensor_copy(iota[:, :], iota_i[:, :])
                dve.wait_ge(s_w, 16 * len(smalls))
                if layer == 0:
                    TS(bn[:, 4, :, :], bn[:, 4, :, :], BN_EPS, None, ALU.add).then_inc(s_bnv, 1)
                    dve.wait_ge(s_bns, 1)
                    dve.sem_inc(s_bns, -1)
                    TT(bn[:, 1, :, :], bn[:, 1, :, :], bn[:, 3, :, :], ALU.subtract)
                    link(nc.vector.reciprocal(bn[:, 4, :, :], bn[:, 4, :, :]))
                    link(TT(bn[:, 0, :, :], bn[:, 0, :, :], bn[:, 4, :, :], ALU.mult))
                    link(TT(bn[:, 1, :, :], bn[:, 1, :, :], bn[:, 0, :, :], ALU.mult))
                    link(TT(bn[:, 2, :, :], bn[:, 2, :, :], bn[:, 1, :, :], ALU.add))
                    dve.sem_inc(s_aff, 1)
                else:
                    link(TT(br[:, 0, :], br[:, 0, :], br[:, 1, :], ALU.add))
                gates_begin(0)
                gates_end(0)
                with dve.Fori(0, CHUNKS - 1) as c:
                    experts(c, True)
                experts(CHUNKS - 1, False)

            @block.scalar
            def _(act):
                def deviation():
                    root(nc, act, st, s_var, s_std)

                def turned_round(i):
                    act.wait_ge(s_t, 1)
                    act.sem_inc(s_t, -1)
                    n = min(4, 2 * CT - 4 * i) // 2
                    o = next_hT[:, :, 2 * i * P:(2 * i + n) * P].rearrange("p k (j e) -> p j k e", j=n)
                    tell(act, nc.scalar.copy(o, pst[:, 0:2 * n * P].rearrange("p (j k e) -> p j k e", j=n, k=2)), s_own, s_hT)

                def exps():
                    act.wait_ge(s_lg, 1)
                    act.sem_inc(s_lg, -1)
                    if layer == 0:
                        nc.scalar.activation(ex[:, :, :], lg[:, :, :], ACT.Exp).then_inc(s_ex, 1)
                    else:
                        nc.scalar.activation(s1[:, :, 1], s1[:, :, 0], ACT.Exp).then_inc(s_ex, 1)

                def move():
                    nc.scalar.copy(hT[:, :, :], next_hT[:, :, :]).then_inc(s_hTc, 1)

                def weights_round(i):
                    act.wait_ge(s_wt, 1)
                    act.sem_inc(s_wt, -1)
                    lo, hi = (0, 4 * P) if i == 0 else (4 * P, CN)
                    nc.scalar.copy(wT[:, lo:hi], pst[0:NEXP, 0:hi - lo]).then_inc(s_wT, 1)

                def evacuate(e, step, m):
                    act.wait_ge(s_m, 1)
                    act.sem_inc(s_m, -1)
                    for i in range(2):
                        lo, hi = SPLIT[i], SPLIT[i + 1]
                        v = psh[:, 2 * (m % 2) + i, 0:hi - lo]
                        k = e * 2 + m
                        if layer == 0:
                            ins = nc.scalar.activation(hid1[step][:, m, lo:hi], v, ACT.Relu, bias=bn[:, 2, step, k:k + 1],
                                                       scale=bn[:, 0, step, k:k + 1])
                        else:
                            ins = nc.scalar.activation(hid1[e % 2][:, m, lo:hi], v, ACT.Relu,
                                                       bias=b1[:, 4 * e + m:4 * e + m + 1])
                    ins.then_inc(s_ev, 1)

                def experts(ahead):
                    for e in range(NEXP):
                        if layer == 0:
                            evacuate(e, 1, 0)
                            evacuate(e, 1, 1)
                        n = (e + 1) % NEXP
                        if n or ahead:
                            evacuate(n, 0, 0)
                            evacuate(n, 0, 1)
                        if ahead and n == 0:
                            weights_round(0)
                            weights_round(1)
                        if ahead and 3 <= e <= 5:
                            turned_round(e - 3)
                        if n or ahead:
                            for m in range(2, hid):
                                evacuate(n, 0, m)
                        if ahead and e == 1:
                            deviation()
                        if ahead and e == 6:
                            exps()
                            move()

                deviation()
                if layer == 0:
                    act.wait_ge(s_bnv, 1)
                    act.sem_inc(s_bnv, -1)
                    nc.scalar.activation(bn[:, 4, :, :], bn[:, 4, :, :], ACT.Sqrt).then_inc(s_bns, 1)
                    act.wait_ge(s_aff, 1)
                    act.sem_inc(s_aff, -1)
                else:
                    act.wait_ge(s_w, 16 * len(smalls))
                for i in range(3):
                    turned_round(i)
                move()
                exps()
                evacuate(0, 0, 0)
                evacuate(0, 0, 1)
                weights_round(0)
                weights_round(1)
                for m in range(2, hid):
                    evacuate(0, 0, m)
                with act.Fori(0, CHUNKS - 1) as c:
                    experts(True)
                experts(False)

            @block.tensor
            def _(pe):
                pe.wait_ge(s_w, 16 * len(smalls))
                pe.wait_ge(S.s_mw[layer], 16 * NEXP * len(S.mw[layer]))

                def hidden(w, e, src, m):
                    for i in range(2):
                        lo, hi = SPLIT[i], SPLIT[i + 1]
                        for k in range(2):
                            ins = nc.tensor.matmul(psh[:, 2 * (m % 2) + i, 0:hi - lo], w[:, e, k, m * 128:(m + 1) * 128],
                                                   src[:, k, lo:hi], start=(k == 0), stop=(k == 1))
                    ins.then_inc(s_m, 1)

                def output(w, e, src):
                    pe.wait_ge(s_od, 1)
                    pe.sem_inc(s_od, -1)
                    for j in range(CT):
                        for k in range(hid):
                            ins = nc.tensor.matmul(pso[:, j // 2, (j % 2) * D:(j % 2 + 1) * D], src[:, k, j * P:(j + 1) * P],
                                                   w[:, e, k, :], start=(k == 0), stop=(k == hid - 1))
                    ins.then_inc(s_o, 1)

                def turn_round(i):
                    if i == 0:
                        pe.wait_ge(s_h, 1)
                        pe.sem_inc(s_h, -1)
                    else:
                        pe.wait_ge(s_hT, 1)
                        pe.sem_inc(s_hT, -1)
                    for b in range(4 * i, min(4 * i + 4, 2 * CT)):
                        ins = nc.tensor.transpose(pst[:, (b % 4) * P:(b % 4 + 1) * P], h[:, b // 2, (b % 2) * 128:(b % 2 + 1) * 128],
                                                  S.ident[0:P, 0:P])
                    ins.then_inc(s_t, 1)

                def logits():
                    pe.wait_ge(s_hT, 1)
                    pe.sem_inc(s_hT, -1)
                    for j in range(CT):
                        for k in range(2):
                            ins = nc.tensor.matmul(psg[:, j * NEXP:(j + 1) * NEXP], next_hT[:, k, j * P:(j + 1) * P], wr[:, k, :],
                                                   start=(k == 0), stop=(k == 1))
                    ins.then_inc(s_g, 1)

                def turn_next(i):
                    if i < 3:
                        turn_round(i)
                    else:
                        logits()

                def turn_weights(i):
                    if i == 0:
                        pe.wait_ge(s_wg, 1)
                        pe.sem_inc(s_wg, -1)
                    else:
                        pe.wait_ge(s_wT, 1)
                        pe.sem_inc(s_wT, -1)
                    for j in (range(4) if i == 0 else (4,)):
                        ins = nc.tensor.transpose(pst[0:NEXP, (j % 4) * P:(j % 4 + 1) * P], wgn[:, j, :], S.ident[0:P, 0:P])
                    ins.then_inc(s_wt, 1)

                def biases():
                    pe.wait_ge(s_wT, 1)
                    pe.sem_inc(s_wT, -1)
                    pe.wait_ge(s_od, 1)
                    pe.sem_inc(s_od, -1)
                    for j in range(CT):
                        ins = nc.tensor.matmul(pso[:, j // 2, (j % 2) * D:(j % 2 + 1) * D], wT[:, j * P:(j + 1) * P], bo[:, :],
                                               start=True, stop=True)
                    ins.then_inc(s_b, 1)

                def first_step(e, blocks):
                    for m in blocks:
                        pe.wait_ge(s_ev, 1)
                        pe.sem_inc(s_ev, -1)
                        hidden(S.mw[layer][0], e, hT, m)

                def experts(ahead):
                    W = S.mw[layer]
                    for e in range(NEXP):
                        n = (e + 1) % NEXP
                        if layer == 0:
                            pe.wait_ge(s_ev, 2)
                            pe.sem_inc(s_ev, -2)
                            hidden(W[1], e, hid1[0], 0)
                            hidden(W[1], e, hid1[0], 1)
                        if e == 0:
                            biases()
                        if n or ahead:
                            if n == 0:
                                pe.wait_ge(s_hTc, 1)
                                pe.sem_inc(s_hTc, -1)
                            first_step(n, range(2))
                            if e == NEXP - 2:
                                first_step(n, range(2, hid))
                        else:
                            pe.wait_ge(s_ev, 2)
                            pe.sem_inc(s_ev, -2)
                        if ahead and n == 0:
                            turn_weights(0)
                        output(W[-1], e, hid1[e % 2 if layer else 1])
                        if ahead and n == 0:
                            turn_weights(1)
                        if ahead and 2 <= e <= 5:
                            turn_next(e - 2)
                        if (n or ahead) and e != NEXP - 2:
                            first_step(n, range(2, hid))

                for i in range(3):
                    turn_round(i)
                logits()
                pe.wait_ge(s_hTc, 1)
                pe.sem_inc(s_hTc, -1)
                for m in range(2):
                    hidden(S.mw[layer][0], 0, hT, m)
                turn_weights(0)
                turn_weights(1)
                first_step(0, range(2, hid))
                with pe.Fori(0, CHUNKS - 1) as c:
                    experts(True)
                experts(False)
                pe.wait_ge(s_od, 1)
                pe.sem_inc(s_od, -1)



def second_nodes(nc, ctx, I, S):
    def sem(name):
        return S.signals.get("sn", name)

    with ExitStack() as loc:
        def tb(name, shape, dt=F32):
            return loc.enter_context(nc.sbuf_tensor("sn_" + name, shape, dt))
        row = [tb(f"row{i}", [P, CT, T2]) for i in range(2)]
        st, hT = tb("st", [P, CT, 9]), tb("hT", [128, 2, CN])
        pst = loc.enter_context(nc.psum_tensor("sn_pst", [128, 3, 512], F32))
        pso = loc.enter_context(nc.psum_tensor("sn_pso", [P, 3, 512], F32))
        s_link, s_var, s_std, s_h, s_t, s_hT, s_d, s_row, s_tab, s_rowfree = (sem(n) for n in (
            "dve_step", "variance", "deviation", "h_ready", "turned", "hT_ready", "vectors_in_psum", "row_ready", "table",
            "row_free"))
        with nc.Block() as block:
            @block.sync
            def _(sp):
                rows = S.table2.rearrange("(p t) d -> p t d", t=NT)
                def store(c, slot):
                    sp.wait_ge(s_row, 1)
                    sp.sem_inc(s_row, -1)
                    sp.dma_start(rows[:, bass.ds(c * CT, CT), :], row[slot][:, :, :]).then_inc(s_tab, 16)
                    sp.wait_ge(s_tab, 16 * c + 16)
                    sp.sem_inc(s_rowfree, 1)
                with sp.Fori(0, CHUNKS // 2) as it:
                    for slot in range(2):
                        store(it * 2 + slot, slot)
                store(CHUNKS - 1, 0)

            @block.vector
            def _(dve):
                link = linker(dve, s_link)
                dve.sem_inc(s_rowfree, 2)

                def norm(c, slot):
                    x, h = S.x[:, bass.ds(c * CT, CT), :], row[slot][:, :, 0:D]
                    dve.wait_ge(s_rowfree, 1)
                    dve.sem_inc(s_rowfree, -1)
                    link(normalise(nc, dve, link, x, h, st, s_var, s_std))
                    dve.sem_inc(s_h, 1)
                    link(nc.vector.tensor_tensor(x, x, h, ALU.add))
                with dve.Fori(0, CHUNKS // 2) as it:
                    for slot in range(2):
                        norm(it * 2 + slot, slot)
                norm(CHUNKS - 1, 0)

            @block.tensor
            def _(pe):
                def turn_in(slot):
                    pe.wait_ge(s_h, 1)
                    pe.sem_inc(s_h, -1)
                    turn(nc, row[slot], S.ident, pst).then_inc(s_t, 1)

                def out():
                    pe.wait_ge(s_hT, 1)
                    pe.sem_inc(s_hT, -1)
                    for j in range(CT):
                        o = (j % 2) * 256
                        nc.tensor.matmul(pso[:, j // 2, o:o + C], hT[:, 0, j * P:(j + 1) * P], S.wd[:, 0, 0:C], start=True, stop=True)
                        ins = nc.tensor.matmul(pso[:, j // 2, o + C:o + 3 * C], hT[:, 1, j * P:(j + 1) * P], S.wd[:, 1, :],
                                               start=True, stop=True)
                    ins.then_inc(s_d, 1)
                turn_in(0)
                with pe.Fori(0, CHUNKS // 2) as it:
                    for slot in range(2):
                        out()
                        turn_in(1 - slot)
                out()

            @block.scalar
            def _(act):
                def turned_in():
                    act.wait_ge(s_t, 1)
                    act.sem_inc(s_t, -1)
                    turned(nc, pst, hT).then_inc(s_hT, 1)

                def out(slot):
                    act.wait_ge(s_d, 1)
                    act.sem_inc(s_d, -1)
                    for b in range(3):
                        v, r = banks(pso, b)
                        ins = nc.scalar.copy(row[slot][:, r, D:T2], v[:, :, 0:3 * C])
                    ins.then_inc(s_row, 1)
                root(nc, act, st, s_var, s_std)
                turned_in()
                with act.Fori(0, CHUNKS // 2) as it:
                    for slot in range(2):
                        root(nc, act, st, s_var, s_std)
                        out(slot)
                        turned_in()
                out(0)



def second_edges(nc, ctx, I, S):
    with ExitStack() as loc:
        def tb(name, shape, dt=F32):
            return loc.enter_context(nc.sbuf_tensor(f"e2_{name}", shape, dt))

        def sem(n):
            return S.signals.get("e2", n)
        B = edge_buffers(nc, loc, S, "e2")
        got = [tb(f"got{s}", [P, GT, C + T2]) for s in range(UNROLL)]
        yx = tb("yx", [128, GE])
        rl = tb("relu", [C, GE])
        cs = [tb(f"c{s}", [P, GT, D]) for s in range(2)]
        ex = tb("exp", [P, GT, C])
        mx, nm, Z, ez, az = (tb(n, [P, GT]) for n in ("max", "neg_max", "Z", "ez", "az"))
        t = tb("t", [P, GT, C])
        prod = tb("prod", [P, GT, 3, C])
        ush = tb("ush", [P, GT, 3, C])
        p_t = loc.enter_context(nc.psum_tensor("e2_pt", [128, 512], F32))
        p_h = loc.enter_context(nc.psum_tensor("e2_ph", [C, 512], F32))
        p_c = loc.enter_context(nc.psum_tensor("e2_pc", [P, 2, 512], F32))
        pss = loc.enter_context(nc.psum_tensor("e2_pss", [P, 2, 512], F32))
        (y_ready, yx_ps, yx_ready, h_ps, relu_ready, c_ps, c_ps_free, c_ready, c_free, nm_ready, e_ready, az_ready, vectors_ready,
         s_link) = (sem(n) for n in (
             "y_ready", "yx_in_psum", "yx_ready", "hidden_in_psum", "relu_ready", "main_in_psum", "main_psum_free",
             "main_ready", "main_free", "neg_max_ready", "exp_ready", "weights_ready", "vector_messages_ready", "dve_step"))

        with nc.Block() as block:
            @block.sync
            def _(sp):
                with sp.Fori(0, NEXP) as it:
                    for c in range(UNROLL):
                        load_row(sp, I, B, Edge(it, c))
                    load_expert(sp, S, 1, it)
                with sp.Fori(0, G // UNROLL - NEXP) as it:
                    for c in range(UNROLL):
                        load_row(sp, I, B, Edge(it, NEXP * UNROLL + c))

            @block.gpsimd
            def _(pool):
                edge_pool(nc, pool, B, S.table2, lambda s, j: got[s][:, j, C:C + T2], S.acc[1])

            @block.tensor
            def _(pe):
                pe.sem_inc(B.msg_free, UNROLL)

                def group_sums(e):
                    pe.wait_ge(vectors_ready, 1)
                    pe.sem_inc(vectors_ready, -1)
                    sum_matmuls(nc, pe, B, e, pss)

                def turn_in(e):
                    pe.wait_ge(y_ready, 1)
                    pe.sem_inc(y_ready, -1)
                    for j in range(GT):
                        ins = nc.tensor.transpose(p_t[:, j * P:(j + 1) * P], got[e.deep][:, j, 0:128], S.ident[0:P, 0:P])
                    ins.then_inc(yx_ps, 1)

                def main(e):
                    pe.wait_ge(yx_ready, 1)
                    pe.sem_inc(yx_ready, -1)
                    nc.tensor.matmul(p_h[:, 0:GE], S.wh[:, :], yx[:, :], start=True, stop=True).then_inc(h_ps, 1)
                    pe.wait_ge(c_ps_free, 1)
                    pe.sem_inc(c_ps_free, -1)
                    for j in range(GT):
                        o = (j % 2) * D
                        nc.tensor.matmul(p_c[:, j // 2, o:o + 3 * C], yx[:, j * P:(j + 1) * P], S.wm[:, 0:3 * C],
                                         start=True, stop=True)
                    pe.wait_ge(relu_ready, 1)
                    pe.sem_inc(relu_ready, -1)
                    for j in range(GT):
                        o = (j % 2) * D
                        nc.tensor.matmul(p_c[:, j // 2, o + 3 * C:o + D], yx[:, j * P:(j + 1) * P], S.wm[:, 3 * C:D],
                                         start=True, stop=False)
                        ins = nc.tensor.matmul(p_c[:, j // 2, o + 3 * C:o + D], rl[:, j * P:(j + 1) * P], S.lsc[:, :],
                                               start=False, stop=True)
                    ins.then_inc(c_ps, 1)

                def body(it, c, sums=True):
                    if sums:
                        group_sums(Edge(it, c - 1))
                    turn_in(Edge(it, c + 2))
                    main(Edge(it, c + 2))
                for c in range(2):
                    turn_in(Edge(0, c))
                    main(Edge(0, c))
                body(0, 0, False)
                with pe.Fori(0, PASSES) as it:
                    for c in range(1, UNROLL + 1):
                        body(it, c)
                body(0, G - 3)
                for c in range(G - 3, G):
                    group_sums(Edge(0, c))

            @block.scalar
            def _(act):
                act.sem_inc(B.sum_free, 2)
                act.sem_inc(B.sum_ps_free, 1)
                act.sem_inc(c_ps_free, 1)

                def yx_copy():
                    act.wait_ge(yx_ps, 1)
                    act.sem_inc(yx_ps, -1)
                    nc.scalar.copy(yx[:, :], p_t[:, 0:GE]).then_inc(yx_ready, 1)

                def relu():
                    act.wait_ge(h_ps, 1)
                    act.sem_inc(h_ps, -1)
                    nc.scalar.activation(rl[:, :], p_h[:, 0:GE], ACT.Relu).then_inc(relu_ready, 1)

                def c_copy(e):
                    act.wait_ge(c_ps, 1)
                    act.sem_inc(c_ps, -1)
                    act.wait_ge(c_free, 1)
                    act.sem_inc(c_free, -1)
                    for b in range(2):
                        ins = nc.scalar.copy(cs[e.slot][:, 2 * b:2 * b + 2, :], p_c[:, b, :].rearrange("p (n d) -> p n d", d=D))
                    tell(act, ins, B.own, c_ready, c_ps_free)

                def exps(e):
                    act.wait_ge(nm_ready, 1)
                    act.sem_inc(nm_ready, -1)
                    nc.scalar.activation(ez[:, :], nm[:, :], ACT.Exp)
                    for j in range(GT):
                        ins = nc.scalar.activation(ex[:, j, :], cs[e.slot][:, j, 3 * C:D], ACT.Exp, bias=nm[:, j:j + 1],
                                                   accum_out=Z[:, j:j + 1])
                    ins.then_inc(e_ready, 1)

                def vectors(e):
                    act.wait_ge(az_ready, 1)
                    act.sem_inc(az_ready, -1)
                    for j in range(GT):
                        ins = nc.scalar.activation(B.msg[e.deep][:, j, C:D], got[e.deep][:, j, C + D:C + T2], ACT.Copy,
                                                   scale=az[:, j:j + 1])
                    tell(act, ins, B.own, vectors_ready, B.got_free)

                def body(it, c, sums=True, ahead=2):
                    exps(Edge(it, c))
                    if ahead > 0:
                        c_copy(Edge(it, c + 1))
                    vectors(Edge(it, c))
                    if sums:
                        sums_done(act, B)
                    if ahead > 1:
                        yx_copy()
                    if sums:
                        sum_copy(nc, act, B, Edge(it, c - 1), pss)
                    if ahead > 1:
                        relu()
                yx_copy()
                relu()
                c_copy(Edge(0, 0))
                yx_copy()
                relu()
                body(0, 0, False)
                with act.Fori(0, PASSES) as it:
                    for c in range(1, UNROLL + 1):
                        body(it, c)
                body(0, G - 3)
                body(0, G - 2, ahead=1)
                body(0, G - 1, ahead=0)
                sums_done(act, B)
                sum_copy(nc, act, B, Edge(0, G - 1), pss)

            @block.vector
            def _(dve):
                link = linker(dve, s_link)
                TT, TS, STT = nc.vector.tensor_tensor, nc.vector.tensor_scalar, nc.vector.scalar_tensor_tensor
                dve.sem_inc(B.row_free, 2)
                dve.sem_inc(B.got_free, UNROLL)
                dve.sem_inc(B.put_free, 2)
                dve.sem_inc(c_free, 2)

                def col(a, e, j):
                    return a[:, bass.ds(e.g * GT + j, 1)]

                def index(e):
                    nc.vector.tensor_copy(B.take_i[e.deep][:, :], S.src[:, bass.ds(e.g * GT, GT)]).then_inc(B.idx_ready, 1)

                def products(e):
                    dve.wait_ge(B.got[e.deep], 16 * GT * e.deep_use)
                    dve.sem_inc(B.passed, 1)
                    return TT(prod[:, :, :, :], got[e.deep][:, :, 2 * C:5 * C].rearrange("p t (k c) -> p t k c", k=3),
                              bc(S.shn[:, bass.ds(e.g * GT, GT), :], C, 3), ALU.mult)

                def maximum(e):
                    dve.wait_ge(c_ready, 1)
                    dve.sem_inc(c_ready, -1)
                    return nc.vector.tensor_reduce(mx[:, :], cs[e.slot][:, :, 3 * C:D], AX, ALU.max)

                def body(it, c, more=True, first=False, ahead=2):
                    e, n, nn = Edge(it, c), Edge(it, c + 1), Edge(it, c + 2)
                    v, m, y = cs[e.slot], B.msg[e.deep], got[nn.deep][:, :, 0:C]
                    d = got[e.deep][:, :, C + D:C + T2].rearrange("p t (k c) -> p t k c", k=3)
                    TS(nm[:, :], mx[:, :], -1.0, 0.0, ALU.mult, ALU.min).then_inc(nm_ready, 1)
                    if more:
                        index(Edge(it, c + 3))
                    TT(ush[:, :, :, :], bc(v[:, :, C:2 * C], 3, 2), bc(S.shn[:, bass.ds(e.g * GT, GT), :], C, 3), ALU.mult)
                    if ahead > 1:
                        products(nn)
                    for j in range(GT):
                        ins = STT(out=t[:, j, :], in0=v[:, j, 2 * C:3 * C], scalar=col(S.q, e, j), in1=v[:, j, 0:C],
                                  op0=ALU.mult, op1=ALU.add)
                    link(ins)
                    TT(d, d, ush[:, :, :, :], ALU.add)
                    if ahead > 1:
                        TT(y, prod[:, :, 0, :], prod[:, :, 1, :], ALU.add)
                    dve.wait_ge(e_ready, 1)
                    dve.sem_inc(e_ready, -1)
                    link(STT(out=Z[:, :], in0=ez[:, :], scalar=float(3 * C), in1=Z[:, :], op0=ALU.mult, op1=ALU.add))
                    dve.sem_inc(c_free, 1)
                    ins = nc.vector.reciprocal(Z[:, :], Z[:, :])
                    if ahead > 1:
                        ins = TT(y, y, prod[:, :, 2, :], ALU.add)
                    link(ins)
                    if ahead > 1:
                        dve.sem_inc(y_ready, 1)
                    TT(az[:, :], ez[:, :], Z[:, :], ALU.mult).then_inc(az_ready, 1)
                    for j in range(GT):
                        ins = STT(out=m[:, j, 0:C], in0=t[:, j, :], scalar=Z[:, j:j + 1], in1=ex[:, j, :], op0=ALU.mult, op1=ALU.mult)
                    ins.then_inc(B.msg_ready, 1)
                    if not first:
                        target(nc, dve, S, B, Edge(it, c - 1))
                    if ahead > 0:
                        make_same(nc, dve, S, B, n).then_inc(B.row_free, 1)
                        link(maximum(n))

                for c in range(3):
                    index(Edge(0, c))
                for c in range(2):
                    y = got[c][:, :, 0:C]
                    link(products(Edge(0, c)))
                    link(TT(y, prod[:, :, 0, :], prod[:, :, 1, :], ALU.add))
                    link(TT(y, y, prod[:, :, 2, :], ALU.add))
                    dve.sem_inc(y_ready, 1)
                make_same(nc, dve, S, B, Edge(0, 0)).then_inc(B.row_free, 1)
                link(maximum(Edge(0, 0)))
                body(0, 0, first=True)
                with dve.Fori(0, PASSES) as it:
                    for c in range(1, UNROLL + 1):
                        body(it, c)
                body(0, G - 3, more=False)
                body(0, G - 2, more=False, ahead=1)
                body(0, G - 1, more=False, ahead=0)
                target(nc, dve, S, B, Edge(0, G - 1))



def expert_weights(nc, ctx, S, layer, shapes, arrays):
    S.mw[layer] = [ctx.enter_context(nc.sbuf_tensor(f"mw{layer}_{i}", s, F32)) for i, s in enumerate(shapes)]
    S.mw_from[layer] = [a.rearrange("e (k p) h -> p e k h", p=128) for a in arrays]


def program(nc, I, out):
    S = State()
    with ExitStack() as ctx:
        S.signals = Signals(nc, ctx)
        for layer in range(2):
            S.s_mw[layer] = ctx.enter_context(nc.semaphore(f"experts{layer}_in"))
        setup(nc, ctx, I, S)
        with ExitStack() as experts:
            expert_weights(nc, experts, S, 0, [[128, NEXP, 2, H1]] * 3, [I["eW1"], I["eW2"], I["eWo"]])
            S.skip = experts.enter_context(nc.sbuf_tensor("skip", [P, NT, D], F32))
            S.fac = experts.enter_context(nc.sbuf_tensor("node_scale", [P, 4, C], F32))
            S.gam = experts.enter_context(nc.sbuf_tensor("gammas", [P, 3, C], F32))
            first_nodes(nc, ctx, I, S)
            first_edges(nc, ctx, I, S)
            last_nodes(nc, ctx, I, S)
            mixture(nc, ctx, I, S, 0)
        with ExitStack() as experts:
            expert_weights(nc, experts, S, 1, [[128, NEXP, 2, H2], [128, NEXP, 4, D]], [I["fW1"], I["fW2"]])
            second_nodes(nc, ctx, I, S)
            second_edges(nc, ctx, I, S)
            mixture(nc, ctx, I, S, 1, out)


def planar(a, axis):
    a = np.moveaxis(np.asarray(a), axis, -1)
    v = a[..., C:].reshape(a.shape[:-1] + (C, 3))
    v = np.swapaxes(v, -1, -2).reshape(a.shape[:-1] + (3 * C,))
    return np.ascontiguousarray(np.moveaxis(np.concatenate([a[..., :C], v], axis=-1), -1, axis))


def kernel(**inputs):
    import concourse.bacc as bacc
    from concourse.bass_utils import run_bass_kernel_spmd as run

    a = {k: np.asarray(v) for k, v in inputs.items()}
    g0, g1, f0, f1 = "L0_gnn_", "L1_gnn_", "L0_ffn_", "L1_ffn_"

    def tiled(v):
        return np.swapaxes(v.reshape((ET, P) + v.shape[1:]), 0, 1)

    def columns(v):
        return v.reshape(-1, 128).T

    m4 = a[g0 + "M4"].reshape(HID, 4, C)
    arrays = {
        "x": planar(a["x"], 1),
        "src_pt": tiled(a["src"]), "dst_pt": tiled(a["dst"]), "dst_row": a["dst"].reshape(1, E),
        "ea3": tiled(a["edge_attr_3"]), "ea4": tiled(a["edge_attr_4"]), 
        "rbfT": a["edge_attr_16"].T.reshape(R, G, 2, HE).transpose(2, 0, 1, 3).reshape(2 * R, G * HE),
        "M1": a[g0 + "M1"], "M2": a[g0 + "M2"], "M3": a[g0 + "M3"],
        "M4": np.concatenate([m4[:, 0], m4[:, 2], m4[:, 1], m4[:, 3]], axis=1),
        "Wup0": a[g0 + "W_up0"], "Wup1": a[g0 + "W_up1"], "Wsc0": a[g0 + "Wsc0"], "Wsc1": a[g0 + "Wsc1"],
        "Wlin0": a[g0 + "W_lin0"], "Wlin1": a[g0 + "W_lin1"], "WB0": a[g0 + "WB0"], "WB1": a[g0 + "WB1"],
        "Wc0r": a[g0 + "Wc0"].T.reshape(1, 5 * C), "Wc1r": a[g0 + "Wc1"].T.reshape(1, 4 * C),
        "gam": np.concatenate([a[g0 + "gamma0"], a[g0 + "beta0"], a[g0 + "gamma1"]]).reshape(1, 3 * C),
        "lsc": a[g1 + "lin_scalar_w"],
        "Wr": planar(a[f0 + "Wr"], 0), "br": a[f0 + "br"].reshape(1, NEXP), "bo": planar(a[f0 + "bo"], 1),
        "bn": np.stack([np.stack([columns(a[f0 + n + s]) for s in "12"], 1) for n in ("g", "b", "be", "m", "v")], 1),
        "eW1": planar(a[f0 + "W1"], 1), "eW2": a[f0 + "W2"], "eWo": planar(a[f0 + "Wo"], 2),
        "Wg": planar(a[f1 + "Wg"], 0), "bg": a[f1 + "bg"].reshape(1, NEXP), "bias": a[f1 + "bias"].reshape(1, NEXP),
        "fW1": planar(a[f1 + "W1"], 1), "b1": columns(a[f1 + "b1"]), "fW2": planar(a[f1 + "W2"], 2),
        "b2": planar(a[f1 + "b2"], 1),
    }
    fac = {"ls0T": a[g1 + "lin_src_w0"].T, "ls1T": a[g1 + "lin_src_w1"].T,
           "w00": a[g1 + "tp1_w00"], "w11": a[g1 + "tp1_w11"], "w01": a[g1 + "tp1_w01"], "w10": a[g1 + "tp1_w10"],
           "lh0": a[g1 + "lin_hidden_w0"], "lh1": a[g1 + "lin_hidden_w1"],
           "t00": a[g1 + "tp2_w00"], "t11": a[g1 + "tp2_w11"], "t01": a[g1 + "tp2_w01"], "t10": a[g1 + "tp2_w10"]}
    arrays["factors"] = np.stack([fac[n] for n in FACTORS], axis=1)
    nc = bacc.Bacc("TRN2", target_bir_lowering=False, num_devices=1)
    feed = {}

    def given(name, v):
        v = np.ascontiguousarray(v)
        feed["in_" + name] = v
        return nc.dram_tensor("in_" + name, v.shape, mybir.dt.from_np(v.dtype), kind="ExternalInput").ap()
    I = {name: given(name, v) for name, v in arrays.items()}
    out = nc.dram_tensor("out", (N, D), F32, kind="ExternalOutput").ap()
    program(nc, I, out)
    y = run(nc, [feed], core_ids=[0]).results[0]["out"]
    return np.concatenate([y[:, :C], np.swapaxes(y[:, C:].reshape(N, 3, C), 1, 2).reshape(N, 3 * C)], axis=1)
```
